# Optimizing a Trainium2 kernel written in Bass

```python
import numpy as np
import jax
import jax.numpy as jnp

def _softmax(x, axis=-1):
    return jax.nn.softmax(x, axis=axis)

def _gelu(x):
    return jax.nn.gelu(x, approximate=True)

def _silu(x):
    return jax.nn.silu(x)

def _sigmoid(x):
    return jax.nn.sigmoid(x)

def _layernorm(x, axis=-1, eps=1e-05):
    m = jnp.mean(x, axis=axis, keepdims=True)
    v = jnp.var(x, axis=axis, keepdims=True)
    return (x - m) / jnp.sqrt(v + eps)

def _scatter_add(tgt, idx, src, axis=0):
    return tgt.at[idx].add(src)

def _segment_sum(src, seg, n):
    return jax.ops.segment_sum(src, seg, n)
kernel_name = 'mk_decoder_postln_d1_seqx_r4_b63617'

def setup_inputs(seed: int=0):
    np.random.seed(seed)
    _w = jnp.asarray

    def _rec_inputs():
        import jax
        import jax.numpy as jnp
        _rk = jax.random.key(seed)
        x = -0.0002928 + 1 * jax.random.normal(jax.random.fold_in(_rk, 1), (16, 128, 256), jnp.float32)
        _lenS = 128 - jax.random.randint(jax.random.fold_in(_rk, 7), (16,), 0, max(1, 128 // 4) + 1, jnp.int32)
        _lenS2 = 128 - jax.random.randint(jax.random.fold_in(_rk, 8), (16,), 0, max(1, 128 // 4) + 1, jnp.int32)
        _ctx_1024P = jax.random.normal(jax.random.fold_in(_rk, 11), (16, 16, 256), jnp.float32)
        _ctx_1024c = jax.random.dirichlet(jax.random.fold_in(_rk, 511), 0.3 * jnp.ones((16,), jnp.float32), (16, 128))
        _ctx_1024t = jnp.einsum('bsk,bkd->bsd', _ctx_1024c, _ctx_1024P)
        _ctx_1024t = _ctx_1024t * jax.lax.rsqrt(jnp.mean(jnp.square(_ctx_1024t)) + 1e-12) * 0.953939
        ctx_1024 = -1.39393e-06 + 0.999914 * (_ctx_1024t + 0.3 * jax.random.normal(jax.random.fold_in(_rk, 611), (16, 128, 256), jnp.float32))
        return (x, ctx_1024)
    x, ctx_1024 = _rec_inputs()

    def _L0_attn_setup():
        import jax, jax.numpy as jnp
        import numpy as np
        B, T, C = (4, 512, 256)

        def wkv(k, v, w, u, reverse):

            def step(carry, kv):
                num, den, mx = carry
                k_t, v_t = kv
                ku = k_t + u
                m = jnp.maximum(mx, ku)
                e1 = jnp.exp(mx - m)
                e2 = jnp.exp(ku - m)
                y = (e1 * num + e2 * v_t) / (e1 * den + e2)
                mw = mx + w
                mn = jnp.maximum(mw, k_t)
                e1s = jnp.exp(mw - mn)
                e2s = jnp.exp(k_t - mn)
                return ((e1s * num + e2s * v_t, e1s * den + e2s, mn), y)
            z = jnp.zeros_like(k[:, 0])
            init = (z, z, jnp.full_like(z, -1e+38))
            ks = jnp.swapaxes(k, 0, 1)
            vs = jnp.swapaxes(v, 0, 1)
            _, ys = jax.lax.scan(step, init, (ks, vs), reverse=reverse)
            return jnp.swapaxes(ys, 0, 1)
        key = jax.random.key(seed)
        k1, k2, k3, k4, k5, k6, k7 = jax.random.split(key, 7)
        x = jax.random.normal(k1, (B, T, C), dtype=jnp.float32)
        rkv_w = jax.random.normal(k2, (6 * C, C), dtype=jnp.float32) / np.sqrt(C)
        out_w = jax.random.normal(k3, (C, 2 * C), dtype=jnp.float32) / np.sqrt(2 * C)
        time_decay = jax.random.uniform(k4, (C,), jnp.float32, -6.0, -5.0)
        time_first = jax.random.uniform(k5, (C,), jnp.float32, -3.0, 0.0)
        time_decay_rev = jax.random.uniform(k6, (C,), jnp.float32, -6.0, -5.0)
        time_first_rev = jax.random.uniform(k7, (C,), jnp.float32, -3.0, 0.0)
        return {'x': x, 'rkv_w': rkv_w, 'out_w': out_w, 'time_decay': time_decay, 'time_first': time_first, 'time_decay_rev': time_decay_rev, 'time_first_rev': time_first_rev}
    _L0_attn_all = _L0_attn_setup()
    _L0_attn_in = {k: v for k, v in _L0_attn_all.items() if k in ('rkv_w', 'out_w', 'time_decay', 'time_first', 'time_decay_rev', 'time_first_rev')}
    del _L0_attn_all

    def _L0_xattn_setup():
        import jax, jax.numpy as jnp
        import numpy as np
        H = 16
        D_MODEL = 256
        D_K = D_MODEL // H

        def _split_heads(x, B, S):
            return x.reshape(B, S, H, D_K).transpose(0, 2, 1, 3)
        key = jax.random.key(seed)
        ks = jax.random.split(key, 11)
        B, S, D = (2, 512, D_MODEL)
        sc = 1.0 / np.sqrt(D)
        return {'query': jax.random.normal(ks[0], (B, S, D), jnp.float32), 'key': jax.random.normal(ks[1], (B, S, D), jnp.float32), 'value': jax.random.normal(ks[2], (B, S, D), jnp.float32), 'Wq': jax.random.normal(ks[3], (D, D), jnp.float32) * sc, 'bq': jnp.zeros((D,), jnp.float32), 'Wk': jax.random.normal(ks[4], (D, D), jnp.float32) * sc, 'bk': jnp.zeros((D,), jnp.float32), 'Wv': jax.random.normal(ks[5], (D, D), jnp.float32) * sc, 'bv': jnp.zeros((D,), jnp.float32), 'Wo': jax.random.normal(ks[6], (D, D), jnp.float32) * sc, 'bo': jnp.zeros((D,), jnp.float32)}
    _L0_xattn_all = _L0_xattn_setup()
    _L0_xattn_in = {k: v for k, v in _L0_xattn_all.items() if k in ('Wq', 'bq', 'Wk', 'bk', 'Wv', 'bv', 'Wo', 'bo')}
    del _L0_xattn_all

    def _L0_ffn_setup():
        import jax, jax.numpy as jnp
        import numpy as np
        H, KVH, HD, D = (8, 2, 128, 256)
        E, TOPK, FFN = (8, 2, 896)
        THETA, EPS = (1000000.0, 1e-05)
        NBITS, GS = (4, 128)
        QMAX = float(2 ** NBITS - 1)
        NEG = -1e+30

        def qgroup(w):
            shp = w.shape
            w2 = w.reshape(-1, GS)
            wmax = jnp.max(w2, -1, keepdims=True)
            wmin = jnp.min(w2, -1, keepdims=True)
            scales = jnp.clip(wmax - wmin, 1e-05, None) / QMAX
            base = jnp.clip(jnp.round(-wmin / scales), 0.0, QMAX)
            wq = (jnp.clip(jnp.round(w2 / scales) + base, 0.0, QMAX) - base) * scales
            return wq.reshape(shp)

        def rms(x, g):
            return x * jax.lax.rsqrt(jnp.mean(x * x, -1, keepdims=True) + EPS) * g

        def rot_half(x):
            h = x.shape[-1] // 2
            return jnp.concatenate([-x[..., h:], x[..., :h]], axis=-1)
        key = jax.random.key(seed)
        ks = jax.random.split(key, 12)
        B, S = (2, 256)
        n = lambda k, s: 0.02 * jax.random.normal(k, s, dtype=jnp.float32)
        return {'hidden_states': jax.random.normal(ks[0], (B, S, D), dtype=jnp.float32), 'w_q': n(ks[1], (H * HD, D)), 'w_k': n(ks[2], (KVH * HD, D)), 'w_v': n(ks[3], (KVH * HD, D)), 'w_o': n(ks[4], (D, H * HD)), 'g1': jnp.ones((D,), jnp.float32), 'g2': jnp.ones((D,), jnp.float32), 'w_gate': n(ks[5], (E, D)), 'w1': n(ks[6], (E, FFN, D)), 'w3': n(ks[7], (E, FFN, D)), 'w2': n(ks[8], (E, D, FFN))}
    _L0_ffn_all = _L0_ffn_setup()
    _L0_ffn_in = {k: v for k, v in _L0_ffn_all.items() if k in ('w_q', 'w_k', 'w_v', 'w_o', 'g1', 'g2', 'w_gate', 'w1', 'w3', 'w2')}
    del _L0_ffn_all
    return {'x': x, 'ctx_1024': ctx_1024, 'L0_attn_rkv_w': _L0_attn_in['rkv_w'], 'L0_attn_out_w': _L0_attn_in['out_w'], 'L0_attn_time_decay': _L0_attn_in['time_decay'], 'L0_attn_time_first': _L0_attn_in['time_first'], 'L0_attn_time_decay_rev': _L0_attn_in['time_decay_rev'], 'L0_attn_time_first_rev': _L0_attn_in['time_first_rev'], 'L0_xattn_Wq': _L0_xattn_in['Wq'], 'L0_xattn_bq': _L0_xattn_in['bq'], 'L0_xattn_Wk': _L0_xattn_in['Wk'], 'L0_xattn_bk': _L0_xattn_in['bk'], 'L0_xattn_Wv': _L0_xattn_in['Wv'], 'L0_xattn_bv': _L0_xattn_in['bv'], 'L0_xattn_Wo': _L0_xattn_in['Wo'], 'L0_xattn_bo': _L0_xattn_in['bo'], 'L0_ffn_w_q': _L0_ffn_in['w_q'], 'L0_ffn_w_k': _L0_ffn_in['w_k'], 'L0_ffn_w_v': _L0_ffn_in['w_v'], 'L0_ffn_w_o': _L0_ffn_in['w_o'], 'L0_ffn_g1': _L0_ffn_in['g1'], 'L0_ffn_g2': _L0_ffn_in['g2'], 'L0_ffn_w_gate': _L0_ffn_in['w_gate'], 'L0_ffn_w1': _L0_ffn_in['w1'], 'L0_ffn_w3': _L0_ffn_in['w3'], 'L0_ffn_w2': _L0_ffn_in['w2']}

def reference(x, ctx_1024, L0_attn_rkv_w, L0_attn_out_w, L0_attn_time_decay, L0_attn_time_first, L0_attn_time_decay_rev, L0_attn_time_first_rev, L0_xattn_Wq, L0_xattn_bq, L0_xattn_Wk, L0_xattn_bk, L0_xattn_Wv, L0_xattn_bv, L0_xattn_Wo, L0_xattn_bo, L0_ffn_w_q, L0_ffn_w_k, L0_ffn_w_v, L0_ffn_w_o, L0_ffn_g1, L0_ffn_g2, L0_ffn_w_gate, L0_ffn_w1, L0_ffn_w3, L0_ffn_w2):
    import jax
    import jax.numpy as jnp

    def _L0_attn_ref(x, rkv_w, out_w, time_decay, time_first, time_decay_rev, time_first_rev):
        import jax, jax.numpy as jnp
        import numpy as np
        B, T, C = (4, 512, 256)

        def wkv(k, v, w, u, reverse):

            def step(carry, kv):
                num, den, mx = carry
                k_t, v_t = kv
                ku = k_t + u
                m = jnp.maximum(mx, ku)
                e1 = jnp.exp(mx - m)
                e2 = jnp.exp(ku - m)
                y = (e1 * num + e2 * v_t) / (e1 * den + e2)
                mw = mx + w
                mn = jnp.maximum(mw, k_t)
                e1s = jnp.exp(mw - mn)
                e2s = jnp.exp(k_t - mn)
                return ((e1s * num + e2s * v_t, e1s * den + e2s, mn), y)
            z = jnp.zeros_like(k[:, 0])
            init = (z, z, jnp.full_like(z, -1e+38))
            ks = jnp.swapaxes(k, 0, 1)
            vs = jnp.swapaxes(v, 0, 1)
            _, ys = jax.lax.scan(step, init, (ks, vs), reverse=reverse)
            return jnp.swapaxes(ys, 0, 1)
        b, t, c = x.shape
        rkv = jnp.einsum('btc,dc->btd', x, rkv_w).reshape(b, t, 2, 3, c)
        r_f, k_f, v_f = (rkv[:, :, 0, 0], rkv[:, :, 0, 1], rkv[:, :, 0, 2])
        r_b, k_b, v_b = (rkv[:, :, 1, 0], rkv[:, :, 1, 1], rkv[:, :, 1, 2])
        out_f = jax.nn.sigmoid(r_f) * wkv(k_f, v_f, -jnp.exp(time_decay), time_first, False)
        out_b = jax.nn.sigmoid(r_b) * wkv(k_b, v_b, -jnp.exp(time_decay_rev), time_first_rev, True)
        out_cat = jnp.concatenate([out_f, out_b], axis=-1)
        return jnp.einsum('btd,cd->btc', out_cat, out_w)

    def _L0_xattn_ref(query, key, value, Wq, bq, Wk, bk, Wv, bv, Wo, bo):
        import jax, jax.numpy as jnp
        import numpy as np
        H = 16
        D_MODEL = 256
        D_K = D_MODEL // H

        def _split_heads(x, B, S):
            return x.reshape(B, S, H, D_K).transpose(0, 2, 1, 3)
        B, S, D = query.shape
        q = _split_heads(query @ Wq + bq, B, S)
        k = _split_heads(key @ Wk + bk, B, key.shape[1])
        v = _split_heads(value @ Wv + bv, B, value.shape[1])
        scores = jnp.einsum('bhqd,bhkd->bhqk', q, k) / jnp.sqrt(jnp.asarray(D_K, q.dtype))
        p_attn = jax.nn.softmax(scores, axis=-1)
        x = jnp.einsum('bhqk,bhkd->bhqd', p_attn, v)
        x = x.transpose(0, 2, 1, 3).reshape(B, S, H * D_K)
        return x @ Wo + bo

    def _L0_ffn_ref(hidden_states, w_q, w_k, w_v, w_o, g1, g2, w_gate, w1, w3, w2):
        import jax, jax.numpy as jnp
        import numpy as np
        H, KVH, HD, D = (8, 2, 128, 256)
        E, TOPK, FFN = (8, 2, 896)
        THETA, EPS = (1000000.0, 1e-05)
        NBITS, GS = (4, 128)
        QMAX = float(2 ** NBITS - 1)
        NEG = -1e+30

        def qgroup(w):
            shp = w.shape
            w2 = w.reshape(-1, GS)
            wmax = jnp.max(w2, -1, keepdims=True)
            wmin = jnp.min(w2, -1, keepdims=True)
            scales = jnp.clip(wmax - wmin, 1e-05, None) / QMAX
            base = jnp.clip(jnp.round(-wmin / scales), 0.0, QMAX)
            wq = (jnp.clip(jnp.round(w2 / scales) + base, 0.0, QMAX) - base) * scales
            return wq.reshape(shp)

        def rms(x, g):
            return x * jax.lax.rsqrt(jnp.mean(x * x, -1, keepdims=True) + EPS) * g

        def rot_half(x):
            h = x.shape[-1] // 2
            return jnp.concatenate([-x[..., h:], x[..., :h]], axis=-1)
        B, S, _ = hidden_states.shape
        T = B * S
        xn = rms(hidden_states, g1)
        q = (xn @ qgroup(w_q).T).reshape(B, S, H, HD).transpose(0, 2, 1, 3)
        k = (xn @ qgroup(w_k).T).reshape(B, S, KVH, HD).transpose(0, 2, 1, 3)
        v = (xn @ qgroup(w_v).T).reshape(B, S, KVH, HD).transpose(0, 2, 1, 3)
        k = qgroup(k)
        pos = jnp.arange(S, dtype=jnp.float32)
        inv = 1.0 / THETA ** (jnp.arange(0, HD, 2, dtype=jnp.float32) / HD)
        freqs = pos[:, None] * inv[None, :]
        emb = jnp.concatenate([freqs, freqs], axis=-1)
        cos = jnp.cos(emb)[None, None]
        sin = jnp.sin(emb)[None, None]
        q = q * cos + rot_half(q) * sin
        k = k * cos + rot_half(k) * sin
        rep = H // KVH
        k = jnp.repeat(k, rep, axis=1)
        v = jnp.repeat(v, rep, axis=1)
        v = qgroup(v)
        scores = jnp.einsum('bhqd,bhkd->bhqk', q, k) / np.float32(np.sqrt(HD))
        causal = jnp.tril(jnp.ones((S, S), dtype=bool))
        scores = jnp.where(causal[None, None], scores, NEG)
        attn = jax.nn.softmax(scores, axis=-1)
        o = jnp.einsum('bhqk,bhkd->bhqd', attn, v).transpose(0, 2, 1, 3).reshape(B, S, H * HD)
        h = hidden_states + o @ qgroup(w_o).T
        hn = rms(h, g2).reshape(T, D)
        logits = hn @ w_gate.T
        probs = jax.nn.softmax(logits, axis=-1)
        tv, ti = jax.lax.top_k(probs, TOPK)
        tv = tv / jnp.sum(tv, axis=-1, keepdims=True)
        rw = jnp.zeros((T, E), hn.dtype).at[jnp.arange(T)[:, None], ti].set(tv)
        moe = jnp.zeros((T, D), hn.dtype)
        for e in range(E):
            up = jax.nn.silu(hn @ qgroup(w1[e]).T) * (hn @ qgroup(w3[e]).T)
            moe = moe + rw[:, e:e + 1] * (up @ qgroup(w2[e]).T)
        return h + moe.reshape(B, S, D)
    x = _layernorm(x + _L0_attn_ref(x, L0_attn_rkv_w, L0_attn_out_w, L0_attn_time_decay, L0_attn_time_first, L0_attn_time_decay_rev, L0_attn_time_first_rev), axis=-1)
    x = _layernorm(x + _L0_xattn_ref(x, ctx_1024, ctx_1024, L0_xattn_Wq, L0_xattn_bq, L0_xattn_Wk, L0_xattn_bk, L0_xattn_Wv, L0_xattn_bv, L0_xattn_Wo, L0_xattn_bo), axis=-1)
    x = _layernorm(x + _L0_ffn_ref(x, L0_ffn_w_q, L0_ffn_w_k, L0_ffn_w_v, L0_ffn_w_o, L0_ffn_g1, L0_ffn_g2, L0_ffn_w_gate, L0_ffn_w1, L0_ffn_w3, L0_ffn_w2), axis=-1)
    return x

_drawn_inputs = setup_inputs


def setup_inputs(seed=0):
    import zlib

    import numpy as np

    out = dict(_drawn_inputs(seed))
    spreads = {'L0_xattn_bq': (0.0, 0.396),
     'L0_xattn_bk': (0.0, 0.8),
     'L0_xattn_bv': (0.0, 0.1),
     'L0_xattn_bo': (0.0, 0.1),
     'L0_ffn_g1': (1.0, 0.6),
     'L0_ffn_g2': (1.0, 0.6)}
    factors = {'L0_attn_time_decay': 8.0,
     'L0_attn_time_first': 6.195,
     'L0_attn_time_decay_rev': 8.0,
     'L0_attn_time_first_rev': 5.555,
     'L0_ffn_w_q': 8.0,
     'L0_ffn_w_k': 8.0,
     'L0_ffn_w_gate': 5.075,
     'L0_ffn_w1': 4.604,
     'L0_ffn_w3': 4.524,
     'L0_ffn_w2': 4.525}
    for name, (base, spread) in spreads.items():
        noise = np.random.default_rng([zlib.crc32(name.encode()), seed]).standard_normal(out[name].shape)
        drawn = base * np.exp(spread * noise) if base else spread * noise
        out[name] = jnp.asarray(drawn.astype(out[name].dtype))
    for name, factor in factors.items():
        out[name] = (out[name] * factor).astype(out[name].dtype)
    return out
```

```python
from contextlib import ExitStack

import numpy as np

import concourse.bass as bass
from concourse import mybir

F32 = mybir.dt.float32
I32 = mybir.dt.int32
ALU = mybir.AluOpType
ACT = mybir.ActivationFunctionType
AX = mybir.AxisListType

P = 128
B, S, D = 16, 128, 256
TOK = B * S
DC = D // P
GROUPS, GB = 4, 4
GT = GB * S
UNITS = 4
XH, XK = 16, 16
HALF = 8
QH, KVH, HD = 8, 2, 128
REP = QH // KVH
E, FFN = 8, 896
FC = FFN // P
LEVELS = 15.0
TILES = 14
JOBS = 27
ROWS = 256
BLOCKS = (2 * TOK + E * (ROWS - 1)) // ROWS
SORTED = BLOCKS * ROWS
MAGIC = 12582912.0
LOWEST = -1e38
MASKED = -1e30
EPS = 1e-5

C_ID, C_COS, C_SIN, C_MASK, C_BEFORE, C_ONES, C_HEAD = 0, 128, 256, 384, 512, 640, 768
C_IOTA, C_BLOCK, C_END = 776, 784, 784 + BLOCKS


class Steps:

    def __init__(self, eng, sem):
        self.eng, self.sem, self.start, self.base, self.at = eng, sem, 0, 0, 0

    def did(self, ins):
        ins.then_inc(self.sem, 1)
        self.at += 1

    def wait(self):
        self.eng.wait_ge(self.sem, self.base + self.at)

    def turn(self, i, per):
        self.base, self.at = self.start + i * per, 0

    def done(self, turns, per):
        assert self.at == per, f"{self.at} steps a turn, not {per}"
        self.start += turns * per
        self.base, self.at = self.start, 0


def wide(ap, n):
    p, a = ap.shape
    return ap.rearrange("p (a o) -> p a o", o=1).to_broadcast([p, a, n])


def each(ap, n):
    p, w = ap.shape
    return ap.rearrange("p (o w) -> p o w", o=1).to_broadcast([p, n, w])



class Shared:

    def __init__(self, nc, t, out, top):
        self.nc, self.t, self.out, self.top = nc, t, out, top
        self.steps = {}

        def dram(name, shape):
            return nc.dram_tensor(name, shape, F32, kind="Internal").ap()

        self.weights_d = dram("weights_d", (JOBS, P, TILES * P))
        self.mixed_d = dram("mixed_d", (TOK, D))
        self.crossed_d = dram("crossed_d", (TOK, D))
        self.hidden_d = dram("hidden_d", (TOK, D))
        self.normed_d = dram("normed_d", (TOK, D))
        self.sorted_d = dram("sorted_d", (SORTED, D))
        self.expert_d = dram("expert_d", (SORTED, D))
        self.banks = top.enter_context(nc.psum_tensor("banks", [P, 8, 512], F32))
        self.consts = self.buffer(top, "consts", [C_END])
        self.ident = self.consts[:, C_ID:C_ID + P]
        self.magic = self.buffer(top, "magic", [1])
        self.minus_half = self.buffer(top, "minus_half", [4])
        self.logits = self.buffer(top, "logits", [B, E])
        self.zeros = self.buffer(top, "zeros", [D])
        self.places = self.buffer(top, "places", [2, B], I32)
        self.shares = self.buffer(top, "shares", [2, B])
        self.block_expert = self.buffer(top, "block_expert", [BLOCKS], I32)
        self.s_consts = self.semaphore("s_consts")
        self.s_fill = self.semaphore("s_fill")
        self.s_zeroed = self.semaphore("s_zeroed")
        self.s_held = self.semaphore("s_held")

    def semaphore(self, name):
        return self.top.enter_context(self.nc.semaphore(name))

    def buffer(self, stack, name, shape, dt=F32):
        return stack.enter_context(self.nc.sbuf_tensor(name, [P] + shape, dt))


def prep_stage(k):
    nc, t, banks = k.nc, k.t, k.banks
    with ExitStack() as own:
        raw = [k.buffer(own, f"raw{j}", [TILES, P]) for j in range(3)]
        level = [k.buffer(own, f"level{j}", [TILES, P]) for j in range(3)]
        turned = [k.buffer(own, f"turned{j}", [TILES, P]) for j in range(3)]
        stat = [k.buffer(own, f"stat{j}", [8, TILES]) for j in range(3)]
    raw_in = [k.semaphore(f"raw_in{j}") for j in range(3)]
    stored = [k.semaphore(f"stored{j}") for j in range(3)]
    slot_free = k.semaphore("slot_free")
    scale_ready = k.semaphore("scale_ready")
    rounded = k.semaphore("rounded")
    clipped = k.semaphore("clipped")
    tiles_turned = k.semaphore("tiles_turned")
    bank_read = k.semaphore("bank_read")
    dequantised = k.semaphore("dequantised")
    TURNS, BANKS_JOB = JOBS // 3, 4
    MAX, MIN, SCALE, INV, BASE, LOW, HIGH, TMP = range(8)

    def sync(sp):
        sp.sem_inc(slot_free, 3)
        with sp.Fori(0, TURNS) as i:
            for j in range(3):
                sp.wait_ge(slot_free, 3 * i + j + 1)
                sp.dma_start(raw[j][:, :, :], t["weight_jobs"][bass.ds(3 * i + j, 1)].rearrange(
                    "o p (a b) -> (o p) a b", a=TILES)).then_inc(raw_in[j], 16)
            for j in range(3):
                sp.wait_ge(bank_read, (3 * i + j + 2) * BANKS_JOB)
                sp.dma_start(k.weights_d[bass.ds(3 * i + j, 1)].rearrange("o p (a b) -> (o p) a b", a=TILES),
                             turned[j][:, :, :]).then_inc(stored[j], 16)
            for j in range(3):
                sp.wait_ge(stored[j], 16 * i + 16)
                sp.sem_inc(slot_free, 1)

    def vector(dve):
        st = k.steps["dve"]
        PER = 3 * 8
        with dve.Fori(0, TURNS) as i:
            st.turn(i, PER)
            for j in range(3):
                a = stat[j]
                dve.wait_ge(raw_in[j], 16 * i + 16)
                dve.tensor_reduce(a[:, MAX, :], raw[j][:, :, :], AX.X, ALU.max)
                st.did(dve.tensor_reduce(a[:, MIN, :], raw[j][:, :, :], AX.X, ALU.min))
                st.wait()
                st.did(dve.tensor_tensor(a[:, TMP, :], a[:, MAX, :], a[:, MIN, :], ALU.subtract))
                st.wait()
                st.did(dve.tensor_scalar(a[:, SCALE, :], a[:, TMP, :], 1e-5, 1.0 / LEVELS, ALU.max, ALU.mult))
                st.wait()
                st.did(dve.reciprocal(a[:, INV, :], a[:, SCALE, :]))
                st.wait()
                st.did(dve.scalar_tensor_tensor(out=a[:, TMP, :], in0=a[:, MIN, :], scalar=-1.0,
                                                in1=a[:, INV, :], op0=ALU.mult, op1=ALU.mult))
                st.wait()
                st.did(dve.tensor_scalar(a[:, BASE, :], a[:, TMP, :], MAGIC, MAGIC, ALU.add, ALU.subtract))
                st.wait()
                st.did(dve.tensor_scalar(a[:, TMP, :], a[:, BASE, :], 0.0, LEVELS, ALU.max, ALU.min))
                st.wait()
                st.did(dve.tensor_scalar(a[:, LOW, :], a[:, TMP, :], -1.0, MAGIC, ALU.mult, ALU.add))
                st.wait()
                dve.tensor_scalar(a[:, HIGH, :], a[:, LOW, :], LEVELS, None, ALU.add).then_inc(scale_ready, 1)
            for j in range(3):
                a = stat[j]
                dve.wait_ge(rounded, 3 * i + j + 1)
                for n in range(TILES):
                    last = dve.tensor_scalar(level[j][:, n, :], level[j][:, n, :], a[:, LOW, n:n + 1],
                                             a[:, HIGH, n:n + 1], ALU.max, ALU.min)
                last.then_inc(clipped, 1)
        st.done(TURNS, PER)

    def scalar(act):
        with act.Fori(0, TURNS) as i:
            for j in range(3):
                act.wait_ge(scale_ready, 3 * i + j + 1)
                for n in range(TILES):
                    last = act.activation(level[j][:, n, :], raw[j][:, n, :], ACT.Identity, bias=k.magic[:, :],
                                          scale=stat[j][:, INV, n:n + 1])
                last.then_inc(rounded, 1)
            for j in range(3):
                for b in range(BANKS_JOB):
                    n = min(4, TILES - 4 * b)
                    act.wait_ge(tiles_turned, (3 * i + j) * BANKS_JOB + b + 1)
                    act.copy(turned[j][:, 4 * b:4 * b + n, :],
                                    banks[:, 4 * (j % 2) + b, 0:n * P].rearrange("p (a b) -> p a b", a=n)).then_inc(bank_read, 1)

    def gpsimd(pool):
        with pool.Fori(0, TURNS) as i:
            for j in range(3):
                pool.wait_ge(clipped, 3 * i + j + 1)
                pool.sem_inc(k.s_held, 1)
                for n in range(TILES):
                    last = pool.tensor_scalar(level[j][:, n, :], level[j][:, n, :], -MAGIC,
                                              stat[j][:, SCALE, n:n + 1], ALU.add, ALU.mult)
                last.then_inc(dequantised, 1)

    def tensor(pe):
        pe.sem_inc(bank_read, BANKS_JOB)
        with pe.Fori(0, TURNS) as i:
            for j in range(3):
                pe.wait_ge(dequantised, 3 * i + j + 1)
                for b in range(BANKS_JOB):
                    if j == 0:
                        pe.wait_ge(bank_read, 3 * i * BANKS_JOB + b + 1)
                    if j == 2:
                        pe.wait_ge(bank_read, (3 * i + 1) * BANKS_JOB + b + 1)
                    for n in range(min(4, TILES - 4 * b)):
                        last = pe.transpose(banks[:, 4 * (j % 2) + b, n * P:(n + 1) * P],
                                            level[j][:, 4 * b + n, :], k.ident)
                    last.then_inc(tiles_turned, 1)

    return sync, tensor, vector, scalar, gpsimd


def mix_stage(k):
    nc, t, banks = k.nc, k.t, k.banks
    with ExitStack() as own:
        x_turned = [k.buffer(own, f"x_turned{d}", [DC, TOK]) for d in range(2)]
        x_rows = k.buffer(own, "x_rows", [B, D])
        w_rkv = k.buffer(own, "w_rkv", [DC, 6 * D])
        w_out = k.buffer(own, "w_out", [UNITS, D])
        decay = k.buffer(own, "decay", [UNITS])
        first = k.buffer(own, "first", [UNITS])
        step_decay = k.buffer(own, "step_decay", [UNITS])
        top = [k.buffer(own, f"top{p}", [GB, S + 1]) for p in range(2)]
        gap = [k.buffer(own, f"gap{p}", [2, GT]) for p in range(2)]
        weight = [k.buffer(own, f"weight{p}", [4, GT]) for p in range(2)]
        values = [k.buffer(own, f"values{p}", [GT]) for p in range(2)]
        gate = [k.buffer(own, f"gate{p}", [GT]) for p in range(2)]
        new_value = [k.buffer(own, f"new_value{p}", [2, GT]) for p in range(2)]
        carry = [k.buffer(own, f"carry{p}", [2, GT + 1]) for p in range(2)]
        old_part = [k.buffer(own, f"old_part{p}", [2, GT]) for p in range(2)]
        ratio = [k.buffer(own, f"ratio{p}", [2, GT]) for p in range(2)]
        y = k.buffer(own, "y", [UNITS, GB, S])
        summed = k.buffer(own, "summed", [GB, D])
        mixed = k.buffer(own, "mixed", [GB, D])
        ln_stat = k.buffer(own, "ln_stat", [GB, 6])
        ln_mean = k.buffer(own, "ln_mean", [GB, 2])
        ln_eps = k.buffer(own, "ln_eps", [GB])
        ln_scale = k.buffer(own, "ln_scale", [GB])
    mix_loads = k.semaphore("mix_loads")
    decay_ready = k.semaphore("decay_ready")
    rkv_ready = k.semaphore("rkv_ready")
    vr_ready = k.semaphore("vr_ready")
    gaps_ready = k.semaphore("gaps_ready")
    weights_ready = k.semaphore("weights_ready")
    new_ready = k.semaphore("new_ready")
    scans_ready = k.semaphore("scans_ready")
    old_ready = k.semaphore("old_ready")
    unit_done = k.semaphore("unit_done")
    mix_out = k.semaphore("mix_out")
    mix_var = k.semaphore("mix_var")
    mix_scale = k.semaphore("mix_scale")
    mix_normed = k.semaphore("mix_normed")
    k.mix_stored = k.semaphore("mix_stored")
    mix_free = k.semaphore("mix_free")
    LOADS = 7
    FROM_PAST, FROM_NEW, OLD, NOW = range(4)

    def sync(sp):
        for src, dst in ((t["rkv_t"], w_rkv), (t["x_fwd_t"], x_turned[0]), (t["x_bwd_t"], x_turned[1])):
            sp.dma_start(dst[:, :, :], src.rearrange("(c p) n -> p c n", p=P)).then_inc(mix_loads, 16)
        sp.dma_start(decay[:, :], t["decay"]).then_inc(mix_loads, 16)
        sp.dma_start(first[:, :], t["first"]).then_inc(mix_loads, 16)
        sp.dma_start(w_out[:, :, :], t["out_t"].rearrange("(c p) n -> p c n", p=P)).then_inc(mix_loads, 16)
        sp.dma_start(x_rows[:, :, :], t["x"].rearrange("(b p) n -> p b n", p=P)).then_inc(mix_loads, 16)
        sp.sem_inc(mix_free, 1)
        with sp.Fori(0, GROUPS) as g:
            sp.wait_ge(mix_normed, g + 1)
            sp.dma_start(k.mixed_d[bass.ds(g * GT, GT), :].rearrange("(b p) n -> p b n", p=P),
                         mixed[:, :, :]).then_inc(k.mix_stored, 16)
            sp.wait_ge(k.mix_stored, 16 * g + 16)
            sp.sem_inc(mix_free, 1)

    def tensor(pe):
        pe.wait_ge(mix_loads, 16 * LOADS)

        def project(g, u, n, wait=True):
            d, c = u // DC, u % DC
            if wait:
                pe.wait_ge(vr_ready, n - 1)
                pe.wait_ge(gaps_ready, n - 1)
            for m in range(3):
                for kc in range(DC):
                    col = (3 * d + m) * D + c * P
                    last = pe.matmul(banks[:, 3 * (u % 2) + m, :], w_rkv[:, kc, col:col + P],
                                     x_turned[d][:, kc, bass.ds(g * GT, GT)], start=(kc == 0), stop=(kc == DC - 1))
            last.then_inc(rkv_ready, 1)

        def project_out(g):
            pe.wait_ge(unit_done, 2 + UNITS * g + UNITS)
            for b in range(GB):
                if b % 2 == 0:
                    pe.wait_ge(mix_free, g + 1)
                for u in range(UNITS):
                    last = pe.matmul(banks[:, 6 + b // 2, (b % 2) * D:(b % 2 + 1) * D], y[:, u, b, :],
                                     w_out[:, u, :], start=(u == 0), stop=(u == UNITS - 1))
                if b % 2:
                    last.then_inc(mix_out, 1)

        project(0, 0, 0, False)
        project(0, 1, 1, False)
        with pe.Fori(0, GROUPS - 1) as g:
            for u in range(UNITS):
                project(g + (u + 2) // UNITS, (u + 2) % UNITS, UNITS * g + u + 2)
            project_out(g)
        for u in (2, 3):
            project(GROUPS - 1, u, UNITS * (GROUPS - 1) + u)
        project_out(GROUPS - 1)

    def scalar(act):
        act.wait_ge(mix_loads, 16 * LOADS)
        act.activation(step_decay[:, :], decay[:, :], ACT.Exp).then_inc(decay_ready, 1)
        with act.Fori(0, GROUPS) as g:
            for u in range(UNITS):
                p, n = u % 2, UNITS * g + u
                act.wait_ge(rkv_ready, n + 1)
                act.wait_ge(unit_done, n + 1)
                act.activation(gate[p][:, :], banks[:, 3 * p, :], ACT.Exp, scale=-1.0)
                act.copy(values[p][:, :], banks[:, 3 * p + 2, :]).then_inc(vr_ready, 1)
                act.wait_ge(gaps_ready, n + 1)
                act.activation(weight[p][:, :, :], weight[p][:, :, :], ACT.Exp).then_inc(weights_ready, 1)

    def gpsimd(pool):
        with pool.Fori(0, GROUPS) as g:
            for u in range(UNITS):
                p, n = u % 2, UNITS * g + u
                pool.wait_ge(weights_ready, n + 1)
                pool.tensor_tensor(new_value[p][:, 0, :], weight[p][:, FROM_NEW, :], values[p][:, :],
                                   ALU.mult).then_inc(new_ready, 1)
                pool.tensor_tensor(new_value[p][:, 1, :], weight[p][:, NOW, :], values[p][:, :], ALU.mult)
                pool.wait_ge(scans_ready, n + 1)
                for m in range(2):
                    last = pool.tensor_tensor(old_part[p][:, m, :], weight[p][:, OLD, :], carry[p][:, m, 0:GT],
                                              ALU.mult)
                last.then_inc(old_ready, 1)
            pool.wait_ge(mix_var, g + 1)
            pool.tensor_tensor(ln_scale[:, :], ln_eps[:, :], k.minus_half[:, 0:GB], ALU.pow).then_inc(mix_scale, 1)

    def vector(dve):
        st = k.steps["dve"]

        def gaps(u, n):
            p = u % 2
            dve.wait_ge(rkv_ready, n + 1)
            key = banks[:, 3 * p + 1, :]
            for b in range(GB):
                last = dve.tensor_tensor_scan(top[p][:, b, 1:S + 1], step_decay[:, u:u + 1].to_broadcast([P, S]),
                                              key[:, b * S:(b + 1) * S], LOWEST, ALU.add, ALU.max)
            st.did(last)
            st.wait()
            before = top[p][:, :, 0:S]
            keys = key.rearrange("p (b s) -> p b s", b=GB)
            past, now = (gap[p][:, m, :].rearrange("p (b s) -> p b s", b=GB) for m in range(2))
            dve.scalar_tensor_tensor(out=past, in0=before, scalar=step_decay[:, u:u + 1], in1=keys,
                                     op0=ALU.add, op1=ALU.subtract)
            st.did(dve.scalar_tensor_tensor(out=now, in0=keys, scalar=first[:, u:u + 1], in1=before,
                                            op0=ALU.add, op1=ALU.subtract))
            st.wait()
            dve.tensor_scalar(weight[p][:, FROM_PAST, :], gap[p][:, 0, :], 0.0, None, ALU.min)
            dve.tensor_scalar(weight[p][:, FROM_NEW, :], gap[p][:, 0, :], -1.0, 0.0, ALU.mult, ALU.min)
            dve.tensor_scalar(weight[p][:, OLD, :], gap[p][:, 1, :], -1.0, 0.0, ALU.mult, ALU.min)
            dve.tensor_scalar(weight[p][:, NOW, :], gap[p][:, 1, :], 0.0, None, ALU.min).then_inc(gaps_ready, 1)

        def scans(u, n):
            p = u % 2
            dve.wait_ge(weights_ready, n + 1)
            dve.tensor_tensor_scan(carry[p][:, 1, 1:GT + 1], weight[p][:, FROM_PAST, :], weight[p][:, FROM_NEW, :],
                                   0.0, ALU.mult, ALU.add)
            dve.wait_ge(new_ready, n + 1)
            dve.tensor_tensor_scan(carry[p][:, 0, 1:GT + 1], weight[p][:, FROM_PAST, :], new_value[p][:, 0, :],
                                   0.0, ALU.mult, ALU.add).then_inc(scans_ready, 1)

        def finish(u, n):
            p = u % 2
            dve.wait_ge(old_ready, n + 1)
            st.did(dve.tensor_tensor(ratio[p][:, 1, :], old_part[p][:, 1, :], weight[p][:, NOW, :], ALU.add))
            st.did(dve.tensor_tensor(ratio[p][:, 0, :], old_part[p][:, 0, :], new_value[p][:, 1, :], ALU.add))
            st.wait()
            st.did(dve.scalar_tensor_tensor(out=old_part[p][:, 1, :], in0=gate[p][:, :], scalar=1.0,
                                            in1=ratio[p][:, 1, :], op0=ALU.add, op1=ALU.mult))
            st.wait()
            st.did(dve.reciprocal(ratio[p][:, 1, :], old_part[p][:, 1, :]))
            st.wait()
            num, rec = (ratio[p][:, m, :].rearrange("p (b s) -> p b s", b=GB) for m in range(2))
            to = y[:, u, :, :] if u < DC else y[:, u, :, ::-1]
            dve.tensor_tensor(to, num, rec, ALU.mult).then_inc(unit_done, 1)

        def norm(g):
            for b in range(GB):
                if b % 2 == 0:
                    dve.wait_ge(mix_out, 2 * g + b // 2 + 1)
                last = dve.tensor_tensor(
                    summed[:, b:b + 1, :], banks[:, 6 + b // 2:7 + b // 2, (b % 2) * D:(b % 2 + 1) * D],
                    x_rows[:, bass.ds(GB * g + b, 1), :], ALU.add)
            st.did(last)
            st.wait()
            for b in range(GB):
                last = dve.bn_stats(ln_stat[:, b, :], summed[:, b, :])
            st.did(last)
            st.wait()
            dve.sem_inc(k.s_held, 1)
            for b in range(GB):
                last = dve.bn_aggr(ln_mean[:, b, :], ln_stat[:, b, :])
            st.did(last)
            st.wait()
            dve.tensor_scalar(ln_eps[:, :], ln_mean[:, :, 1], EPS, None, ALU.add).then_inc(mix_var, 1)
            dve.wait_ge(mix_scale, g + 1)
            dve.wait_ge(mix_free, g + 1)
            for b in range(GB):
                last = dve.tensor_scalar(mixed[:, b, :], summed[:, b, :], ln_mean[:, b, 0:1], ln_scale[:, b:b + 1],
                                         ALU.subtract, ALU.mult)
            last.then_inc(mix_normed, 1)

        dve.wait_ge(mix_loads, 16 * LOADS)
        for p in range(2):
            dve.memset(top[p][:, :, 0:1], LOWEST)
            st.did(dve.memset(carry[p][:, :, 0:1], 0.0))
        dve.sem_inc(unit_done, 2)
        dve.wait_ge(decay_ready, 1)
        st.did(dve.tensor_scalar(step_decay[:, :], step_decay[:, :], -1.0, None, ALU.mult))
        st.wait()
        st.done(1, 3)
        PER = 6 * UNITS + 3
        gaps(0, 0)
        st.done(1, 2)
        with dve.Fori(0, GROUPS - 1) as g:
            st.turn(g, PER)
            for u in range(UNITS):
                n = UNITS * g + u
                scans(u, n)
                gaps((u + 1) % UNITS, n + 1)
                finish(u, n)
            norm(g)
        st.done(GROUPS - 1, PER)
        for u in range(UNITS):
            n = UNITS * (GROUPS - 1) + u
            scans(u, n)
            if u + 1 < UNITS:
                gaps(u + 1, n + 1)
            finish(u, n)
        norm(GROUPS - 1)
        st.done(1, PER - 2)

    return sync, tensor, vector, scalar, gpsimd


def norm_stats(k, dve, st, stats, mean, eps, rows):
    st.did(dve.bn_stats(stats, rows))
    st.wait()
    dve.sem_inc(k.s_held, 1)
    st.did(dve.bn_aggr(mean, stats))
    st.wait()
    return dve.tensor_scalar(eps, mean[:, 1:2], EPS, None, ALU.add)


def cross_stage(k):
    nc, t, banks = k.nc, k.t, k.banks
    with ExitStack() as own:
        wq, wk, wv, wo = (k.buffer(own, n, [DC, D]) for n in ("w_q", "w_k", "w_v", "w_o"))
        bqk = k.buffer(own, "bqk", [2 * DC])
        bias_rows = k.buffer(own, "bias_rows", [2, D])
        x_in = [k.buffer(own, f"x_in{j}", [D]) for j in range(2)]
        ctx_t = [k.buffer(own, f"ctx_t{j}", [DC, S]) for j in range(2)]
        x_t = [k.buffer(own, f"x_t{j}", [DC, S]) for j in range(2)]
        q_t = [k.buffer(own, f"q_t{j}", [DC, S]) for j in range(2)]
        k_t = [k.buffer(own, f"k_t{j}", [DC, S]) for j in range(2)]
        spread = [k.buffer(own, f"spread{h}", [HALF, S]) for h in range(2)]
        v_ones = [k.buffer(own, f"v_ones{j}", [XH, XK + 1]) for j in range(2)]
        x_bias = [k.buffer(own, f"x_bias{j}", [D]) for j in range(2)]
        peak = [k.buffer(own, f"peak{h}", [HALF]) for h in range(2)]
        probs = [k.buffer(own, f"probs{h}", [HALF, S]) for h in range(2)]
        probs_t = [k.buffer(own, f"probs_t{h}", [HALF, S]) for h in range(2)]
        total = k.buffer(own, "total", [XH])
        heads = [k.buffer(own, f"heads{j}", [XH, XK]) for j in range(2)]
        heads_t = [k.buffer(own, f"heads_t{j}", [DC, S]) for j in range(2)]
        joined = [k.buffer(own, f"joined{j}", [D]) for j in range(2)]
        ln = [k.buffer(own, f"cross_ln{j}", [12]) for j in range(2)]
        crossed = [k.buffer(own, f"crossed{j}", [D]) for j in range(2)]
    cross_loads = k.semaphore("cross_loads")
    rows_in = [k.semaphore(f"rows_in{j}") for j in range(2)]
    x_turned = k.semaphore("cross_x_turned")
    x_t_ready = k.semaphore("x_t_ready")
    qk_ready = k.semaphore("qk_ready")
    qk_read = k.semaphore("qk_read")
    v_ready = k.semaphore("v_ready")
    v_read = k.semaphore("v_read")
    spread_ready = k.semaphore("spread_ready")
    bias_added = k.semaphore("bias_added")
    scores_ready = k.semaphore("scores_ready")
    scores_read = k.semaphore("scores_read")
    exp_ready = k.semaphore("exp_ready")
    probs_turned = k.semaphore("probs_turned")
    probs_t_ready = k.semaphore("probs_t_ready")
    heads_summed = k.semaphore("heads_summed")
    heads_ready = k.semaphore("heads_ready")
    heads_turned = k.semaphore("heads_turned")
    heads_t_ready = k.semaphore("heads_t_ready")
    joined_ready = k.semaphore("joined_ready")
    cross_var = k.semaphore("cross_var")
    cross_scale = k.semaphore("cross_scale")
    cross_normed = k.semaphore("cross_normed")
    k.cross_stored = [k.semaphore(f"cross_stored{j}") for j in range(2)]
    LOADS = 7
    TURNS = B // 2
    TURN, QK, V, SCORES, PROBS_T, HEADS = 0, 1, 2, 3, 5, 7

    joined_read = k.semaphore("joined_read")

    def sync(sp):
        for n, dst in (("wq", wq), ("wk", wk), ("wv", wv), ("wo", wo)):
            sp.dma_start(dst[:, :, :], t[n].rearrange("(c p) n -> p c n", p=P)).then_inc(cross_loads, 16)
        sp.dma_start(bqk[:, :], t["bqk"]).then_inc(cross_loads, 16)
        for m in range(2):
            sp.dma_start(bias_rows[:, m, :], t["rows"][m:m + 1, :].to_broadcast([P, D])).then_inc(cross_loads, 16)
        for j in range(2):
            sp.sem_inc(k.cross_stored[j], 16)

        def load(j, n):
            sp.dma_start(x_in[j][:, :], k.mixed_d[bass.ds(n * S, S), :]).then_inc(rows_in[j], 16)
            sp.dma_start(ctx_t[j][:, :, :], t["ctx_t"].rearrange("(c p) n -> p c n", p=P)[
                :, :, bass.ds(n * S, S)]).then_inc(rows_in[j], 16)

        def store(j, n):
            sp.wait_ge(cross_normed, n + 1)
            sp.dma_start(k.crossed_d[bass.ds(n * S, S), :], crossed[j][:, :]).then_inc(k.cross_stored[j], 16)

        load(0, 0)
        load(1, 1)
        with sp.Fori(0, TURNS - 1) as i:
            for j in range(2):
                n = 2 * i + j
                sp.wait_ge(qk_ready, n + 1)
                sp.wait_ge(bias_added, n + 1)
                load(j, n + 2)
                store(j, n)
        for j in range(2):
            store(j, B - 2 + j)
            sp.wait_ge(k.cross_stored[j], 16 * TURNS + 16)

    def tensor(pe):
        pe.wait_ge(cross_loads, 16 * LOADS)
        pe.sem_inc(scores_ready, 2)
        pe.sem_inc(probs_turned, 4)

        def front(j, n, i, begin=False):
            pe.wait_ge(rows_in[j], 32 * i + 32)
            if not begin:
                pe.wait_ge(heads_t_ready, n)
            for c in range(DC):
                last = pe.transpose(banks[:, TURN, c * P:(c + 1) * P], x_in[j][:, c * P:(c + 1) * P], k.ident)
            last.then_inc(x_turned, 1)
            if not begin:
                pe.wait_ge(v_read, n)
                pe.wait_ge(joined_read, n)
            for c in range(DC):
                last = pe.matmul(banks[:, V, 0:D], ctx_t[j][:, c, :], wv[:, c, :], start=(c == 0), stop=(c == DC - 1))
            last.then_inc(v_ready, 1)
            if not begin:
                pe.wait_ge(qk_read, n)
            for m in range(DC):
                for c in range(DC):
                    pe.matmul(banks[:, QK, (DC + m) * P:(DC + m + 1) * P], wk[:, c, m * P:(m + 1) * P],
                              ctx_t[j][:, c, :], start=(c == 0), stop=(c == DC - 1))
            pe.wait_ge(x_t_ready, n + 1)
            for m in range(DC):
                for c in range(DC):
                    last = pe.matmul(banks[:, QK, m * P:(m + 1) * P], wq[:, c, m * P:(m + 1) * P],
                                     x_t[j][:, c, :], start=(c == 0), stop=(c == DC - 1))
            last.then_inc(qk_ready, 1)

        def scores(j, h, n, begin=False):
            pe.wait_ge(spread_ready, 2 * n + h + 1)
            if not begin:
                pe.wait_ge(scores_read, 2 * n + h)
            for m in range(2):
                last = pe.matmul(banks[:, SCORES + m, :], q_t[j][:, h, :],
                                 spread[h][:, 4 * m:4 * m + 4, :].rearrange("p h s -> p (h s)"), start=True, stop=True)
            last.then_inc(scores_ready, 1)

        def sums(j, h, n):
            pe.wait_ge(exp_ready, 2 * n + h + 1)
            for m in range(2):
                pe.wait_ge(probs_t_ready, 4 * n + 2 * h + m + 1)
                for a in range(4):
                    last = pe.transpose(banks[:, PROBS_T + m, a * P:(a + 1) * P], probs[h][:, 4 * m + a, :], k.ident)
                last.then_inc(probs_turned, 1)
            if h == 0:
                pe.wait_ge(v_read, n + 1)
                pe.wait_ge(heads_ready, n + 1)
            for m in range(2):
                pe.wait_ge(probs_t_ready, 4 * n + 2 * h + m + 3)
                for a in range(4):
                    head = HALF * h + 4 * m + a
                    last = pe.matmul(banks[:, HEADS, head * (XK + 1):(head + 1) * (XK + 1)], probs_t[h][:, 4 * m + a, :],
                                     v_ones[j][:, head, :], start=True, stop=True)
            if h:
                last.then_inc(heads_summed, 1)

        def back(j, n, more):
            pe.wait_ge(heads_ready, n + 2)
            pe.wait_ge(x_t_ready, n + 1 + more)
            for c in range(DC):
                last = pe.transpose(banks[:, TURN, c * P:(c + 1) * P],
                                    heads[j][:, HALF * c:HALF * (c + 1), :].rearrange("p h d -> p (h d)"), k.ident)
            last.then_inc(heads_turned, 1)
            pe.wait_ge(heads_t_ready, n + 2)
            pe.wait_ge(v_read, n + 1 + more)
            for c in range(DC):
                last = pe.matmul(banks[:, V, 0:D], heads_t[j][:, c, :], wo[:, c, :], start=(c == 0), stop=(c == DC - 1))
            last.then_inc(joined_ready, 1)

        def element(j, n, i, more):
            if more:
                front(1 - j, n + 1, i + j)
            scores(j, 1, n)
            sums(j, 0, n)
            if more:
                scores(1 - j, 0, n + 1)
            sums(j, 1, n)
            back(j, n, more)

        front(0, 0, 0, True)
        scores(0, 0, 0, True)
        with pe.Fori(0, TURNS - 1) as i:
            for j in range(2):
                element(j, 2 * i + j, i, 1)
        element(0, B - 2, TURNS - 1, 1)
        element(1, B - 1, TURNS - 1, 0)

    def scalar(act):
        act.wait_ge(cross_loads, 16 * LOADS)
        act.sem_inc(heads_t_ready, 1)
        act.sem_inc(probs_t_ready, 2)

        def front(j, n):
            act.wait_ge(x_turned, n + 1)
            act.copy(x_t[j][:, :, :], banks[:, TURN, 0:D].rearrange("p (c s) -> p c s", c=DC)).then_inc(x_t_ready, 1)
            act.wait_ge(qk_ready, n + 1)
            for c in range(DC):
                act.activation(k_t[j][:, c, :], banks[:, QK, (DC + c) * P:(DC + c + 1) * P], ACT.Identity,
                               bias=bqk[:, DC + c:DC + c + 1])
            for c in range(DC):
                last = act.activation(q_t[j][:, c, :], banks[:, QK, c * P:(c + 1) * P], ACT.Identity,
                                      bias=bqk[:, c:c + 1])
            last.then_inc(qk_read, 1)

        def soften(h, n):
            act.wait_ge(scores_read, 2 * n + h + 1)
            act.activation(probs[h][:, :, :], probs[h][:, :, :], ACT.Exp, scale=float(XK) ** -0.5).then_inc(exp_ready, 1)

        def collect(h, n):
            for m in range(2):
                act.wait_ge(probs_turned, 4 * n + 2 * h + m + 5)
                act.copy(probs_t[h][:, 4 * m:4 * m + 4, :], banks[:, PROBS_T + m, :].rearrange(
                    "p (a s) -> p a s", a=4)).then_inc(probs_t_ready, 1)

        def back(j, n):
            act.wait_ge(heads_turned, n + 1)
            act.copy(heads_t[j][:, :, :], banks[:, TURN, 0:D].rearrange("p (c s) -> p c s", c=DC)).then_inc(
                heads_t_ready, 1)

        def element(j, n, more):
            if more:
                front(1 - j, n + 1)
            soften(1, n)
            collect(0, n)
            if more:
                soften(0, n + 1)
            collect(1, n)
            back(j, n)

        front(0, 0)
        soften(0, 0)
        with act.Fori(0, TURNS - 1) as i:
            for j in range(2):
                element(j, 2 * i + j, 1)
        element(0, B - 2, 1)
        element(1, B - 1, 0)

    def gpsimd(pool):
        pool.wait_ge(cross_loads, 16 * LOADS)
        head_mask = k.consts[:, C_HEAD:C_HEAD + HALF]

        def spread_keys(j, h, n):
            pool.wait_ge(qk_read, n + 1)
            pool.wait_ge(scores_ready, 2 * n + h + 1)
            pool.tensor_tensor(spread[h][:, :, :], each(k_t[j][:, h, :], HALF), wide(head_mask, S),
                               ALU.mult).then_inc(spread_ready, 1)

        def add_bias(j, n, i, begin=False):
            pool.wait_ge(rows_in[j], 32 * i + 32)
            if not begin:
                pool.wait_ge(joined_read, n)
            pool.tensor_tensor(x_bias[j][:, :], x_in[j][:, :], bias_rows[:, 1, :], ALU.add).then_inc(bias_added, 1)

        def element(j, n, i, more):
            if more:
                add_bias(1 - j, n + 1, i + j)
                spread_keys(1 - j, 0, n + 1)
                spread_keys(1 - j, 1, n + 1)
            pool.wait_ge(cross_var, n + 1)
            pool.tensor_tensor(ln[j][:, 9:10], ln[j][:, 8:9], k.minus_half[:, 0:1], ALU.pow).then_inc(cross_scale, 1)

        add_bias(0, 0, 0, True)
        for h in range(2):
            spread_keys(0, h, 0)
        with pool.Fori(0, TURNS - 1) as i:
            for j in range(2):
                element(j, 2 * i + j, i, 1)
        element(0, B - 2, TURNS - 1, 1)
        element(1, B - 1, TURNS - 1, 0)

    def vector(dve):
        st = k.steps["dve"]

        def take_values(j, n):
            dve.wait_ge(v_ready, n + 1)
            dve.tensor_tensor(v_ones[j][:, :, 0:XK], banks[:, V, 0:D].rearrange("p (h d) -> p h d", h=XH),
                              bias_rows[:, 0, :].rearrange("p (h d) -> p h d", h=XH), ALU.add).then_inc(v_read, 1)

        def peaks(h, n):
            dve.wait_ge(scores_ready, 2 * n + h + 3)
            chunk = banks[:, SCORES:SCORES + 2, :].rearrange("p m (a s) -> p (m a) s", a=4)
            st.did(dve.tensor_reduce(peak[h][:, :], chunk, AX.X, ALU.max))
            st.wait()
            dve.wait_ge(probs_turned, 4 * n + 2 * h + 2)
            dve.tensor_tensor(probs[h][:, :, :], chunk, wide(peak[h][:, :], S), ALU.subtract).then_inc(scores_read, 1)

        def normalise(j, n):
            dve.wait_ge(heads_summed, n + 1)
            all_heads = banks[:, HEADS, 0:XH * (XK + 1)].rearrange("p (h d) -> p h d", h=XH)
            st.did(dve.reciprocal(total[:, :], all_heads[:, :, XK]))
            st.wait()
            dve.tensor_tensor(heads[j][:, :, :], all_heads[:, :, 0:XK], wide(total[:, :], XK), ALU.mult).then_inc(
                heads_ready, 1)

        def join(j, n, i):
            dve.wait_ge(joined_ready, n + 1)
            dve.wait_ge(bias_added, n + 1)
            dve.tensor_tensor(joined[j][:, :], banks[:, V, 0:D], x_bias[j][:, :], ALU.add).then_inc(joined_read, 1)
            dve.wait_ge(joined_read, n + 2)
            norm_stats(k, dve, st, ln[j][:, 0:6], ln[j][:, 6:8], ln[j][:, 8:9], joined[j][:, :]).then_inc(cross_var, 1)
            dve.wait_ge(cross_scale, n + 1)
            dve.wait_ge(k.cross_stored[j], 16 * i + 16)
            dve.tensor_scalar(crossed[j][:, :], joined[j][:, :], ln[j][:, 6:7], ln[j][:, 9:10],
                              ALU.subtract, ALU.mult).then_inc(cross_normed, 1)

        def element(j, n, i, more):
            if more:
                take_values(1 - j, n + 1)
            peaks(1, n)
            if more:
                peaks(0, n + 1)
            normalise(j, n)
            join(j, n, i)

        dve.wait_ge(cross_loads, 16 * LOADS)
        dve.sem_inc(joined_read, 1)
        dve.sem_inc(heads_ready, 1)
        for j in range(2):
            dve.memset(v_ones[j][:, :, XK:XK + 1], 1.0)
        take_values(0, 0)
        peaks(0, 0)
        st.done(1, 1)
        PER = 2 * 5
        with dve.Fori(0, TURNS - 1) as i:
            st.turn(i, PER)
            for j in range(2):
                element(j, 2 * i + j, i, 1)
        st.done(TURNS - 1, PER)
        element(0, B - 2, TURNS - 1, 1)
        element(1, B - 1, TURNS - 1, 0)
        st.done(1, PER - 1)

    return sync, tensor, vector, scalar, gpsimd


def attend_stage(k):
    nc, t, banks = k.nc, k.t, k.banks
    QKV = (QH + 2 * KVH) * HD
    with ExitStack() as own:
        weights = k.buffer(own, "attend_w", [3 * TILES, P])
        gate_w = k.buffer(own, "gate_w", [DC, E])
        gains = k.buffer(own, "gains", [2, D])
        row_in = [k.buffer(own, f"row_in{j}", [D]) for j in range(2)]
        row_res = [k.buffer(own, f"row_res{j}", [D]) for j in range(2)]
        squares = [k.buffer(own, f"squares{a}", [D]) for a in range(2)]
        rms = [k.buffer(own, f"rms{a}", [3]) for a in range(2)]
        xn = k.buffer(own, "xn", [D])
        xn_t = k.buffer(own, "xn_t", [DC, S])
        q_rot = k.buffer(own, "q_rot", [QH, HD])
        q_sin = k.buffer(own, "q_sin", [QH, HD])
        kv_stat = k.buffer(own, "kv_stat", [8, 2 * KVH])
        kvq = [k.buffer(own, f"kvq{j}", [2 * KVH, HD]) for j in range(2)]
        k_rot = k.buffer(own, "k_rot", [KVH, HD])
        k_sin = k.buffer(own, "k_sin", [KVH, HD])
        q_turn = k.buffer(own, "q_turn", [QH, S])
        k_turn = k.buffer(own, "k_turn", [KVH, S])
        probs = k.buffer(own, "att_probs", [QH, S])
        low_peak = k.buffer(own, "low_peak", [QH])
        total = k.buffer(own, "att_total", [QH])
        share = k.buffer(own, "att_share", [QH])
        probs_turn = k.buffer(own, "probs_turn", [QH, S])
        o_turn = k.buffer(own, "o_turn", [QH, S])
        hidden = [k.buffer(own, f"hidden{j}", [D]) for j in range(2)]
        normed = [k.buffer(own, f"normed{j}", [D]) for j in range(2)]
        hn_turn = k.buffer(own, "hn_turn", [DC, S])
    names = ("attend_loads xn_var xn_scale xn_ready xn_turned xn_t_ready kv_ready q_ready roped_q q_rot_ready kv_scaled "
             "kv_rounded k_rot_ready q_turned q_t_ready scores2 masked peaked exped share_ready probs_ready probs_turned2 "
             "probs_t2 o_summed o_t_ready hidden_ready hn_var hn_scale hn_ready hn_turned hn_t_ready logits_ready").split()
    s = {n: k.semaphore(n) for n in names}
    k.logits_read = k.semaphore("logits_read")
    row_loaded = [k.semaphore(f"row_loaded{j}") for j in range(2)]
    res_loaded = [k.semaphore(f"res_loaded{j}") for j in range(2)]
    attend_stored = [k.semaphore(f"attend_stored{j}") for j in range(2)]
    LOADS, TURNS = 6, B // 2
    TURN, Q, KV, TURN4, TURN_K, O = 0, 1, 3, 4, 6, 6
    MAX, MIN, SCALE, INV, BASE, LOW, HIGH, TMP = range(8)
    HALF_HD = HD // 2

    def in_pipeline(emit, eng, st=None, per=None):
        with eng.Fori(0, TURNS - 1) as i:
            if st:
                st.turn(i, per)
            for j in range(2):
                emit(j, 2 * i + j, i, 2)
        if st:
            st.done(TURNS - 1, per)
        emit(0, B - 2, TURNS - 1, 1)
        emit(1, B - 1, TURNS - 1, 0)

    def sync(sp):
        for m in range(3):
            sp.dma_start(weights[:, TILES * m:TILES * (m + 1), :],
                         k.weights_d[m].rearrange("p (a b) -> p a b", a=TILES)).then_inc(s["attend_loads"], 16)
        sp.dma_start(gate_w[:, :, :], t["gate_t"].rearrange("(c p) e -> p c e", p=P)).then_inc(s["attend_loads"], 16)
        for m in range(2):
            sp.dma_start(gains[:, m, :], t["rows"][2 + m:3 + m, :].to_broadcast([P, D])).then_inc(s["attend_loads"], 16)

        def load(dst, sem, n):
            sp.dma_start(dst[:, :], k.crossed_d[bass.ds(n * S, S), :]).then_inc(sem, 16)

        def element(j, n, i, more):
            if more == 2:
                sp.wait_ge(s["xn_ready"], n + 1)
                load(row_in[j], row_loaded[j], n + 2)
            sp.wait_ge(s["hn_ready"], n + 1)
            for src, dst in ((hidden, k.hidden_d), (normed, k.normed_d)):
                sp.dma_start(dst[bass.ds(n * S, S), :], src[j][:, :]).then_inc(attend_stored[j], 16)
            if more == 2:
                load(row_res[j], res_loaded[j], n + 2)

        for j in range(2):
            sp.sem_inc(attend_stored[j], 32)
            load(row_in[j], row_loaded[j], j)
            load(row_res[j], res_loaded[j], j)
        in_pipeline(element, sp)
        for j in range(2):
            sp.wait_ge(attend_stored[j], 32 * TURNS + 32)

    def tensor(pe):
        pe.wait_ge(s["attend_loads"], 16 * LOADS)
        w_qkv = weights[:, 0:2 * QKV // P, :].rearrange("p (c r) j -> p c (r j)", c=DC)
        w_o = weights[:, 2 * QKV // P:2 * QKV // P + DC * QH, :].rearrange("p (h c) j -> p h (c j)", c=DC)

        def project(n):
            pe.wait_ge(s["xn_ready"], n + 1)
            if not isinstance(n, int) or n >= 2:
                pe.wait_ge(k.logits_read, n - 1)
            for c in range(DC):
                last = pe.transpose(banks[:, TURN, c * P:(c + 1) * P], xn[:, c * P:(c + 1) * P], k.ident)
            last.then_inc(s["xn_turned"], 1)
            pe.wait_ge(s["xn_t_ready"], n + 1)
            first = isinstance(n, int) and n == 0
            if not first:
                pe.wait_ge(s["kv_rounded"], n)
            for c in range(DC):
                last = pe.matmul(banks[:, KV, :], xn_t[:, c, :], w_qkv[:, c, QH * HD:QKV], start=(c == 0), stop=(c == DC - 1))
            last.then_inc(s["kv_ready"], 1)
            if not first:
                pe.wait_ge(s["masked"], n)
            for m in range(2):
                for c in range(DC):
                    last = pe.matmul(banks[:, Q + m, :], xn_t[:, c, :], w_qkv[:, c, 512 * m:512 * m + 512],
                                     start=(c == 0), stop=(c == DC - 1))
            last.then_inc(s["q_ready"], 1)

        def turn_qk(n):
            first = isinstance(n, int) and n == 0
            pe.wait_ge(s["q_rot_ready"], n + 1)
            for m in range(2):
                if not first:
                    pe.wait_ge(s["probs_t2"], 2 * n)
                for a in range(4):
                    last = pe.transpose(banks[:, TURN4 + m, a * P:(a + 1) * P], q_rot[:, 4 * m + a, :], k.ident)
                last.then_inc(s["q_turned"], 1)
            pe.wait_ge(s["k_rot_ready"], n + 1)
            if not first:
                pe.wait_ge(s["o_t_ready"], 2 * n)
            for a in range(KVH):
                last = pe.transpose(banks[:, TURN_K, a * P:(a + 1) * P], k_rot[:, a, :], k.ident)
            last.then_inc(s["q_turned"], 1)

        def scores(n):
            pe.wait_ge(s["q_t_ready"], 3 * n + 3)
            for h in range(QH):
                last = pe.matmul(banks[:, Q + h // 4, (h % 4) * S:(h % 4 + 1) * S], q_turn[:, h, :], k_turn[:, h // REP, :],
                                 start=True, stop=True)
            last.then_inc(s["scores2"], 1)

        def sums(j, n):
            pe.wait_ge(s["probs_ready"], n + 1)
            for m in range(2):
                for a in range(4):
                    last = pe.transpose(banks[:, TURN4 + m, a * P:(a + 1) * P], probs[:, 4 * m + a, :], k.ident)
                last.then_inc(s["probs_turned2"], 1)
            for m in range(KVH):
                pe.wait_ge(s["probs_t2"], 2 * n + m + 1)
                if m and not (isinstance(n, int) and n == 0):
                    pe.wait_ge(s["o_t_ready"], 2 * n)
                pe.matmul(banks[:, O + m, :], kvq[j][:, KVH + m, :],
                          probs_turn[:, REP * m:REP * (m + 1), :].rearrange("p h s -> p (h s)"),
                          start=True, stop=True).then_inc(s["o_summed"], 1)

        def join(n, more):
            pe.wait_ge(s["o_t_ready"], 2 * n + 2)
            pe.wait_ge(s["xn_t_ready"], n + 1 + min(more, 1))
            for h in range(QH):
                last = pe.matmul(banks[:, TURN, 0:D], o_turn[:, h, :], w_o[:, h, :], start=(h == 0), stop=(h == QH - 1))
            last.then_inc(s["hidden_ready"], 1)

        def route(j, n):
            pe.wait_ge(s["hn_ready"], n + 1)
            for c in range(DC):
                last = pe.transpose(banks[:, TURN, c * P:(c + 1) * P], normed[j][:, c * P:(c + 1) * P], k.ident)
            last.then_inc(s["hn_turned"], 1)
            pe.wait_ge(s["hn_t_ready"], n + 1)
            for c in range(DC):
                last = pe.matmul(banks[:, TURN, D:D + E], hn_turn[:, c, :], gate_w[:, c, :], start=(c == 0), stop=(c == DC - 1))
            last.then_inc(s["logits_ready"], 1)

        def element(j, n, i, more):
            if more:
                project(n + 1)
            sums(j, n)
            join(n, more)
            if more:
                turn_qk(n + 1)
                scores(n + 1)
            route(j, n)

        project(0)
        turn_qk(0)
        scores(0)
        element(0, 0, 0, 2)
        element(1, 1, 0, 2)
        with pe.Fori(1, TURNS - 1) as i:
            for j in range(2):
                element(j, 2 * i + j, i, 2)
        element(0, B - 2, TURNS - 1, 1)
        element(1, B - 1, TURNS - 1, 0)

    def scalar(act):
        act.wait_ge(s["attend_loads"], 16 * LOADS)

        def take_x(n):
            act.wait_ge(s["xn_turned"], n + 1)
            act.copy(xn_t[:, :, :], banks[:, TURN, 0:D].rearrange("p (c s) -> p c s", c=DC)).then_inc(s["xn_t_ready"], 1)

        def round_kv(j, n):
            act.wait_ge(s["kv_scaled"], n + 1)
            for a in range(2 * KVH):
                last = act.activation(kvq[j][:, a, :], banks[:, KV, a * HD:(a + 1) * HD], ACT.Identity,
                                      bias=k.magic[:, :], scale=kv_stat[:, INV, a:a + 1])
            last.then_inc(s["kv_rounded"], 1)

        def take_qk(n):
            for m in range(2):
                act.wait_ge(s["q_turned"], 3 * n + m + 1)
                act.copy(q_turn[:, 4 * m:4 * m + 4, :], banks[:, TURN4 + m, :].rearrange(
                    "p (a s) -> p a s", a=4)).then_inc(s["q_t_ready"], 1)
            act.wait_ge(s["q_turned"], 3 * n + 3)
            act.copy(k_turn[:, :, :], banks[:, TURN_K, 0:KVH * S].rearrange("p (a s) -> p a s", a=KVH)).then_inc(
                s["q_t_ready"], 1)

        def soften(n):
            act.wait_ge(s["peaked"], n + 1)
            for h in range(QH):
                last = act.activation(probs[:, h, :], probs[:, h, :], ACT.Exp, bias=low_peak[:, h:h + 1],
                                      accum_out=total[:, h:h + 1])
            last.then_inc(s["exped"], 1)

        def collect(n):
            for m in range(2):
                act.wait_ge(s["probs_turned2"], 2 * n + m + 1)
                act.copy(probs_turn[:, 4 * m:4 * m + 4, :], banks[:, TURN4 + m, :].rearrange(
                    "p (a s) -> p a s", a=4)).then_inc(s["probs_t2"], 1)
            for m in range(KVH):
                act.wait_ge(s["o_summed"], 2 * n + m + 1)
                act.copy(o_turn[:, REP * m:REP * (m + 1), :], banks[:, O + m, :].rearrange(
                    "p (a s) -> p a s", a=REP)).then_inc(s["o_t_ready"], 1)

        def take_logits(n):
            act.wait_ge(s["hn_turned"], n + 1)
            act.copy(hn_turn[:, :, :], banks[:, TURN, 0:D].rearrange("p (c s) -> p c s", c=DC)).then_inc(s["hn_t_ready"], 1)
            act.wait_ge(s["logits_ready"], n + 1)
            act.copy(k.logits[:, bass.ds(n, 1), :], banks[:, TURN:TURN + 1, D:D + E]).then_inc(k.logits_read, 1)

        def element(j, n, i, more):
            if more:
                take_x(n + 1)
            soften(n)
            if more:
                round_kv(1 - j, n + 1)
            collect(n)
            if more:
                take_qk(n + 1)
            take_logits(n)

        take_x(0)
        round_kv(0, 0)
        take_qk(0)
        in_pipeline(element, act)

    def gpsimd(pool):
        pool.wait_ge(s["attend_loads"], 16 * LOADS)

        def rotate(n):
            pool.wait_ge(s["roped_q"], n + 1)
            pool.tensor_tensor(q_rot[:, :, :], q_rot[:, :, :], q_sin[:, :, :], ALU.add).then_inc(s["q_rot_ready"], 1)

        def scale(a, name, n):
            pool.wait_ge(s[name + "_var"], n + 1)
            pool.tensor_tensor(rms[a][:, 2:3], rms[a][:, 1:2], k.minus_half[:, 0:1], ALU.pow).then_inc(s[name + "_scale"], 1)

        def element(j, n, i, more):
            if more:
                rotate(n + 1)
            pool.wait_ge(s["share_ready"], n + 1)
            pool.tensor_tensor(probs[:, :, :], probs[:, :, :], wide(share[:, :], S), ALU.mult).then_inc(s["probs_ready"], 1)
            if more == 2:
                scale(0, "xn", n + 2)
            scale(1, "hn", n)

        scale(0, "xn", 0)
        scale(0, "xn", 1)
        rotate(0)
        in_pipeline(element, pool)

    def vector(dve):
        st = k.steps["dve"]
        dve.wait_ge(s["attend_loads"], 16 * LOADS)
        cos, sin = k.consts[:, C_COS:C_COS + HD], k.consts[:, C_SIN:C_SIN + HD]
        mask = k.consts[:, C_MASK:C_MASK + S]

        def mean_square(a, rows, name):
            st.did(dve.tensor_tensor_reduce(squares[a][:, :], rows, rows, 1.0, 0.0, ALU.mult, ALU.add, rms[a][:, 0:1]))
            st.wait()
            dve.tensor_scalar(rms[a][:, 1:2], rms[a][:, 0:1], 1.0 / D, EPS, ALU.mult, ALU.add).then_inc(s[name + "_var"], 1)

        def x_stats(j, n, i):
            dve.wait_ge(row_loaded[j], 16 * i + 16)
            mean_square(0, row_in[j][:, :], "xn")

        def x_norm(j, n):
            dve.wait_ge(s["xn_scale"], n + 1)
            if not (isinstance(n, int) and n == 0):
                dve.wait_ge(s["xn_turned"], n)
            dve.scalar_tensor_tensor(out=xn[:, :], in0=row_in[j][:, :], scalar=rms[0][:, 2:3], in1=gains[:, 0, :],
                                     op0=ALU.mult, op1=ALU.mult).then_inc(s["xn_ready"], 1)

        def rotate_q(n):
            q = banks[:, Q:Q + 2, :].rearrange("p m (a d) -> p (m a) d", a=4)
            dve.wait_ge(s["q_ready"], n + 1)
            if not (isinstance(n, int) and n == 0):
                dve.wait_ge(s["q_turned"], 3 * n)
            dve.tensor_tensor(q_rot[:, :, :], q, each(cos, QH), ALU.mult)
            for a, b in ((0, HALF_HD), (HALF_HD, 0)):
                last = dve.tensor_tensor(q_sin[:, :, a:a + HALF_HD], q[:, :, b:b + HALF_HD],
                                         each(sin[:, a:a + HALF_HD], QH), ALU.mult)
            last.then_inc(s["roped_q"], 1)

        def kv_stats(n):
            a = kv_stat
            kv = banks[:, KV, :].rearrange("p (g d) -> p g d", g=2 * KVH)
            dve.wait_ge(s["kv_ready"], n + 1)
            dve.tensor_reduce(a[:, MAX, :], kv, AX.X, ALU.max)
            st.did(dve.tensor_reduce(a[:, MIN, :], kv, AX.X, ALU.min))
            st.wait()
            st.did(dve.tensor_tensor(a[:, TMP, :], a[:, MAX, :], a[:, MIN, :], ALU.subtract))
            st.wait()
            st.did(dve.tensor_scalar(a[:, SCALE, :], a[:, TMP, :], 1e-5, 1.0 / LEVELS, ALU.max, ALU.mult))
            st.wait()
            dve.reciprocal(a[:, INV, :], a[:, SCALE, :]).then_inc(s["kv_scaled"], 1)
            dve.wait_ge(s["kv_scaled"], n + 1)
            st.did(dve.scalar_tensor_tensor(out=a[:, TMP, :], in0=a[:, MIN, :], scalar=-1.0, in1=a[:, INV, :],
                                            op0=ALU.mult, op1=ALU.mult))
            st.wait()
            st.did(dve.tensor_scalar(a[:, BASE, :], a[:, TMP, :], MAGIC, MAGIC, ALU.add, ALU.subtract))
            st.wait()
            st.did(dve.tensor_scalar(a[:, TMP, :], a[:, BASE, :], 0.0, LEVELS, ALU.max, ALU.min))
            st.wait()
            st.did(dve.tensor_scalar(a[:, LOW, :], a[:, TMP, :], -1.0, MAGIC, ALU.mult, ALU.add))
            st.wait()
            st.did(dve.tensor_scalar(a[:, HIGH, :], a[:, LOW, :], LEVELS, None, ALU.add))
            st.wait()

        def kv_finish(j, n):
            a, x = kv_stat, kvq[j]
            dve.wait_ge(s["kv_rounded"], n + 1)
            for g in range(2 * KVH):
                last = dve.tensor_scalar(x[:, g, :], x[:, g, :], a[:, LOW, g:g + 1], a[:, HIGH, g:g + 1], ALU.max, ALU.min)
            st.did(last)
            st.wait()
            for g in range(2 * KVH):
                last = dve.tensor_scalar(x[:, g, :], x[:, g, :], MAGIC, a[:, SCALE, g:g + 1], ALU.subtract, ALU.mult)
            st.did(last)
            st.wait()
            keys = x[:, 0:KVH, :]
            dve.tensor_tensor(k_rot[:, :, :], keys, each(cos, KVH), ALU.mult)
            for lo, hi in ((0, HALF_HD), (HALF_HD, 0)):
                last = dve.tensor_tensor(k_sin[:, :, lo:lo + HALF_HD], keys[:, :, hi:hi + HALF_HD],
                                         each(sin[:, lo:lo + HALF_HD], KVH), ALU.mult)
            st.did(last)
            st.wait()
            dve.tensor_tensor(k_rot[:, :, :], k_rot[:, :, :], k_sin[:, :, :], ALU.add).then_inc(s["k_rot_ready"], 1)

        def mask_scores(n):
            dve.wait_ge(s["scores2"], n + 1)
            if not (isinstance(n, int) and n == 0):
                dve.wait_ge(s["probs_turned2"], 2 * n)
            dve.scalar_tensor_tensor(out=probs[:, :, :], in0=banks[:, Q:Q + 2, :].rearrange("p m (a d) -> p (m a) d", a=4),
                                     scalar=float(HD) ** -0.5, in1=each(mask, QH), op0=ALU.mult, op1=ALU.add).then_inc(s["masked"], 1)
            dve.wait_ge(s["masked"], n + 1)
            dve.tensor_reduce(low_peak[:, :], probs[:, :, :], AX.X, ALU.max, negate=True).then_inc(s["peaked"], 1)

        def shares(n):
            dve.wait_ge(s["exped"], n + 1)
            dve.reciprocal(share[:, :], total[:, :]).then_inc(s["share_ready"], 1)

        def h_stats(j, n, i):
            dve.wait_ge(s["hidden_ready"], n + 1)
            dve.wait_ge(res_loaded[j], 16 * i + 16)
            dve.wait_ge(attend_stored[j], 32 * i + 32)
            st.did(dve.tensor_tensor(hidden[j][:, :], banks[:, TURN, 0:D], row_res[j][:, :], ALU.add))
            st.wait()
            mean_square(1, hidden[j][:, :], "hn")

        def h_norm(j, n):
            dve.wait_ge(s["hn_scale"], n + 1)
            dve.scalar_tensor_tensor(out=normed[j][:, :], in0=hidden[j][:, :], scalar=rms[1][:, 2:3], in1=gains[:, 1, :],
                                     op0=ALU.mult, op1=ALU.mult).then_inc(s["hn_ready"], 1)

        def element(j, n, i, more):
            mask_scores(n)
            if more:
                rotate_q(n + 1)
                kv_stats(n + 1)
            shares(n)
            if more:
                kv_finish(1 - j, n + 1)
            if more == 2:
                x_stats(j, n + 2, i + 1)
            h_stats(j, n, i)
            if more == 2:
                x_norm(j, n + 2)
            h_norm(j, n)

        x_stats(0, 0, 0)
        x_norm(0, 0)
        x_stats(1, 1, 0)
        x_norm(1, 1)
        rotate_q(0)
        kv_stats(0)
        kv_finish(0, 0)
        st.done(1, 13)
        PER = 2 * (11 + 3)
        with dve.Fori(0, TURNS - 1) as i:
            st.turn(i, PER)
            for j in range(2):
                element(j, 2 * i + j, i, 2)
        st.done(TURNS - 1, PER)
        element(0, B - 2, TURNS - 1, 1)
        element(1, B - 1, TURNS - 1, 0)
        st.done(1, PER - 13)

    return sync, tensor, vector, scalar, gpsimd


def route_stage(k):
    nc, t, banks = k.nc, k.t, k.banks
    with ExitStack() as own:
        rows = k.buffer(own, "route_rows", [B, D])
        less = k.buffer(own, "less", [B, E])
        other = k.buffer(own, "other", [B, E])
        key = k.buffer(own, "key", [B, E])
        chosen = [k.buffer(own, f"chosen{m}", [B, E]) for m in range(2)]
        both = k.buffer(own, "both", [B, E])
        peak = k.buffer(own, "route_peak", [2, B])
        index = k.buffer(own, "index", [2, B])
        second = k.buffer(own, "second", [B])
        norm = k.buffer(own, "route_norm", [2, B])
        counts = k.buffer(own, "counts", [E, B])
        upto = k.buffer(own, "upto", [E, B])
        before = k.buffer(own, "before", [E, B])
        per_expert = k.buffer(own, "per_expert", [6, E])
        place = k.buffer(own, "place", [B, E])
        hit = [k.buffer(own, f"hit{m}", [B, E]) for m in range(2)]
        sums = k.buffer(own, "place_sums", [2, B])
        passed = k.buffer(own, "passed", [BLOCKS, E])
        block_sum = k.buffer(own, "block_sum", [2, BLOCKS])
    route_loads = k.semaphore("route_loads")
    second_ready = k.semaphore("second_ready")
    second_exped = k.semaphore("second_exped")
    chosen_ready = k.semaphore("chosen_ready")
    counted = k.semaphore("counted")
    places_ready = k.semaphore("places_ready")
    k.blocks_ready = k.semaphore("blocks_ready")
    scattered = k.semaphore("scattered")
    NEED, BLOCKS_E, UPTO_E, BEGIN, TOTAL, SHIFT = range(6)
    RANK, ALL = banks[:, 0, 0:B * E], banks[:, 0, B * E:2 * B * E]

    def sync(sp):
        sp.dma_start(rows[:, :, :], k.normed_d.rearrange("(b p) n -> p b n", p=P)).then_inc(route_loads, 16)
        sp.wait_ge(scattered, 16 * 2 * B)

    def tensor(pe):
        pe.wait_ge(chosen_ready, 1)
        flat = both[:, :, :].rearrange("p b e -> p (b e)")
        pe.matmul(RANK, k.consts[:, C_BEFORE:C_BEFORE + P], flat, start=True, stop=True)
        pe.matmul(ALL, k.consts[:, C_ONES:C_ONES + P], flat, start=True, stop=True).then_inc(counted, 1)

    def scalar(act):
        act.wait_ge(second_ready, 1)
        act.activation(second[:, :], peak[:, 1, :], ACT.Exp).then_inc(second_exped, 1)

    def gpsimd(pool):
        pool.wait_ge(route_loads, 16)
        pool.wait_ge(k.s_zeroed, 16)
        pool.wait_ge(places_ready, 2)
        for b in range(B):
            for m in range(2):
                pool.indirect_dma_start(
                    out=k.sorted_d, out_offset=bass.IndirectOffsetOnAxis(ap=k.places[:, m, b:b + 1], axis=0),
                    in_=rows[:, b, :], in_offset=None).then_inc(scattered, 16)

    def vector(dve):
        st = k.steps["dve"]
        iota = each(k.consts[:, C_IOTA:C_IOTA + E], B)

        def step(ins):
            st.did(ins)
            st.wait()

        def choose(m, logits):
            step(dve.tensor_reduce(peak[:, m, :], logits, AX.X, ALU.max))
            step(dve.tensor_tensor(key[:, :, :], logits, wide(peak[:, m, :], E), ALU.is_lt))
            step(dve.scalar_tensor_tensor(out=key[:, :, :], in0=key[:, :, :], scalar=float(E), in1=iota,
                                          op0=ALU.mult, op1=ALU.add))
            step(dve.tensor_reduce(index[:, m, :], key[:, :, :], AX.X, ALU.min))
            step(dve.tensor_tensor(chosen[m][:, :, :], iota, wide(index[:, m, :], E), ALU.is_equal))

        dve.wait_ge(route_loads, 16)
        dve.wait_ge(k.logits_read, B)
        step(dve.tensor_reduce(norm[:, 0, :], k.logits[:, :, :], AX.X, ALU.max))
        step(dve.tensor_tensor(less[:, :, :], k.logits[:, :, :], wide(norm[:, 0, :], E), ALU.subtract))
        choose(0, less[:, :, :])
        step(dve.scalar_tensor_tensor(out=other[:, :, :], in0=chosen[0][:, :, :], scalar=LOWEST, in1=less[:, :, :],
                                      op0=ALU.mult, op1=ALU.add))
        choose(1, other[:, :, :])
        dve.tensor_tensor(both[:, :, :], chosen[0][:, :, :], chosen[1][:, :, :], ALU.add).then_inc(chosen_ready, 1)
        dve.sem_inc(second_ready, 1)

        dve.wait_ge(second_exped, 1)
        step(dve.tensor_scalar(norm[:, 1, :], second[:, :], 1.0, None, ALU.add))
        step(dve.reciprocal(k.shares[:, 0, :], norm[:, 1, :]))
        step(dve.tensor_tensor(k.shares[:, 1, :], k.shares[:, 0, :], second[:, :], ALU.mult))

        dve.wait_ge(counted, 1)
        step(dve.tensor_copy(counts[:, :, :], ALL.rearrange("p (b e) -> p e b", b=B)))
        ones = k.consts[:, C_ONES:C_ONES + P]
        step(dve.tensor_tensor_scan(upto[:, :, :].rearrange("p e b -> p (e b)"), ones,
                                    counts[:, :, :].rearrange("p e b -> p (e b)"), 0.0, ALU.mult, ALU.add))
        step(dve.tensor_tensor(before[:, :, :], upto[:, :, :], counts[:, :, :], ALU.subtract))
        a = per_expert
        step(dve.tensor_tensor(a[:, TOTAL, :], upto[:, :, B - 1], before[:, :, 0], ALU.subtract))
        step(dve.tensor_scalar(a[:, NEED, :], a[:, TOTAL, :], 1.0 / ROWS, 0.5 - 0.5 / ROWS, ALU.mult, ALU.add))
        step(dve.tensor_scalar(a[:, BLOCKS_E, :], a[:, NEED, :], MAGIC, MAGIC, ALU.add, ALU.subtract))
        step(dve.tensor_tensor_scan(a[:, UPTO_E, :], ones[:, 0:E], a[:, BLOCKS_E, :], 0.0, ALU.mult, ALU.add))
        step(dve.tensor_tensor(a[:, BEGIN, :], a[:, UPTO_E, :], a[:, BLOCKS_E, :], ALU.subtract))
        step(dve.scalar_tensor_tensor(out=a[:, SHIFT, :], in0=a[:, BEGIN, :], scalar=float(ROWS), in1=before[:, :, 0],
                                      op0=ALU.mult, op1=ALU.subtract))
        step(dve.tensor_tensor(place[:, :, :], RANK.rearrange("p (b e) -> p b e", b=B), each(a[:, SHIFT, :], B), ALU.add))
        step(dve.tensor_tensor(place[:, :, :], place[:, :, :], before[:, :, :].rearrange("p e b -> p b e"), ALU.add))
        for m in range(2):
            step(dve.tensor_tensor(hit[m][:, :, :], place[:, :, :], chosen[m][:, :, :], ALU.mult))
            step(dve.tensor_reduce(sums[:, m, :], hit[m][:, :, :], AX.X, ALU.add))
            dve.tensor_copy(k.places[:, m, :], sums[:, m, :]).then_inc(places_ready, 1)

        step(dve.tensor_tensor(passed[:, :, :], wide(k.consts[:, C_BLOCK:C_BLOCK + BLOCKS], E), each(a[:, UPTO_E, :], BLOCKS),
                               ALU.is_ge))
        step(dve.tensor_reduce(block_sum[:, 0, :], passed[:, :, :], AX.X, ALU.add))
        step(dve.tensor_scalar(block_sum[:, 1, :], block_sum[:, 0, :], float(E - 1), None, ALU.min))
        dve.tensor_copy(k.block_expert[:, :], block_sum[:, 1, :]).then_inc(k.blocks_ready, 1)
        st.done(1, st.at)

    return sync, tensor, vector, scalar, gpsimd


def experts_stage(k):
    nc, t, banks = k.nc, k.t, k.banks
    HALVES = ROWS // P
    with ExitStack() as own:
        weights = [k.buffer(own, f"expert_w{j}", [3 * TILES, P]) for j in range(2)]
        rows = [k.buffer(own, f"expert_rows{j}", [HALVES, D]) for j in range(2)]
        rows_t = [k.buffer(own, f"expert_rows_t{j}", [DC, ROWS]) for j in range(2)]
        silu = [k.buffer(own, f"silu{a}", [ROWS]) for a in range(2)]
        up = [k.buffer(own, f"up{j}", [FC, ROWS]) for j in range(2)]
        y = [k.buffer(own, f"expert_y{j}", [HALVES, D]) for j in range(2)]
    weights_in = [k.semaphore(f"weights_in{j}") for j in range(2)]
    block_in = [k.semaphore(f"block_in{j}") for j in range(2)]
    expert_stored = [k.semaphore(f"expert_stored{j}") for j in range(2)]
    block_turned = k.semaphore("block_turned")
    rows_t_ready = k.semaphore("rows_t_ready")
    up_summed = k.semaphore("up_summed")
    silu_ready = k.semaphore("silu_ready")
    up_ready = k.semaphore("up_ready")
    y_summed = k.semaphore("y_summed")
    y_ready = k.semaphore("y_ready")
    UP, TURN, Y = 0, 2, 4
    TURNS = (BLOCKS - 1) // 2
    assert BLOCKS % 2

    def in_pipeline(emit, eng):
        with eng.Fori(0, TURNS - 1) as i:
            for j in range(2):
                emit(j, 2 * i + j, i, 2)
        emit(0, BLOCKS - 3, TURNS - 1, 2)
        emit(1, BLOCKS - 2, TURNS - 1, 1)
        emit(0, BLOCKS - 1, TURNS, 0)

    def sync(sp):
        def load(j, n):
            expert = sp.value_load(k.block_expert[0:1, bass.ds(n, 1)], min_val=0, max_val=E - 1)
            sp.dma_start(weights[j][:, :, :].rearrange("p (o a) b -> p o (a b)", o=3),
                         k.weights_d[bass.ds(3 * expert + 3, 3)].rearrange("o p n -> p o n")).then_inc(weights_in[j], 16)
            sp.dma_start(rows[j][:, :, :], k.sorted_d[bass.ds(n * ROWS, ROWS), :].rearrange(
                "(a p) d -> p a d", p=P)).then_inc(block_in[j], 16)

        def element(j, n, i, more):
            if more == 2:
                sp.wait_ge(y_summed, n + 1)
                load(j, n + 2)
            sp.wait_ge(y_ready, n + 3)
            sp.dma_start(k.expert_d[bass.ds(n * ROWS, ROWS), :].rearrange("(a p) d -> p a d", p=P),
                         y[j][:, :, :]).then_inc(expert_stored[j], 16)

        for j in range(2):
            sp.sem_inc(expert_stored[j], 16)
        sp.wait_ge(k.blocks_ready, 1)
        load(0, 0)
        load(1, 1)
        in_pipeline(element, sp)
        sp.wait_ge(expert_stored[0], 16 * (TURNS + 2))
        sp.wait_ge(expert_stored[1], 16 * (TURNS + 1))

    def tensor(pe):
        def turn(j, n, i):
            pe.wait_ge(block_in[j], 16 * i + 16)
            for c in range(DC):
                for a in range(HALVES):
                    last = pe.transpose(banks[:, TURN + j, (c * HALVES + a) * P:(c * HALVES + a + 1) * P],
                                        rows[j][:, a, c * P:(c + 1) * P], k.ident)
            last.then_inc(block_turned, 1)

        def element(j, n, i, more):
            w = weights[j]
            pe.wait_ge(weights_in[j], 16 * i + 16)
            pe.wait_ge(rows_t_ready, n + 1)
            for f in range(FC):
                g = FC * n + f
                pe.wait_ge(up_ready, g + 1)
                for m in range(2):
                    for c in range(DC):
                        last = pe.matmul(banks[:, UP + (FC * j + f) % 2, m * ROWS:(m + 1) * ROWS],
                                         w[:, m * TILES + f * DC + c, :], rows_t[j][:, c, :],
                                         start=(c == 0), stop=(c == DC - 1))
                last.then_inc(up_summed, 1)
            if more:
                turn(1 - j, n + 1, i + j)
            pe.wait_ge(y_ready, n + 1)
            for a in range(HALVES):
                for f in range(FC):
                    if a == 0:
                        pe.wait_ge(up_ready, FC * n + f + 3)
                    last = pe.matmul(banks[:, Y + j, a * D:(a + 1) * D], up[j][:, f, a * P:(a + 1) * P],
                                     w[:, 2 * TILES + DC * f:2 * TILES + DC * (f + 1), :].rearrange("p c d -> p (c d)"),
                                     start=(f == 0), stop=(f == FC - 1))
            last.then_inc(y_summed, 1)

        turn(0, 0, 0)
        in_pipeline(element, pe)

    def scalar(act):
        def take_rows(j, n):
            act.wait_ge(block_turned, n + 1)
            act.copy(rows_t[j][:, :, :].rearrange("p c s -> p (c s)"), banks[:, TURN + j, :]).then_inc(rows_t_ready, 1)

        def element(j, n, i, more):
            for f in range(FC):
                act.wait_ge(up_summed, FC * n + f + 1)
                act.activation(silu[(FC * j + f) % 2][:, :], banks[:, UP + (FC * j + f) % 2, 0:ROWS],
                               ACT.Silu).then_inc(silu_ready, 1)
            if more:
                take_rows(1 - j, n + 1)
            act.wait_ge(y_summed, n + 1)
            act.wait_ge(expert_stored[j], 16 * i + 16)
            act.copy(y[j][:, :, :].rearrange("p a d -> p (a d)"), banks[:, Y + j, :]).then_inc(y_ready, 1)

        act.sem_inc(y_ready, 2)
        take_rows(0, 0)
        in_pipeline(element, act)

    def vector(dve):
        def element(j, n, i, more):
            for f in range(FC):
                dve.wait_ge(silu_ready, FC * n + f + 1)
                dve.tensor_tensor(up[j][:, f, :], silu[(FC * j + f) % 2][:, :],
                                  banks[:, UP + (FC * j + f) % 2, ROWS:2 * ROWS], ALU.mult).then_inc(up_ready, 1)

        dve.sem_inc(up_ready, 2)
        in_pipeline(element, dve)

    def gpsimd(pool):
        pass

    return sync, tensor, vector, scalar, gpsimd


def finish_stage(k):
    nc, t = k.nc, k.t
    GROUP = 4
    N_GROUPS = B // GROUP
    with ExitStack() as own:
        taken = [k.buffer(own, f"taken{m}", [B, D]) for m in range(2)]
        h = k.buffer(own, "finish_h", [B, D])
        x = k.buffer(own, "finish_x", [B, D])
        decoded = k.buffer(own, "decoded_rows", [B, D])
        stats = k.buffer(own, "finish_stats", [GROUP, 6])
        mean = k.buffer(own, "finish_mean", [GROUP, 2])
        eps = k.buffer(own, "finish_eps", [GROUP])
        scale = k.buffer(own, "finish_scale", [GROUP])
    finish_loads = k.semaphore("finish_loads")
    gather_begin = k.semaphore("gather_begin")
    gathered = [k.semaphore(f"gathered{j}") for j in range(2)]
    finish_var = k.semaphore("finish_var")
    finish_scale = k.semaphore("finish_scale")
    finish_normed = k.semaphore("finish_normed")
    finish_stored = k.semaphore("finish_stored")

    def sync(sp):
        sp.sem_inc(gather_begin, 1)
        sp.dma_start(h[:, :, :], k.hidden_d.rearrange("(b p) n -> p b n", p=P)).then_inc(finish_loads, 16)
        sp.dma_start(x[:, :, :], k.crossed_d.rearrange("(b p) n -> p b n", p=P)).then_inc(finish_loads, 16)
        with sp.Fori(0, N_GROUPS) as g:
            sp.wait_ge(finish_normed, g + 1)
            sp.dma_start(k.out[bass.ds(g * GROUP * P, GROUP * P), :].rearrange("(b p) n -> p b n", p=P),
                         decoded[:, bass.ds(GROUP * g, GROUP), :]).then_inc(finish_stored, 16)
        sp.wait_ge(finish_stored, 16 * N_GROUPS)

    def gpsimd(pool):
        pool.wait_ge(gather_begin, 1)

        def gather(g):
            for b in range(GROUP * g, GROUP * (g + 1)):
                for m in range(2):
                    pool.indirect_dma_start(
                        out=taken[m][:, b, :], out_offset=None, in_=k.expert_d,
                        in_offset=bass.IndirectOffsetOnAxis(ap=k.places[:, m, b:b + 1], axis=0)).then_inc(gathered[g % 2], 16)

        gather(0)
        for g in range(N_GROUPS):
            if g + 1 < N_GROUPS:
                if g:
                    pool.wait_ge(gathered[(g + 1) % 2], 32 * GROUP * ((g + 1) // 2))
                gather(g + 1)
            pool.wait_ge(finish_var, g + 1)
            pool.tensor_tensor(scale[:, :], eps[:, :], k.minus_half[:, 0:GROUP], ALU.pow).then_inc(finish_scale, 1)

    def vector(dve):
        st = k.steps["dve"]
        dve.wait_ge(finish_loads, 32)
        for b in range(0, B, GROUP):
            last = dve.tensor_tensor(h[:, b:b + GROUP, :], h[:, b:b + GROUP, :], x[:, b:b + GROUP, :], ALU.add)
        st.did(last)
        st.wait()
        for g in range(N_GROUPS):
            tiles = range(GROUP * g, GROUP * (g + 1))
            dve.wait_ge(gathered[g % 2], 32 * GROUP * (g // 2 + 1))
            for m in range(2):
                for b in tiles:
                    last = dve.scalar_tensor_tensor(out=h[:, b, :], in0=taken[m][:, b, :], scalar=k.shares[:, m, b:b + 1],
                                                    in1=h[:, b, :], op0=ALU.mult, op1=ALU.add)
                st.did(last)
                st.wait()
            for a, b in enumerate(tiles):
                last = dve.bn_stats(stats[:, a, :], h[:, b, :])
            st.did(last)
            st.wait()
            for a in range(GROUP):
                last = dve.bn_aggr(mean[:, a, :], stats[:, a, :])
            st.did(last)
            st.wait()
            dve.tensor_scalar(eps[:, :], mean[:, :, 1], EPS, None, ALU.add).then_inc(finish_var, 1)
            dve.wait_ge(finish_scale, g + 1)
            for a, b in enumerate(tiles):
                last = dve.tensor_scalar(decoded[:, b, :], h[:, b, :], mean[:, a, 0:1], scale[:, a:a + 1],
                                         ALU.subtract, ALU.mult)
            last.then_inc(finish_normed, 1)
        st.done(1, st.at)

    def tensor(pe):
        pass

    def scalar(act):
        pass

    return sync, tensor, vector, scalar, gpsimd


STAGES = (prep_stage, mix_stage, cross_stage, attend_stage, route_stage, experts_stage, finish_stage)


def decoder_layer(nc, t, out):
    with ExitStack() as top:
        k = Shared(nc, t, out, top)
        stages = [stage(k) for stage in STAGES]
        s_dve = k.semaphore("dve_steps")
        block = top.enter_context(nc.Block())

        @block.sync
        def _(sp):
            sp.dma_start(k.consts[:, :], t["constants"]).then_inc(k.s_consts, 16)
            sp.wait_ge(k.s_fill, 3)
            sp.dma_start(k.sorted_d.rearrange("(a p) d -> p a d", p=P), each(k.zeros[:, :], SORTED // P)).then_inc(
                k.s_zeroed, 16)
            for sync, *_ in stages:
                sync(sp)

        @block.tensor
        def _(pe):
            pe.wait_ge(k.s_consts, 16)
            for _, tensor, *_ in stages:
                tensor(pe)

        @block.vector
        def _(dve):
            k.steps["dve"] = Steps(dve, s_dve)
            dve.memset(k.magic[:, :], MAGIC).then_inc(k.s_fill, 1)
            dve.memset(k.minus_half[:, :], -0.5).then_inc(k.s_fill, 1)
            dve.memset(k.zeros[:, :], 0.0).then_inc(k.s_fill, 1)
            dve.wait_ge(k.s_consts, 16)
            for _, _, vector, *_ in stages:
                vector(dve)

        @block.scalar
        def _(act):
            act.wait_ge(k.s_consts, 16)
            act.wait_ge(k.s_fill, 3)
            for _, _, _, scalar, _ in stages:
                scalar(act)

        @block.gpsimd
        def _(pool):
            pool.wait_ge(k.s_consts, 16)
            pool.wait_ge(k.s_fill, 3)
            for _, _, _, _, gpsimd in stages:
                gpsimd(pool)


def shape_constants():
    c = np.zeros((P, C_END), np.float32)
    i = np.arange(P)
    c[:, C_ID:C_ID + P] = np.eye(P)
    inv = np.float32(1.0) / np.float32(1000000.0) ** (np.arange(0, HD, 2, dtype=np.float32) / np.float32(HD))
    angle = (i.astype(np.float32)[:, None] * inv[None, :]).astype(np.float32)
    angle = np.concatenate([angle, angle], axis=1)
    c[:, C_COS:C_COS + HD] = np.cos(angle)
    c[:, C_SIN:C_SIN + HD] = np.sin(angle) * np.where(np.arange(HD) < HD // 2, -1, 1)
    c[:, C_MASK:C_MASK + S] = np.where(i[:, None] >= i[None, :], 0.0, MASKED)
    c[:, C_BEFORE:C_BEFORE + P] = i[:, None] < i[None, :]
    c[:, C_ONES:C_ONES + P] = 1.0
    c[:, C_HEAD:C_HEAD + HALF] = i[:, None] // XK == np.arange(HALF)[None, :]
    c[:, C_IOTA:C_IOTA + E] = np.arange(E)
    c[:, C_BLOCK:C_BLOCK + BLOCKS] = np.arange(BLOCKS)
    return c


def laid_out(x, ctx_1024, L0_attn_rkv_w, L0_attn_out_w, L0_attn_time_decay, L0_attn_time_first,
             L0_attn_time_decay_rev, L0_attn_time_first_rev, L0_xattn_Wq, L0_xattn_bq, L0_xattn_Wk, L0_xattn_bk,
             L0_xattn_Wv, L0_xattn_bv, L0_xattn_Wo, L0_xattn_bo, L0_ffn_w_q, L0_ffn_w_k, L0_ffn_w_v, L0_ffn_w_o,
             L0_ffn_g1, L0_ffn_g2, L0_ffn_w_gate, L0_ffn_w1, L0_ffn_w3, L0_ffn_w2):
    def columns(*vectors):
        return np.concatenate([v.reshape(-1, P) for v in vectors]).T

    qkv = np.concatenate([L0_ffn_w_q, L0_ffn_w_k, L0_ffn_w_v])
    tiles = [qkv.reshape(-1, P, DC, P).transpose(1, 2, 0, 3).reshape(P, -1, P),
             L0_ffn_w_o.reshape(DC, P, QH, P).transpose(1, 2, 0, 3).reshape(P, -1, P)]
    tiles.append(np.zeros((P, 3 * TILES - sum(a.shape[1] for a in tiles), P), np.float32))
    jobs = [np.concatenate(tiles, axis=1).reshape(P, 3, TILES * P).transpose(1, 0, 2)]
    for e in range(E):
        for w in (L0_ffn_w1, L0_ffn_w3):
            jobs.append(w[e].reshape(FC, P, DC * P).transpose(1, 0, 2).reshape(1, P, TILES * P))
        jobs.append(L0_ffn_w2[e].reshape(DC, P, FC, P).transpose(1, 2, 0, 3).reshape(1, P, TILES * P))
    arrays = {
        "constants": shape_constants(),
        "x": x.reshape(TOK, D),
        "x_fwd_t": x.reshape(TOK, D).T,
        "x_bwd_t": x[:, ::-1].reshape(TOK, D).T,
        "ctx_t": ctx_1024.reshape(TOK, D).T,
        "rkv_t": L0_attn_rkv_w.T,
        "out_t": L0_attn_out_w.T,
        "decay": columns(L0_attn_time_decay, L0_attn_time_decay_rev),
        "first": columns(L0_attn_time_first, L0_attn_time_first_rev),
        "wq": L0_xattn_Wq, "wk": L0_xattn_Wk, "wv": L0_xattn_Wv, "wo": L0_xattn_Wo,
        "bqk": columns(L0_xattn_bq, L0_xattn_bk),
        "rows": np.stack([L0_xattn_bv, L0_xattn_bo, L0_ffn_g1, L0_ffn_g2]).reshape(4, D),
        "gate_t": L0_ffn_w_gate.T,
        "weight_jobs": np.concatenate(jobs),
    }
    return {f"in_{n}": np.ascontiguousarray(a) for n, a in arrays.items()}


def build(nc, arrays):
    t = {n.removeprefix("in_"): nc.dram_tensor(n, a.shape, F32, kind="ExternalInput").ap() for n, a in arrays.items()}
    out = nc.dram_tensor("decoded", (TOK, D), F32, kind="ExternalOutput").ap()
    decoder_layer(nc, t, out)


def kernel(**inputs):
    import concourse.bacc as bacc
    from concourse.bass_utils import run_bass_kernel_spmd

    arrays = laid_out(**{n: np.asarray(a) for n, a in inputs.items()})
    nc = bacc.Bacc("TRN2", target_bir_lowering=False, num_devices=1)
    build(nc, arrays)
    result = run_bass_kernel_spmd(nc, [arrays], core_ids=[0])
    return result.results[0]["decoded"].reshape(B, S, D)
```

```python
from contextlib import ExitStack

import numpy as np

import concourse.bass as bass
from concourse import mybir

F32 = mybir.dt.float32
I32 = mybir.dt.int32
ALU = mybir.AluOpType
ACT = mybir.ActivationFunctionType
AX = mybir.AxisListType

P = 128
B, S, D = 16, 128, 256
TOK = B * S
DC = D // P
GROUPS, GB = 4, 4
GT = GB * S
UNITS = 4
XH, XK = 16, 16
HALF = 8
QH, KVH, HD = 8, 2, 128
REP = QH // KVH
E, FFN = 8, 896
FC = FFN // P
LEVELS = 15.0
TILES = 14
JOBS = 27
ROWS = 256
BLOCKS = (2 * TOK + E * (ROWS - 1)) // ROWS
SORTED = BLOCKS * ROWS
MAGIC = 12582912.0
LOWEST = -1e38
MASKED = -1e30
EPS = 1e-5

C_ID, C_COS, C_SIN, C_MASK, C_BEFORE, C_ONES, C_HEAD = 0, 128, 256, 384, 512, 640, 768
C_IOTA, C_BLOCK, C_END = 776, 784, 784 + BLOCKS


class Steps:

    def __init__(self, eng, sem):
        self.eng, self.sem, self.start, self.base, self.at = eng, sem, 0, 0, 0

    def did(self, ins):
        ins.then_inc(self.sem, 1)
        self.at += 1

    def wait(self):
        self.eng.wait_ge(self.sem, self.base + self.at)

    def turn(self, i, per):
        self.base, self.at = self.start + i * per, 0

    def done(self, turns, per):
        assert self.at == per, f"{self.at} steps a turn, not {per}"
        self.start += turns * per
        self.base, self.at = self.start, 0


def wide(ap, n):
    p, a = ap.shape
    return ap.rearrange("p (a o) -> p a o", o=1).to_broadcast([p, a, n])


def each(ap, n):
    p, w = ap.shape
    return ap.rearrange("p (o w) -> p o w", o=1).to_broadcast([p, n, w])



class Shared:

    def __init__(self, nc, t, out, top):
        self.nc, self.t, self.out, self.top = nc, t, out, top
        self.steps = {}

        def dram(name, shape):
            return nc.dram_tensor(name, shape, F32, kind="Internal").ap()

        self.weights_d = dram("weights_d", (JOBS, P, TILES * P))
        self.mixed_d = dram("mixed_d", (TOK, D))
        self.crossed_d = dram("crossed_d", (TOK, D))
        self.hidden_d = dram("hidden_d", (TOK, D))
        self.normed_d = dram("normed_d", (TOK, D))
        self.sorted_d = dram("sorted_d", (SORTED, D))
        self.expert_d = dram("expert_d", (SORTED, D))
        self.banks = top.enter_context(nc.psum_tensor("banks", [P, 8, 512], F32))
        self.consts = self.buffer(top, "consts", [C_END])
        self.ident = self.consts[:, C_ID:C_ID + P]
        self.magic = self.buffer(top, "magic", [1])
        self.minus_half = self.buffer(top, "minus_half", [4])
        self.logits = self.buffer(top, "logits", [B, E])
        self.zeros = self.buffer(top, "zeros", [D])
        self.places = self.buffer(top, "places", [2, B], I32)
        self.shares = self.buffer(top, "shares", [2, B])
        self.block_expert = self.buffer(top, "block_expert", [BLOCKS], I32)
        self.s_consts = self.semaphore("s_consts")
        self.s_fill = self.semaphore("s_fill")
        self.s_zeroed = self.semaphore("s_zeroed")
        self.s_held = self.semaphore("s_held")

    def semaphore(self, name):
        return self.top.enter_context(self.nc.semaphore(name))

    def buffer(self, stack, name, shape, dt=F32):
        return stack.enter_context(self.nc.sbuf_tensor(name, [P] + shape, dt))


def prep_stage(k):
    nc, t, banks = k.nc, k.t, k.banks
    with ExitStack() as own:
        raw = [k.buffer(own, f"raw{j}", [TILES, P]) for j in range(3)]
        level = [k.buffer(own, f"level{j}", [TILES, P]) for j in range(3)]
        turned = [k.buffer(own, f"turned{j}", [TILES, P]) for j in range(3)]
        stat = [k.buffer(own, f"stat{j}", [8, TILES]) for j in range(3)]
    raw_in = [k.semaphore(f"raw_in{j}") for j in range(3)]
    stored = [k.semaphore(f"stored{j}") for j in range(3)]
    scale_ready = k.semaphore("scale_ready")
    rounded = k.semaphore("rounded")
    clipped = k.semaphore("clipped")
    pool_clipped = k.semaphore("pool_clipped")
    tiles_turned = k.semaphore("tiles_turned")
    bank_read = k.semaphore("bank_read")
    dequantised = k.semaphore("dequantised")
    TURNS, BANKS_JOB = JOBS // 3, 4
    DVE_TILES = 12
    MAX, MIN, SCALE, INV, BASE, LOW, HIGH, TMP = range(8)

    def in_pipeline(emit, eng, st=None, per=None):
        with eng.Fori(0, TURNS - 1) as i:
            if st:
                st.turn(i, per)
            for j in range(3):
                emit(j, 3 * i + j, i, 3)
        if st:
            st.done(TURNS - 1, per)
        for j in range(3):
            emit(j, JOBS - 3 + j, TURNS - 1, 2 - j)

    def sync(sp):
        def load(j, n):
            sp.dma_start(raw[j][:, :, :], t["weight_jobs"][bass.ds(n, 1)].rearrange(
                "o p (a b) -> (o p) a b", a=TILES)).then_inc(raw_in[j], 16)

        def store(j, n):
            sp.wait_ge(bank_read, (n + 2) * BANKS_JOB)
            sp.dma_start(k.weights_d[bass.ds(n, 1)].rearrange("o p (a b) -> (o p) a b", a=TILES),
                         turned[j][:, :, :]).then_inc(stored[j], 16)

        def element(j, n, more=True, begin=False):
            if more:
                sp.wait_ge(rounded, n + 1)
                load(j, n + 3)
            if not begin:
                store((j + 1) % 3, n - 2)

        for j in range(3):
            load(j, j)
            sp.sem_inc(stored[j], 16)
        for j in range(3):
            element(j, j, begin=(j < 2))
        with sp.Fori(1, TURNS - 1) as i:
            for j in range(3):
                element(j, 3 * i + j)
        for j in range(3):
            element(j, JOBS - 3 + j, more=False)
        for j in (1, 2):
            store(j, JOBS - 3 + j)
        for j in range(3):
            sp.wait_ge(stored[j], 16 * (TURNS + 1))

    def vector(dve):
        st = k.steps["dve"]

        def steps_of(j, n, i):
            a = stat[j]
            dve.wait_ge(raw_in[j], 16 * i + 16)
            dve.wait_ge(dequantised, n + 1)
            dve.tensor_reduce(a[:, MAX, :], raw[j][:, :, :], AX.X, ALU.max)
            st.did(dve.tensor_reduce(a[:, MIN, :], raw[j][:, :, :], AX.X, ALU.min))
            st.wait()
            st.did(dve.tensor_tensor(a[:, TMP, :], a[:, MAX, :], a[:, MIN, :], ALU.subtract))
            st.wait()
            st.did(dve.tensor_scalar(a[:, SCALE, :], a[:, TMP, :], 1e-5, 1.0 / LEVELS, ALU.max, ALU.mult))
            st.wait()
            st.did(dve.reciprocal(a[:, INV, :], a[:, SCALE, :]))
            st.wait()
            st.did(dve.scalar_tensor_tensor(out=a[:, TMP, :], in0=a[:, MIN, :], scalar=-1.0,
                                            in1=a[:, INV, :], op0=ALU.mult, op1=ALU.mult))
            st.wait()
            st.did(dve.tensor_scalar(a[:, BASE, :], a[:, TMP, :], MAGIC, MAGIC, ALU.add, ALU.subtract))
            st.wait()
            st.did(dve.tensor_scalar(a[:, TMP, :], a[:, BASE, :], 0.0, LEVELS, ALU.max, ALU.min))
            st.wait()
            st.did(dve.tensor_scalar(a[:, LOW, :], a[:, TMP, :], -1.0, MAGIC, ALU.mult, ALU.add))
            st.wait()
            dve.tensor_scalar(a[:, HIGH, :], a[:, LOW, :], LEVELS, None, ALU.add).then_inc(scale_ready, 1)

        def element(j, n, i, more):
            if more:
                steps_of((j + 1) % 3, n + 1, i + (j + 1) // 3)
            dve.wait_ge(rounded, n + 1)
            for a in range(DVE_TILES):
                last = dve.tensor_scalar(level[j][:, a, :], level[j][:, a, :], stat[j][:, LOW, a:a + 1],
                                         stat[j][:, HIGH, a:a + 1], ALU.max, ALU.min)
            last.then_inc(clipped, 1)

        steps_of(0, 0, 0)
        st.done(1, 8)
        in_pipeline(element, dve, st, 24)
        st.done(1, 16)

    def scalar(act):
        def round_levels(j, n):
            act.wait_ge(scale_ready, n + 1)
            for a in range(TILES):
                last = act.activation(level[j][:, a, :], raw[j][:, a, :], ACT.Identity, bias=k.magic[:, :],
                                      scale=stat[j][:, INV, a:a + 1])
            last.then_inc(rounded, 1)

        def take_tiles(j, n, i):
            act.wait_ge(stored[j], 16 * i + 16)
            for b in range(BANKS_JOB):
                tiles = min(4, TILES - 4 * b)
                act.wait_ge(tiles_turned, n * BANKS_JOB + b + 1)
                act.copy(turned[j][:, 4 * b:4 * b + tiles, :],
                         banks[:, 4 * (j % 2) + b, 0:tiles * P].rearrange("p (a b) -> p a b", a=tiles)).then_inc(bank_read, 1)

        def element(j, n, i, more):
            if more > 1:
                round_levels((j + 2) % 3, n + 2)
            take_tiles(j, n, i)

        round_levels(0, 0)
        round_levels(1, 1)
        in_pipeline(element, act)

    def gpsimd(pool):
        def element(j, n, i, more):
            pool.wait_ge(rounded, n + 1)
            pool.sem_inc(k.s_held, 1)
            for a in range(DVE_TILES, TILES):
                last = pool.tensor_scalar(level[j][:, a, :], level[j][:, a, :], stat[j][:, LOW, a:a + 1],
                                          stat[j][:, HIGH, a:a + 1], ALU.max, ALU.min)
            last.then_inc(pool_clipped, 1)
            pool.wait_ge(clipped, n + 1)
            pool.wait_ge(pool_clipped, n + 1)
            pool.sem_inc(k.s_held, 1)
            for a in range(TILES):
                last = pool.tensor_scalar(level[j][:, a, :], level[j][:, a, :], -MAGIC,
                                          stat[j][:, SCALE, a:a + 1], ALU.add, ALU.mult)
            last.then_inc(dequantised, 1)

        pool.sem_inc(dequantised, 3)
        in_pipeline(element, pool)

    def tensor(pe):
        def element(j, n, i, more):
            pe.wait_ge(dequantised, n + 4)
            for b in range(BANKS_JOB):
                if j == 0:
                    pe.wait_ge(bank_read, n * BANKS_JOB + b + 1)
                if j == 2:
                    pe.wait_ge(bank_read, (n - 1) * BANKS_JOB + b + 1)
                for a in range(min(4, TILES - 4 * b)):
                    last = pe.transpose(banks[:, 4 * (j % 2) + b, a * P:(a + 1) * P], level[j][:, 4 * b + a, :], k.ident)
                last.then_inc(tiles_turned, 1)

        pe.sem_inc(bank_read, BANKS_JOB)
        in_pipeline(element, pe)

    return sync, tensor, vector, scalar, gpsimd


def mix_stage(k):
    nc, t, banks = k.nc, k.t, k.banks
    with ExitStack() as own:
        x_turned = [k.buffer(own, f"x_turned{d}", [DC, TOK]) for d in range(2)]
        x_rows = k.buffer(own, "x_rows", [B, D])
        w_rkv = k.buffer(own, "w_rkv", [DC, 6 * D])
        w_out = k.buffer(own, "w_out", [UNITS, D])
        decay = k.buffer(own, "decay", [UNITS])
        first = k.buffer(own, "first", [UNITS])
        step_decay = k.buffer(own, "step_decay", [UNITS])
        top = [k.buffer(own, f"top{p}", [GB, S + 1]) for p in range(2)]
        gap = [k.buffer(own, f"gap{p}", [2, GT]) for p in range(2)]
        weight = [k.buffer(own, f"weight{p}", [4, GT]) for p in range(2)]
        values = [k.buffer(own, f"values{p}", [GT]) for p in range(2)]
        gate = [k.buffer(own, f"gate{p}", [GT]) for p in range(2)]
        new_value = [k.buffer(own, f"new_value{p}", [2, GT]) for p in range(2)]
        carry = [k.buffer(own, f"carry{p}", [2, GT + 1]) for p in range(2)]
        old_part = [k.buffer(own, f"old_part{p}", [2, GT]) for p in range(2)]
        ratio = [k.buffer(own, f"ratio{p}", [2, GT]) for p in range(2)]
        y = k.buffer(own, "y", [UNITS, GB, S])
        summed = k.buffer(own, "summed", [GB, D])
        mixed = k.buffer(own, "mixed", [GB, D])
        ln_stat = k.buffer(own, "ln_stat", [GB, 6])
        ln_mean = k.buffer(own, "ln_mean", [GB, 2])
        ln_eps = k.buffer(own, "ln_eps", [GB])
        ln_scale = k.buffer(own, "ln_scale", [GB])
    mix_loads = k.semaphore("mix_loads")
    decay_ready = k.semaphore("decay_ready")
    rkv_ready = k.semaphore("rkv_ready")
    vr_ready = k.semaphore("vr_ready")
    gaps_ready = k.semaphore("gaps_ready")
    weights_ready = k.semaphore("weights_ready")
    new_ready = k.semaphore("new_ready")
    scans_ready = k.semaphore("scans_ready")
    old_ready = k.semaphore("old_ready")
    unit_done = k.semaphore("unit_done")
    mix_out = k.semaphore("mix_out")
    mix_var = k.semaphore("mix_var")
    mix_scale = k.semaphore("mix_scale")
    mix_normed = k.semaphore("mix_normed")
    k.mix_stored = k.semaphore("mix_stored")
    mix_free = k.semaphore("mix_free")
    LOADS = 7
    FROM_PAST, FROM_NEW, OLD, NOW = range(4)

    def sync(sp):
        for src, dst in ((t["rkv_t"], w_rkv), (t["x_fwd_t"], x_turned[0]), (t["x_bwd_t"], x_turned[1])):
            sp.dma_start(dst[:, :, :], src.rearrange("(c p) n -> p c n", p=P)).then_inc(mix_loads, 16)
        sp.dma_start(decay[:, :], t["decay"]).then_inc(mix_loads, 16)
        sp.dma_start(first[:, :], t["first"]).then_inc(mix_loads, 16)
        sp.dma_start(w_out[:, :, :], t["out_t"].rearrange("(c p) n -> p c n", p=P)).then_inc(mix_loads, 16)
        sp.dma_start(x_rows[:, :, :], t["x"].rearrange("(b p) n -> p b n", p=P)).then_inc(mix_loads, 16)
        sp.sem_inc(mix_free, 1)
        with sp.Fori(0, GROUPS) as g:
            sp.wait_ge(mix_normed, g + 1)
            sp.dma_start(k.mixed_d[bass.ds(g * GT, GT), :].rearrange("(b p) n -> p b n", p=P),
                         mixed[:, :, :]).then_inc(k.mix_stored, 16)
            sp.wait_ge(k.mix_stored, 16 * g + 16)
            sp.sem_inc(mix_free, 1)

    def tensor(pe):
        pe.wait_ge(mix_loads, 16 * LOADS)

        def project(g, u, n, wait=True):
            d, c = u // DC, u % DC
            if wait:
                pe.wait_ge(vr_ready, n - 1)
                pe.wait_ge(gaps_ready, n - 1)
            for m in range(3):
                for kc in range(DC):
                    col = (3 * d + m) * D + c * P
                    last = pe.matmul(banks[:, 3 * (u % 2) + m, :], w_rkv[:, kc, col:col + P],
                                     x_turned[d][:, kc, bass.ds(g * GT, GT)], start=(kc == 0), stop=(kc == DC - 1))
            last.then_inc(rkv_ready, 1)

        def project_out(g):
            pe.wait_ge(unit_done, 2 + UNITS * g + UNITS)
            for b in range(GB):
                if b % 2 == 0:
                    pe.wait_ge(mix_free, g + 1)
                for u in range(UNITS):
                    last = pe.matmul(banks[:, 6 + b // 2, (b % 2) * D:(b % 2 + 1) * D], y[:, u, b, :],
                                     w_out[:, u, :], start=(u == 0), stop=(u == UNITS - 1))
                if b % 2:
                    last.then_inc(mix_out, 1)

        project(0, 0, 0, False)
        project(0, 1, 1, False)
        with pe.Fori(0, GROUPS - 1) as g:
            for u in range(UNITS):
                project(g + (u + 2) // UNITS, (u + 2) % UNITS, UNITS * g + u + 2)
            project_out(g)
        for u in (2, 3):
            project(GROUPS - 1, u, UNITS * (GROUPS - 1) + u)
        project_out(GROUPS - 1)

    def scalar(act):
        act.wait_ge(mix_loads, 16 * LOADS)
        act.activation(step_decay[:, :], decay[:, :], ACT.Exp).then_inc(decay_ready, 1)
        with act.Fori(0, GROUPS) as g:
            for u in range(UNITS):
                p, n = u % 2, UNITS * g + u
                act.wait_ge(rkv_ready, n + 1)
                act.wait_ge(unit_done, n + 1)
                act.activation(gate[p][:, :], banks[:, 3 * p, :], ACT.Exp, scale=-1.0)
                act.copy(values[p][:, :], banks[:, 3 * p + 2, :]).then_inc(vr_ready, 1)
                act.wait_ge(gaps_ready, n + 1)
                act.activation(weight[p][:, :, :], weight[p][:, :, :], ACT.Exp).then_inc(weights_ready, 1)

    def gpsimd(pool):
        with pool.Fori(0, GROUPS) as g:
            for u in range(UNITS):
                p, n = u % 2, UNITS * g + u
                pool.wait_ge(weights_ready, n + 1)
                pool.tensor_tensor(new_value[p][:, 0, :], weight[p][:, FROM_NEW, :], values[p][:, :],
                                   ALU.mult).then_inc(new_ready, 1)
                pool.tensor_tensor(new_value[p][:, 1, :], weight[p][:, NOW, :], values[p][:, :], ALU.mult)
                pool.wait_ge(scans_ready, n + 1)
                for m in range(2):
                    last = pool.tensor_tensor(old_part[p][:, m, :], weight[p][:, OLD, :], carry[p][:, m, 0:GT],
                                              ALU.mult)
                last.then_inc(old_ready, 1)
            pool.wait_ge(mix_var, g + 1)
            pool.tensor_tensor(ln_scale[:, :], ln_eps[:, :], k.minus_half[:, 0:GB], ALU.pow).then_inc(mix_scale, 1)

    def vector(dve):
        st = k.steps["dve"]

        def gaps(u, n):
            p = u % 2
            dve.wait_ge(rkv_ready, n + 1)
            key = banks[:, 3 * p + 1, :]
            for b in range(GB):
                last = dve.tensor_tensor_scan(top[p][:, b, 1:S + 1], step_decay[:, u:u + 1].to_broadcast([P, S]),
                                              key[:, b * S:(b + 1) * S], LOWEST, ALU.add, ALU.max)
            st.did(last)
            st.wait()
            before = top[p][:, :, 0:S]
            keys = key.rearrange("p (b s) -> p b s", b=GB)
            past, now = (gap[p][:, m, :].rearrange("p (b s) -> p b s", b=GB) for m in range(2))
            dve.scalar_tensor_tensor(out=past, in0=before, scalar=step_decay[:, u:u + 1], in1=keys,
                                     op0=ALU.add, op1=ALU.subtract)
            st.did(dve.scalar_tensor_tensor(out=now, in0=keys, scalar=first[:, u:u + 1], in1=before,
                                            op0=ALU.add, op1=ALU.subtract))
            st.wait()
            dve.tensor_scalar(weight[p][:, FROM_PAST, :], gap[p][:, 0, :], 0.0, None, ALU.min)
            dve.tensor_scalar(weight[p][:, FROM_NEW, :], gap[p][:, 0, :], -1.0, 0.0, ALU.mult, ALU.min)
            dve.tensor_scalar(weight[p][:, OLD, :], gap[p][:, 1, :], -1.0, 0.0, ALU.mult, ALU.min)
            dve.tensor_scalar(weight[p][:, NOW, :], gap[p][:, 1, :], 0.0, None, ALU.min).then_inc(gaps_ready, 1)

        def scans(u, n):
            p = u % 2
            dve.wait_ge(weights_ready, n + 1)
            dve.tensor_tensor_scan(carry[p][:, 1, 1:GT + 1], weight[p][:, FROM_PAST, :], weight[p][:, FROM_NEW, :],
                                   0.0, ALU.mult, ALU.add)
            dve.wait_ge(new_ready, n + 1)
            dve.tensor_tensor_scan(carry[p][:, 0, 1:GT + 1], weight[p][:, FROM_PAST, :], new_value[p][:, 0, :],
                                   0.0, ALU.mult, ALU.add).then_inc(scans_ready, 1)

        def finish(u, n):
            p = u % 2
            dve.wait_ge(old_ready, n + 1)
            st.did(dve.tensor_tensor(ratio[p][:, 1, :], old_part[p][:, 1, :], weight[p][:, NOW, :], ALU.add))
            st.did(dve.tensor_tensor(ratio[p][:, 0, :], old_part[p][:, 0, :], new_value[p][:, 1, :], ALU.add))
            st.wait()
            st.did(dve.scalar_tensor_tensor(out=old_part[p][:, 1, :], in0=gate[p][:, :], scalar=1.0,
                                            in1=ratio[p][:, 1, :], op0=ALU.add, op1=ALU.mult))
            st.wait()
            st.did(dve.reciprocal(ratio[p][:, 1, :], old_part[p][:, 1, :]))
            st.wait()
            num, rec = (ratio[p][:, m, :].rearrange("p (b s) -> p b s", b=GB) for m in range(2))
            to = y[:, u, :, :] if u < DC else y[:, u, :, ::-1]
            dve.tensor_tensor(to, num, rec, ALU.mult).then_inc(unit_done, 1)

        def norm(g):
            for b in range(GB):
                if b % 2 == 0:
                    dve.wait_ge(mix_out, 2 * g + b // 2 + 1)
                last = dve.tensor_tensor(
                    summed[:, b:b + 1, :], banks[:, 6 + b // 2:7 + b // 2, (b % 2) * D:(b % 2 + 1) * D],
                    x_rows[:, bass.ds(GB * g + b, 1), :], ALU.add)
            st.did(last)
            st.wait()
            for b in range(GB):
                last = dve.bn_stats(ln_stat[:, b, :], summed[:, b, :])
            st.did(last)
            st.wait()
            dve.sem_inc(k.s_held, 1)
            for b in range(GB):
                last = dve.bn_aggr(ln_mean[:, b, :], ln_stat[:, b, :])
            st.did(last)
            st.wait()
            dve.tensor_scalar(ln_eps[:, :], ln_mean[:, :, 1], EPS, None, ALU.add).then_inc(mix_var, 1)
            dve.wait_ge(mix_scale, g + 1)
            dve.wait_ge(mix_free, g + 1)
            for b in range(GB):
                last = dve.tensor_scalar(mixed[:, b, :], summed[:, b, :], ln_mean[:, b, 0:1], ln_scale[:, b:b + 1],
                                         ALU.subtract, ALU.mult)
            last.then_inc(mix_normed, 1)

        dve.wait_ge(mix_loads, 16 * LOADS)
        for p in range(2):
            dve.memset(top[p][:, :, 0:1], LOWEST)
            st.did(dve.memset(carry[p][:, :, 0:1], 0.0))
        dve.sem_inc(unit_done, 2)
        dve.wait_ge(decay_ready, 1)
        st.did(dve.tensor_scalar(step_decay[:, :], step_decay[:, :], -1.0, None, ALU.mult))
        st.wait()
        st.done(1, 3)
        PER = 6 * UNITS + 3
        gaps(0, 0)
        st.done(1, 2)
        with dve.Fori(0, GROUPS - 1) as g:
            st.turn(g, PER)
            for u in range(UNITS):
                n = UNITS * g + u
                scans(u, n)
                gaps((u + 1) % UNITS, n + 1)
                finish(u, n)
            norm(g)
        st.done(GROUPS - 1, PER)
        for u in range(UNITS):
            n = UNITS * (GROUPS - 1) + u
            scans(u, n)
            if u + 1 < UNITS:
                gaps(u + 1, n + 1)
            finish(u, n)
        norm(GROUPS - 1)
        st.done(1, PER - 2)

    return sync, tensor, vector, scalar, gpsimd


def norm_stats(k, dve, st, stats, mean, eps, rows):
    st.did(dve.bn_stats(stats, rows))
    st.wait()
    dve.sem_inc(k.s_held, 1)
    st.did(dve.bn_aggr(mean, stats))
    st.wait()
    return dve.tensor_scalar(eps, mean[:, 1:2], EPS, None, ALU.add)


def cross_stage(k):
    nc, t, banks = k.nc, k.t, k.banks
    with ExitStack() as own:
        wq, wk, wv, wo = (k.buffer(own, n, [DC, D]) for n in ("w_q", "w_k", "w_v", "w_o"))
        bqk = k.buffer(own, "bqk", [2 * DC])
        bias_rows = k.buffer(own, "bias_rows", [2, D])
        x_in = [k.buffer(own, f"x_in{j}", [D]) for j in range(2)]
        ctx_t = [k.buffer(own, f"ctx_t{j}", [DC, S]) for j in range(2)]
        x_t = [k.buffer(own, f"x_t{j}", [DC, S]) for j in range(2)]
        q_t = [k.buffer(own, f"q_t{j}", [DC, S]) for j in range(2)]
        k_t = [k.buffer(own, f"k_t{j}", [DC, S]) for j in range(2)]
        spread = [k.buffer(own, f"spread{h}", [HALF, S]) for h in range(2)]
        v_ones = [k.buffer(own, f"v_ones{j}", [XH, XK + 1]) for j in range(2)]
        x_bias = [k.buffer(own, f"x_bias{j}", [D]) for j in range(2)]
        peak = [k.buffer(own, f"peak{h}", [HALF]) for h in range(2)]
        probs = [k.buffer(own, f"probs{h}", [HALF, S]) for h in range(2)]
        probs_t = [k.buffer(own, f"probs_t{h}", [HALF, S]) for h in range(2)]
        total = k.buffer(own, "total", [XH])
        heads = [k.buffer(own, f"heads{j}", [XH, XK]) for j in range(2)]
        heads_t = [k.buffer(own, f"heads_t{j}", [DC, S]) for j in range(2)]
        joined = [k.buffer(own, f"joined{j}", [D]) for j in range(2)]
        ln = [k.buffer(own, f"cross_ln{j}", [12]) for j in range(2)]
        crossed = [k.buffer(own, f"crossed{j}", [D]) for j in range(2)]
    cross_loads = k.semaphore("cross_loads")
    rows_in = [k.semaphore(f"rows_in{j}") for j in range(2)]
    x_turned = k.semaphore("cross_x_turned")
    x_t_ready = k.semaphore("x_t_ready")
    qk_ready = k.semaphore("qk_ready")
    qk_read = k.semaphore("qk_read")
    v_ready = k.semaphore("v_ready")
    v_read = k.semaphore("v_read")
    spread_ready = k.semaphore("spread_ready")
    bias_added = k.semaphore("bias_added")
    scores_ready = k.semaphore("scores_ready")
    scores_read = k.semaphore("scores_read")
    exp_ready = k.semaphore("exp_ready")
    probs_turned = k.semaphore("probs_turned")
    probs_t_ready = k.semaphore("probs_t_ready")
    heads_summed = k.semaphore("heads_summed")
    heads_ready = k.semaphore("heads_ready")
    heads_turned = k.semaphore("heads_turned")
    heads_t_ready = k.semaphore("heads_t_ready")
    joined_ready = k.semaphore("joined_ready")
    cross_var = k.semaphore("cross_var")
    cross_scale = k.semaphore("cross_scale")
    cross_normed = k.semaphore("cross_normed")
    k.cross_stored = [k.semaphore(f"cross_stored{j}") for j in range(2)]
    LOADS = 7
    TURNS = B // 2
    TURN, QK, V, SCORES, PROBS_T, HEADS = 0, 1, 2, 3, 5, 7

    joined_read = k.semaphore("joined_read")

    def in_steps(emit, eng, st=None, per=None):
        emit(0, 0, -1, False, True)
        if st:
            st.done(1, st.at)
        with eng.Fori(0, TURNS - 1) as i:
            if st:
                st.turn(i, per)
            for j in (1, 0):
                emit(j, 2 * i + 2 - j, i, True, True)
        if st:
            st.done(TURNS - 1, per)
        emit(1, B - 1, TURNS - 1, True, False)

    def sync(sp):
        for n, dst in (("wq", wq), ("wk", wk), ("wv", wv), ("wo", wo)):
            sp.dma_start(dst[:, :, :], t[n].rearrange("(c p) n -> p c n", p=P)).then_inc(cross_loads, 16)
        sp.dma_start(bqk[:, :], t["bqk"]).then_inc(cross_loads, 16)
        for m in range(2):
            sp.dma_start(bias_rows[:, m, :], t["rows"][m:m + 1, :].to_broadcast([P, D])).then_inc(cross_loads, 16)
        for j in range(2):
            sp.sem_inc(k.cross_stored[j], 16)

        def load(j, n):
            sp.dma_start(x_in[j][:, :], k.mixed_d[bass.ds(n * S, S), :]).then_inc(rows_in[j], 16)
            sp.dma_start(ctx_t[j][:, :, :], t["ctx_t"].rearrange("(c p) n -> p c n", p=P)[
                :, :, bass.ds(n * S, S)]).then_inc(rows_in[j], 16)

        def store(j, n):
            sp.wait_ge(cross_normed, n + 1)
            sp.dma_start(k.crossed_d[bass.ds(n * S, S), :], crossed[j][:, :]).then_inc(k.cross_stored[j], 16)

        load(0, 0)
        load(1, 1)
        with sp.Fori(0, TURNS - 1) as i:
            for j in range(2):
                n = 2 * i + j
                sp.wait_ge(v_ready, n + 1)
                sp.wait_ge(bias_added, n + 1)
                load(j, n + 2)
                store(j, n)
        for j in range(2):
            store(j, B - 2 + j)
            sp.wait_ge(k.cross_stored[j], 16 * TURNS + 16)

    def tensor(pe):
        pe.wait_ge(cross_loads, 16 * LOADS)
        pe.sem_inc(scores_ready, 2)
        pe.sem_inc(probs_turned, 4)

        def front(j, n, i, begin=False):
            pe.wait_ge(rows_in[j], 32 * i + 32)
            if not begin:
                pe.wait_ge(heads_t_ready, n)
            for c in range(DC):
                last = pe.transpose(banks[:, TURN, c * P:(c + 1) * P], x_in[j][:, c * P:(c + 1) * P], k.ident)
            last.then_inc(x_turned, 1)
            if not begin:
                pe.wait_ge(qk_read, n)
            for m in range(DC):
                for c in range(DC):
                    pe.matmul(banks[:, QK, (DC + m) * P:(DC + m + 1) * P], wk[:, c, m * P:(m + 1) * P],
                              ctx_t[j][:, c, :], start=(c == 0), stop=(c == DC - 1))
            pe.wait_ge(x_t_ready, n + 1)
            for m in range(DC):
                for c in range(DC):
                    last = pe.matmul(banks[:, QK, m * P:(m + 1) * P], wq[:, c, m * P:(m + 1) * P],
                                     x_t[j][:, c, :], start=(c == 0), stop=(c == DC - 1))
            last.then_inc(qk_ready, 1)
            if not begin:
                pe.wait_ge(v_read, n)
                pe.wait_ge(joined_read, n)
            for c in range(DC):
                last = pe.matmul(banks[:, V, 0:D], ctx_t[j][:, c, :], wv[:, c, :], start=(c == 0), stop=(c == DC - 1))
            last.then_inc(v_ready, 1)

        def scores(j, h, n, begin=False):
            pe.wait_ge(spread_ready, 2 * n + h + 1)
            if not begin:
                pe.wait_ge(scores_read, 2 * n + h)
            for m in range(2):
                last = pe.matmul(banks[:, SCORES + m, :], q_t[j][:, h, :],
                                 spread[h][:, 4 * m:4 * m + 4, :].rearrange("p h s -> p (h s)"), start=True, stop=True)
            last.then_inc(scores_ready, 1)

        def turn_probs(h, n):
            pe.wait_ge(exp_ready, 2 * n + h + 1)
            for m in range(2):
                pe.wait_ge(probs_t_ready, 4 * n + 2 * h + m + 1)
                for a in range(4):
                    last = pe.transpose(banks[:, PROBS_T + m, a * P:(a + 1) * P], probs[h][:, 4 * m + a, :], k.ident)
                last.then_inc(probs_turned, 1)

        def sums(j, h, n):
            if h == 0:
                pe.wait_ge(v_read, n + 1)
                pe.wait_ge(heads_ready, n + 1)
            for m in range(2):
                pe.wait_ge(probs_t_ready, 4 * n + 2 * h + m + 3)
                for a in range(4):
                    head = HALF * h + 4 * m + a
                    last = pe.matmul(banks[:, HEADS, head * (XK + 1):(head + 1) * (XK + 1)], probs_t[h][:, 4 * m + a, :],
                                     v_ones[j][:, head, :], start=True, stop=True)
            if h:
                last.then_inc(heads_summed, 1)

        def turn_heads(j, n, more):
            pe.wait_ge(heads_ready, n + 2)
            pe.wait_ge(x_t_ready, n + 1 + more)
            for c in range(DC):
                last = pe.transpose(banks[:, TURN, c * P:(c + 1) * P],
                                    heads[j][:, HALF * c:HALF * (c + 1), :].rearrange("p h d -> p (h d)"), k.ident)
            last.then_inc(heads_turned, 1)

        def join(j, n, more):
            pe.wait_ge(heads_t_ready, n + 2)
            pe.wait_ge(v_read, n + 1 + more)
            for c in range(DC):
                last = pe.matmul(banks[:, V, 0:D], heads_t[j][:, c, :], wo[:, c, :], start=(c == 0), stop=(c == DC - 1))
            last.then_inc(joined_ready, 1)

        def step(j, n, i, prev, more):
            scores(j, 1, n)
            if prev:
                turn_heads(1 - j, n - 1, 1)
            turn_probs(0, n)
            if prev:
                join(1 - j, n - 1, 1)
            if more:
                front(1 - j, n + 1, i + 1)
            sums(j, 0, n)
            turn_probs(1, n)
            if more:
                scores(1 - j, 0, n + 1)
            sums(j, 1, n)

        front(0, 0, 0, True)
        scores(0, 0, 0, True)
        in_steps(step, pe)
        turn_heads(1, B - 1, 0)
        join(1, B - 1, 0)

    def scalar(act):
        act.wait_ge(cross_loads, 16 * LOADS)
        act.sem_inc(heads_t_ready, 1)
        act.sem_inc(probs_t_ready, 2)

        def front(j, n):
            act.wait_ge(x_turned, n + 1)
            act.copy(x_t[j][:, :, :], banks[:, TURN, 0:D].rearrange("p (c s) -> p c s", c=DC)).then_inc(x_t_ready, 1)
            act.wait_ge(qk_ready, n + 1)
            for c in range(DC):
                act.activation(k_t[j][:, c, :], banks[:, QK, (DC + c) * P:(DC + c + 1) * P], ACT.Identity,
                               bias=bqk[:, DC + c:DC + c + 1])
            for c in range(DC):
                last = act.activation(q_t[j][:, c, :], banks[:, QK, c * P:(c + 1) * P], ACT.Identity,
                                      bias=bqk[:, c:c + 1])
            last.then_inc(qk_read, 1)

        def soften(h, n):
            act.wait_ge(scores_read, 2 * n + h + 1)
            act.activation(probs[h][:, :, :], probs[h][:, :, :], ACT.Exp, scale=float(XK) ** -0.5).then_inc(exp_ready, 1)

        def collect(h, n):
            for m in range(2):
                act.wait_ge(probs_turned, 4 * n + 2 * h + m + 5)
                act.copy(probs_t[h][:, 4 * m:4 * m + 4, :], banks[:, PROBS_T + m, :].rearrange(
                    "p (a s) -> p a s", a=4)).then_inc(probs_t_ready, 1)

        def back(j, n):
            act.wait_ge(heads_turned, n + 1)
            act.copy(heads_t[j][:, :, :], banks[:, TURN, 0:D].rearrange("p (c s) -> p c s", c=DC)).then_inc(
                heads_t_ready, 1)

        def step(j, n, i, prev, more):
            if prev:
                back(1 - j, n - 1)
            collect(0, n)
            soften(1, n)
            if more:
                front(1 - j, n + 1)
            collect(1, n)
            if more:
                soften(0, n + 1)

        front(0, 0)
        soften(0, 0)
        in_steps(step, act)
        back(1, B - 1)

    def gpsimd(pool):
        pool.wait_ge(cross_loads, 16 * LOADS)
        head_mask = k.consts[:, C_HEAD:C_HEAD + HALF]

        def spread_keys(j, h, n):
            pool.wait_ge(qk_read, n + 1)
            pool.wait_ge(scores_ready, 2 * n + h + 1)
            pool.tensor_tensor(spread[h][:, :, :], each(k_t[j][:, h, :], HALF), wide(head_mask, S),
                               ALU.mult).then_inc(spread_ready, 1)

        def add_bias(j, n, i, begin=False):
            pool.wait_ge(rows_in[j], 32 * i + 32)
            if not begin:
                pool.wait_ge(joined_read, n)
            pool.tensor_tensor(x_bias[j][:, :], x_in[j][:, :], bias_rows[:, 1, :], ALU.add).then_inc(bias_added, 1)

        def scale(j, n):
            pool.wait_ge(cross_var, n + 1)
            pool.tensor_tensor(ln[j][:, 9:10], ln[j][:, 8:9], k.minus_half[:, 0:1], ALU.pow).then_inc(cross_scale, 1)

        def step(j, n, i, prev, more):
            if prev:
                scale(1 - j, n - 1)
            if more:
                add_bias(1 - j, n + 1, i + 1, not prev)
                spread_keys(1 - j, 0, n + 1)
                spread_keys(1 - j, 1, n + 1)

        add_bias(0, 0, 0, True)
        for h in range(2):
            spread_keys(0, h, 0)
        in_steps(step, pool)
        scale(1, B - 1)

    def vector(dve):
        st = k.steps["dve"]

        def take_values(j, n):
            dve.wait_ge(v_ready, n + 1)
            dve.tensor_tensor(v_ones[j][:, :, 0:XK], banks[:, V, 0:D].rearrange("p (h d) -> p h d", h=XH),
                              bias_rows[:, 0, :].rearrange("p (h d) -> p h d", h=XH), ALU.add).then_inc(v_read, 1)

        def peaks(h, n):
            dve.wait_ge(scores_ready, 2 * n + h + 3)
            chunk = banks[:, SCORES:SCORES + 2, :].rearrange("p m (a s) -> p (m a) s", a=4)
            st.did(dve.tensor_reduce(peak[h][:, :], chunk, AX.X, ALU.max))
            st.wait()
            dve.wait_ge(probs_turned, 4 * n + 2 * h + 2)
            dve.tensor_tensor(probs[h][:, :, :], chunk, wide(peak[h][:, :], S), ALU.subtract).then_inc(scores_read, 1)

        def normalise(j, n):
            dve.wait_ge(heads_summed, n + 1)
            all_heads = banks[:, HEADS, 0:XH * (XK + 1)].rearrange("p (h d) -> p h d", h=XH)
            st.did(dve.reciprocal(total[:, :], all_heads[:, :, XK]))
            st.wait()
            dve.tensor_tensor(heads[j][:, :, :], all_heads[:, :, 0:XK], wide(total[:, :], XK), ALU.mult).then_inc(
                heads_ready, 1)

        def join(j, n, i):
            dve.wait_ge(joined_ready, n + 1)
            dve.wait_ge(bias_added, n + 1)
            dve.tensor_tensor(joined[j][:, :], banks[:, V, 0:D], x_bias[j][:, :], ALU.add).then_inc(joined_read, 1)
            dve.wait_ge(joined_read, n + 2)
            norm_stats(k, dve, st, ln[j][:, 0:6], ln[j][:, 6:8], ln[j][:, 8:9], joined[j][:, :]).then_inc(cross_var, 1)
            dve.wait_ge(cross_scale, n + 1)
            dve.wait_ge(k.cross_stored[j], 16 * i + 16)
            dve.tensor_scalar(crossed[j][:, :], joined[j][:, :], ln[j][:, 6:7], ln[j][:, 9:10],
                              ALU.subtract, ALU.mult).then_inc(cross_normed, 1)

        def step(j, n, i, prev, more):
            peaks(1, n)
            if prev:
                join(1 - j, n - 1, i)
            if more:
                take_values(1 - j, n + 1)
                peaks(0, n + 1)
            normalise(j, n)

        dve.wait_ge(cross_loads, 16 * LOADS)
        dve.sem_inc(joined_read, 1)
        dve.sem_inc(heads_ready, 1)
        for j in range(2):
            dve.memset(v_ones[j][:, :, XK:XK + 1], 1.0)
        take_values(0, 0)
        peaks(0, 0)
        st.done(1, 1)
        in_steps(step, dve, st, 2 * 5)
        join(1, B - 1, TURNS - 1)
        st.done(1, st.at)

    return sync, tensor, vector, scalar, gpsimd


def attend_stage(k):
    nc, t, banks = k.nc, k.t, k.banks
    QKV = (QH + 2 * KVH) * HD
    with ExitStack() as own:
        weights = k.buffer(own, "attend_w", [3 * TILES, P])
        gate_w = k.buffer(own, "gate_w", [DC, E])
        gains = k.buffer(own, "gains", [2, D])
        row_in = [k.buffer(own, f"row_in{j}", [D]) for j in range(2)]
        row_res = [k.buffer(own, f"row_res{j}", [D]) for j in range(2)]
        squares = [k.buffer(own, f"squares{a}", [D]) for a in range(2)]
        rms = [k.buffer(own, f"rms{a}", [3]) for a in range(2)]
        xn = k.buffer(own, "xn", [D])
        xn_t = k.buffer(own, "xn_t", [DC, S])
        q_rot = k.buffer(own, "q_rot", [QH, HD])
        q_sin = k.buffer(own, "q_sin", [QH, HD])
        kv_stat = k.buffer(own, "kv_stat", [8, 2 * KVH])
        kvq = [k.buffer(own, f"kvq{j}", [2 * KVH, HD]) for j in range(2)]
        k_rot = k.buffer(own, "k_rot", [KVH, HD])
        k_sin = k.buffer(own, "k_sin", [KVH, HD])
        q_turn = k.buffer(own, "q_turn", [QH, S])
        k_turn = k.buffer(own, "k_turn", [KVH, S])
        probs = k.buffer(own, "att_probs", [QH, S])
        low_peak = k.buffer(own, "low_peak", [QH])
        total = k.buffer(own, "att_total", [QH])
        share = k.buffer(own, "att_share", [QH])
        probs_turn = k.buffer(own, "probs_turn", [QH, S])
        o_turn = k.buffer(own, "o_turn", [QH, S])
        hidden = [k.buffer(own, f"hidden{j}", [D]) for j in range(2)]
        normed = [k.buffer(own, f"normed{j}", [D]) for j in range(2)]
        hn_turn = k.buffer(own, "hn_turn", [DC, S])
    names = ("attend_loads xn_var xn_scale xn_ready xn_turned xn_t_ready kv_ready q_ready roped_q q_rot_ready kv_scaled "
             "kv_rounded k_rot_ready q_turned q_t_ready k_turned k_t_ready scores2 masked peaked exped share_ready probs_ready probs_turned2 "
             "probs_t2 o_summed o_t_ready hidden_ready hn_var hn_scale hn_ready hn_turned hn_t_ready logits_ready").split()
    s = {n: k.semaphore(n) for n in names}
    k.logits_read = k.semaphore("logits_read")
    row_loaded = [k.semaphore(f"row_loaded{j}") for j in range(2)]
    res_loaded = [k.semaphore(f"res_loaded{j}") for j in range(2)]
    attend_stored = [k.semaphore(f"attend_stored{j}") for j in range(2)]
    LOADS, TURNS = 6, B // 2
    TURN, Q, KV, PROBS_T, Q_T = 0, 1, 3, 4, 6
    MAX, MIN, SCALE, INV, BASE, LOW, HIGH, TMP = range(8)
    HALF_HD = HD // 2

    def in_steps(emit, eng, st=None, per=None):
        emit(0, 0, -1, False, 2)
        if st:
            st.done(1, st.at)
        with eng.Fori(0, TURNS - 2) as i:
            if st:
                st.turn(i, per)
            for j in (1, 0):
                emit(j, 2 * i + 2 - j, i, True, 2)
        if st:
            st.done(TURNS - 2, per)
        for j, n, more in ((1, B - 3, 2), (0, B - 2, 1), (1, B - 1, 0)):
            emit(j, n, (n - 1) // 2, True, more)

    def sync(sp):
        for m in range(3):
            sp.dma_start(weights[:, TILES * m:TILES * (m + 1), :],
                         k.weights_d[m].rearrange("p (a b) -> p a b", a=TILES)).then_inc(s["attend_loads"], 16)
        sp.dma_start(gate_w[:, :, :], t["gate_t"].rearrange("(c p) e -> p c e", p=P)).then_inc(s["attend_loads"], 16)
        for m in range(2):
            sp.dma_start(gains[:, m, :], t["rows"][2 + m:3 + m, :].to_broadcast([P, D])).then_inc(s["attend_loads"], 16)

        def load(dst, sem, n):
            sp.dma_start(dst[:, :], k.crossed_d[bass.ds(n * S, S), :]).then_inc(sem, 16)

        def load_row(j, n, begin=False):
            if not begin:
                sp.wait_ge(s["xn_ready"], n - 1)
            load(row_in[j], row_loaded[j], n)

        def element(j, n, rows=True, res=True):
            sp.wait_ge(s["hn_ready"], n + 1)
            for src, dst in ((hidden, k.hidden_d), (normed, k.normed_d)):
                sp.dma_start(dst[bass.ds(n * S, S), :], src[j][:, :]).then_inc(attend_stored[j], 16)
            if res:
                load(row_res[j], res_loaded[j], n + 2)
            if rows:
                load_row(1 - j, n + 5)

        for j in range(2):
            sp.sem_inc(attend_stored[j], 32)
            load_row(j, j, True)
            load(row_res[j], res_loaded[j], j)
        for n in range(2, 5):
            load_row(n % 2, n)
        with sp.Fori(0, (B - 6) // 2) as i:
            for j in range(2):
                element(j, 2 * i + j)
        for n in range(B - 6, B):
            element(n % 2, n, n + 5 < B, n + 2 < B)
        for j in range(2):
            sp.wait_ge(attend_stored[j], 32 * TURNS + 32)

    def tensor(pe):
        pe.wait_ge(s["attend_loads"], 16 * LOADS)
        w_qkv = weights[:, 0:2 * QKV // P, :].rearrange("p (c r) j -> p c (r j)", c=DC)
        w_o = weights[:, 2 * QKV // P:2 * QKV // P + DC * QH, :].rearrange("p (h c) j -> p h (c j)", c=DC)

        def turn_x(n):
            pe.wait_ge(s["xn_ready"], n + 1)
            for c in range(DC):
                last = pe.transpose(banks[:, TURN, c * P:(c + 1) * P], xn[:, c * P:(c + 1) * P], k.ident)
            last.then_inc(s["xn_turned"], 1)

        def project(n, begin=False):
            pe.wait_ge(s["xn_t_ready"], n + 1)
            if not begin:
                pe.wait_ge(s["k_t_ready"], n)
            for c in range(DC):
                last = pe.matmul(banks[:, KV, :], xn_t[:, c, :], w_qkv[:, c, QH * HD:QKV], start=(c == 0), stop=(c == DC - 1))
            last.then_inc(s["kv_ready"], 1)
            if not begin:
                pe.wait_ge(s["masked"], n)
            for m in range(2):
                for c in range(DC):
                    last = pe.matmul(banks[:, Q + m, :], xn_t[:, c, :], w_qkv[:, c, 512 * m:512 * m + 512],
                                     start=(c == 0), stop=(c == DC - 1))
            last.then_inc(s["q_ready"], 1)

        def turn_q(n):
            pe.wait_ge(s["q_rot_ready"], n + 1)
            for m in range(2):
                for a in range(4):
                    last = pe.transpose(banks[:, Q_T + m, a * P:(a + 1) * P], q_rot[:, 4 * m + a, :], k.ident)
                last.then_inc(s["q_turned"], 1)

        def turn_k(n):
            pe.wait_ge(s["k_rot_ready"], n + 1)
            for a in range(KVH):
                last = pe.transpose(banks[:, KV, a * P:(a + 1) * P], k_rot[:, a, :], k.ident)
            last.then_inc(s["k_turned"], 1)

        def scores(n):
            pe.wait_ge(s["q_t_ready"], 2 * n + 2)
            pe.wait_ge(s["k_t_ready"], n + 1)
            for h in range(QH):
                last = pe.matmul(banks[:, Q + h // 4, (h % 4) * S:(h % 4 + 1) * S], q_turn[:, h, :], k_turn[:, h // REP, :],
                                 start=True, stop=True)
            last.then_inc(s["scores2"], 1)

        def turn_probs(n):
            pe.wait_ge(s["probs_ready"], n + 1)
            for m in range(2):
                for a in range(4):
                    last = pe.transpose(banks[:, PROBS_T + m, a * P:(a + 1) * P], probs[:, 4 * m + a, :], k.ident)
                last.then_inc(s["probs_turned2"], 1)

        def sums(j, n):
            for m in range(KVH):
                pe.wait_ge(s["probs_t2"], 2 * n + m + 1)
                pe.matmul(banks[:, PROBS_T + m, :], kvq[j][:, KVH + m, :],
                          probs_turn[:, REP * m:REP * (m + 1), :].rearrange("p h s -> p (h s)"),
                          start=True, stop=True).then_inc(s["o_summed"], 1)

        def join(n):
            pe.wait_ge(s["o_t_ready"], 2 * n + 2)
            for h in range(QH):
                last = pe.matmul(banks[:, TURN, 0:D], o_turn[:, h, :], w_o[:, h, :], start=(h == 0), stop=(h == QH - 1))
            last.then_inc(s["hidden_ready"], 1)

        def turn_hn(j, n):
            pe.wait_ge(s["hn_ready"], n + 1)
            for c in range(DC):
                last = pe.transpose(banks[:, TURN, c * P:(c + 1) * P], normed[j][:, c * P:(c + 1) * P], k.ident)
            last.then_inc(s["hn_turned"], 1)

        def route(n, more):
            pe.wait_ge(s["hn_t_ready"], n + 1)
            pe.wait_ge(s["o_t_ready"], 2 * n + 1 + 2 * more)
            for c in range(DC):
                last = pe.matmul(banks[:, PROBS_T, 0:E], hn_turn[:, c, :], gate_w[:, c, :], start=(c == 0), stop=(c == DC - 1))
            last.then_inc(s["logits_ready"], 1)

        def step(j, n, i, prev, more):
            if more:
                turn_x(n + 1)
            scores(n)
            if more:
                project(n + 1)
            if prev:
                join(n - 1)
            turn_probs(n)
            if more:
                turn_q(n + 1)
            sums(j, n)
            if prev:
                turn_hn(1 - j, n - 1)
            if more:
                turn_k(n + 1)
            if prev:
                route(n - 1, 1)

        turn_x(0)
        project(0, True)
        turn_q(0)
        turn_k(0)
        in_steps(step, pe)
        join(B - 1)
        turn_hn(1, B - 1)
        route(B - 1, 0)

    def scalar(act):
        act.wait_ge(s["attend_loads"], 16 * LOADS)

        def take_x(n):
            act.wait_ge(s["xn_turned"], n + 1)
            act.copy(xn_t[:, :, :], banks[:, TURN, 0:D].rearrange("p (c s) -> p c s", c=DC)).then_inc(s["xn_t_ready"], 1)

        def round_kv(j, n):
            act.wait_ge(s["kv_scaled"], n + 1)
            for a in range(2 * KVH):
                last = act.activation(kvq[j][:, a, :], banks[:, KV, a * HD:(a + 1) * HD], ACT.Identity,
                                      bias=k.magic[:, :], scale=kv_stat[:, INV, a:a + 1])
            last.then_inc(s["kv_rounded"], 1)

        def take_q(n):
            for m in range(2):
                act.wait_ge(s["q_turned"], 2 * n + m + 1)
                act.copy(q_turn[:, 4 * m:4 * m + 4, :], banks[:, Q_T + m, :].rearrange(
                    "p (a s) -> p a s", a=4)).then_inc(s["q_t_ready"], 1)

        def take_k(n):
            act.wait_ge(s["k_turned"], n + 1)
            act.copy(k_turn[:, :, :], banks[:, KV, 0:KVH * S].rearrange("p (a s) -> p a s", a=KVH)).then_inc(
                s["k_t_ready"], 1)

        def soften(n):
            act.wait_ge(s["peaked"], n + 1)
            for h in range(QH):
                last = act.activation(probs[:, h, :], probs[:, h, :], ACT.Exp, bias=low_peak[:, h:h + 1],
                                      accum_out=total[:, h:h + 1])
            last.then_inc(s["exped"], 1)

        def take_probs(n):
            for m in range(2):
                act.wait_ge(s["probs_turned2"], 2 * n + m + 1)
                act.copy(probs_turn[:, 4 * m:4 * m + 4, :], banks[:, PROBS_T + m, :].rearrange(
                    "p (a s) -> p a s", a=4)).then_inc(s["probs_t2"], 1)

        def take_outputs(n):
            for m in range(KVH):
                act.wait_ge(s["o_summed"], 2 * n + m + 1)
                act.copy(o_turn[:, REP * m:REP * (m + 1), :], banks[:, PROBS_T + m, :].rearrange(
                    "p (a s) -> p a s", a=REP)).then_inc(s["o_t_ready"], 1)

        def take_hn(n):
            act.wait_ge(s["hn_turned"], n + 1)
            act.copy(hn_turn[:, :, :], banks[:, TURN, 0:D].rearrange("p (c s) -> p c s", c=DC)).then_inc(s["hn_t_ready"], 1)

        def take_logits(n):
            act.wait_ge(s["logits_ready"], n + 1)
            act.copy(k.logits[:, bass.ds(n, 1), :], banks[:, PROBS_T:PROBS_T + 1, 0:E]).then_inc(k.logits_read, 1)

        def step(j, n, i, prev, more):
            if more:
                take_x(n + 1)
            soften(n)
            if more:
                round_kv(1 - j, n + 1)
            take_probs(n)
            if more:
                take_q(n + 1)
            take_outputs(n)
            if prev:
                take_hn(n - 1)
            if more:
                take_k(n + 1)
            if prev:
                take_logits(n - 1)

        take_x(0)
        round_kv(0, 0)
        take_q(0)
        take_k(0)
        in_steps(step, act)
        take_hn(B - 1)
        take_logits(B - 1)

    def gpsimd(pool):
        pool.wait_ge(s["attend_loads"], 16 * LOADS)

        def rotate(n):
            pool.wait_ge(s["roped_q"], n + 1)
            pool.tensor_tensor(q_rot[:, :, :], q_rot[:, :, :], q_sin[:, :, :], ALU.add).then_inc(s["q_rot_ready"], 1)

        def scale(a, name, n):
            pool.wait_ge(s[name + "_var"], n + 1)
            pool.tensor_tensor(rms[a][:, 2:3], rms[a][:, 1:2], k.minus_half[:, 0:1], ALU.pow).then_inc(s[name + "_scale"], 1)

        def step(j, n, i, prev, more):
            pool.wait_ge(s["share_ready"], n + 1)
            pool.tensor_tensor(probs[:, :, :], probs[:, :, :], wide(share[:, :], S), ALU.mult).then_inc(s["probs_ready"], 1)
            if more:
                rotate(n + 1)
            if prev:
                scale(1, "hn", n - 1)
            if more == 2:
                scale(0, "xn", n + 2)

        scale(0, "xn", 0)
        scale(0, "xn", 1)
        rotate(0)
        in_steps(step, pool)
        scale(1, "hn", B - 1)

    def vector(dve):
        st = k.steps["dve"]
        dve.wait_ge(s["attend_loads"], 16 * LOADS)
        cos, sin = k.consts[:, C_COS:C_COS + HD], k.consts[:, C_SIN:C_SIN + HD]
        mask = k.consts[:, C_MASK:C_MASK + S]

        def mean_square(a, rows, name):
            st.did(dve.tensor_tensor_reduce(squares[a][:, :], rows, rows, 1.0, 0.0, ALU.mult, ALU.add, rms[a][:, 0:1]))
            st.wait()
            dve.tensor_scalar(rms[a][:, 1:2], rms[a][:, 0:1], 1.0 / D, EPS, ALU.mult, ALU.add).then_inc(s[name + "_var"], 1)

        def x_stats(j, n, i):
            dve.wait_ge(row_loaded[j], 16 * i + 16)
            mean_square(0, row_in[j][:, :], "xn")

        def x_norm(j, n):
            dve.wait_ge(s["xn_scale"], n + 1)
            if not (isinstance(n, int) and n == 0):
                dve.wait_ge(s["xn_turned"], n)
            dve.scalar_tensor_tensor(out=xn[:, :], in0=row_in[j][:, :], scalar=rms[0][:, 2:3], in1=gains[:, 0, :],
                                     op0=ALU.mult, op1=ALU.mult).then_inc(s["xn_ready"], 1)

        def rotate_q(n):
            q = banks[:, Q:Q + 2, :].rearrange("p m (a d) -> p (m a) d", a=4)
            dve.wait_ge(s["q_ready"], n + 1)
            if not (isinstance(n, int) and n == 0):
                dve.wait_ge(s["q_turned"], 2 * n)
            dve.tensor_tensor(q_rot[:, :, :], q, each(cos, QH), ALU.mult)
            for a, b in ((0, HALF_HD), (HALF_HD, 0)):
                last = dve.tensor_tensor(q_sin[:, :, a:a + HALF_HD], q[:, :, b:b + HALF_HD],
                                         each(sin[:, a:a + HALF_HD], QH), ALU.mult)
            last.then_inc(s["roped_q"], 1)

        def kv_stats(n):
            a = kv_stat
            kv = banks[:, KV, :].rearrange("p (g d) -> p g d", g=2 * KVH)
            dve.wait_ge(s["kv_ready"], n + 1)
            dve.tensor_reduce(a[:, MAX, :], kv, AX.X, ALU.max)
            st.did(dve.tensor_reduce(a[:, MIN, :], kv, AX.X, ALU.min))
            st.wait()
            st.did(dve.tensor_tensor(a[:, TMP, :], a[:, MAX, :], a[:, MIN, :], ALU.subtract))
            st.wait()
            st.did(dve.tensor_scalar(a[:, SCALE, :], a[:, TMP, :], 1e-5, 1.0 / LEVELS, ALU.max, ALU.mult))
            st.wait()
            dve.reciprocal(a[:, INV, :], a[:, SCALE, :]).then_inc(s["kv_scaled"], 1)
            dve.wait_ge(s["kv_scaled"], n + 1)
            st.did(dve.scalar_tensor_tensor(out=a[:, TMP, :], in0=a[:, MIN, :], scalar=-1.0, in1=a[:, INV, :],
                                            op0=ALU.mult, op1=ALU.mult))
            st.wait()
            st.did(dve.tensor_scalar(a[:, BASE, :], a[:, TMP, :], MAGIC, MAGIC, ALU.add, ALU.subtract))
            st.wait()
            st.did(dve.tensor_scalar(a[:, TMP, :], a[:, BASE, :], 0.0, LEVELS, ALU.max, ALU.min))
            st.wait()
            st.did(dve.tensor_scalar(a[:, LOW, :], a[:, TMP, :], -1.0, MAGIC, ALU.mult, ALU.add))
            st.wait()
            st.did(dve.tensor_scalar(a[:, HIGH, :], a[:, LOW, :], LEVELS, None, ALU.add))
            st.wait()

        def kv_finish(j, n):
            a, x = kv_stat, kvq[j]
            dve.wait_ge(s["kv_rounded"], n + 1)
            for g in range(2 * KVH):
                last = dve.tensor_scalar(x[:, g, :], x[:, g, :], a[:, LOW, g:g + 1], a[:, HIGH, g:g + 1], ALU.max, ALU.min)
            st.did(last)
            st.wait()
            for g in range(2 * KVH):
                last = dve.tensor_scalar(x[:, g, :], x[:, g, :], MAGIC, a[:, SCALE, g:g + 1], ALU.subtract, ALU.mult)
            st.did(last)
            st.wait()
            keys = x[:, 0:KVH, :]
            if not (isinstance(n, int) and n == 0):
                dve.wait_ge(s["k_turned"], n)
            dve.tensor_tensor(k_rot[:, :, :], keys, each(cos, KVH), ALU.mult)
            for lo, hi in ((0, HALF_HD), (HALF_HD, 0)):
                last = dve.tensor_tensor(k_sin[:, :, lo:lo + HALF_HD], keys[:, :, hi:hi + HALF_HD],
                                         each(sin[:, lo:lo + HALF_HD], KVH), ALU.mult)
            st.did(last)
            st.wait()
            dve.tensor_tensor(k_rot[:, :, :], k_rot[:, :, :], k_sin[:, :, :], ALU.add).then_inc(s["k_rot_ready"], 1)

        def mask_scores(n):
            dve.wait_ge(s["scores2"], n + 1)
            if not (isinstance(n, int) and n == 0):
                dve.wait_ge(s["probs_turned2"], 2 * n)
            dve.scalar_tensor_tensor(out=probs[:, :, :], in0=banks[:, Q:Q + 2, :].rearrange("p m (a d) -> p (m a) d", a=4),
                                     scalar=float(HD) ** -0.5, in1=each(mask, QH), op0=ALU.mult, op1=ALU.add).then_inc(s["masked"], 1)
            dve.wait_ge(s["masked"], n + 1)
            dve.tensor_reduce(low_peak[:, :], probs[:, :, :], AX.X, ALU.max, negate=True).then_inc(s["peaked"], 1)

        def shares(n):
            dve.wait_ge(s["exped"], n + 1)
            dve.reciprocal(share[:, :], total[:, :]).then_inc(s["share_ready"], 1)

        def h_stats(j, n, i):
            dve.wait_ge(s["hidden_ready"], n + 1)
            dve.wait_ge(res_loaded[j], 16 * i + 16)
            dve.wait_ge(attend_stored[j], 32 * i + 32)
            st.did(dve.tensor_tensor(hidden[j][:, :], banks[:, TURN, 0:D], row_res[j][:, :], ALU.add))
            st.wait()
            mean_square(1, hidden[j][:, :], "hn")

        def h_norm(j, n):
            dve.wait_ge(s["hn_scale"], n + 1)
            dve.scalar_tensor_tensor(out=normed[j][:, :], in0=hidden[j][:, :], scalar=rms[1][:, 2:3], in1=gains[:, 1, :],
                                     op0=ALU.mult, op1=ALU.mult).then_inc(s["hn_ready"], 1)

        def step(j, n, i, prev, more):
            mask_scores(n)
            if more:
                kv_stats(n + 1)
            shares(n)
            if more:
                rotate_q(n + 1)
                kv_finish(1 - j, n + 1)
            if prev:
                h_stats(1 - j, n - 1, i)
            if more == 2:
                x_stats(j, n + 2, i + 2 - j)
            if prev:
                h_norm(1 - j, n - 1)
            if more == 2:
                x_norm(j, n + 2)

        x_stats(0, 0, 0)
        x_norm(0, 0)
        x_stats(1, 1, 0)
        x_norm(1, 1)
        rotate_q(0)
        kv_stats(0)
        kv_finish(0, 0)
        st.done(1, st.at)
        in_steps(step, dve, st, 2 * (11 + 3))
        h_stats(1, B - 1, TURNS - 1)
        h_norm(1, B - 1)
        st.done(1, st.at)

    return sync, tensor, vector, scalar, gpsimd


def route_stage(k):
    nc, t, banks = k.nc, k.t, k.banks
    with ExitStack() as own:
        rows = k.buffer(own, "route_rows", [B, D])
        less = k.buffer(own, "less", [B, E])
        other = k.buffer(own, "other", [B, E])
        key = k.buffer(own, "key", [B, E])
        chosen = [k.buffer(own, f"chosen{m}", [B, E]) for m in range(2)]
        both = k.buffer(own, "both", [B, E])
        peak = k.buffer(own, "route_peak", [2, B])
        index = k.buffer(own, "index", [2, B])
        second = k.buffer(own, "second", [B])
        norm = k.buffer(own, "route_norm", [2, B])
        counts = k.buffer(own, "counts", [E, B])
        upto = k.buffer(own, "upto", [E, B])
        before = k.buffer(own, "before", [E, B])
        per_expert = k.buffer(own, "per_expert", [6, E])
        place = k.buffer(own, "place", [B, E])
        hit = [k.buffer(own, f"hit{m}", [B, E]) for m in range(2)]
        sums = k.buffer(own, "place_sums", [2, B])
        passed = k.buffer(own, "passed", [BLOCKS, E])
        block_sum = k.buffer(own, "block_sum", [2, BLOCKS])
    route_loads = k.semaphore("route_loads")
    second_ready = k.semaphore("second_ready")
    second_exped = k.semaphore("second_exped")
    chosen_ready = k.semaphore("chosen_ready")
    counted = k.semaphore("counted")
    places_ready = k.semaphore("places_ready")
    k.blocks_ready = k.semaphore("blocks_ready")
    scattered = k.semaphore("scattered")
    NEED, BLOCKS_E, UPTO_E, BEGIN, TOTAL, SHIFT = range(6)
    RANK, ALL = banks[:, 0, 0:B * E], banks[:, 0, B * E:2 * B * E]

    def sync(sp):
        sp.dma_start(rows[:, :, :], k.normed_d.rearrange("(b p) n -> p b n", p=P)).then_inc(route_loads, 16)
        sp.wait_ge(scattered, 16 * 2 * B)

    def tensor(pe):
        pe.wait_ge(chosen_ready, 1)
        flat = both[:, :, :].rearrange("p b e -> p (b e)")
        pe.matmul(RANK, k.consts[:, C_BEFORE:C_BEFORE + P], flat, start=True, stop=True)
        pe.matmul(ALL, k.consts[:, C_ONES:C_ONES + P], flat, start=True, stop=True).then_inc(counted, 1)

    def scalar(act):
        act.wait_ge(second_ready, 1)
        act.activation(second[:, :], peak[:, 1, :], ACT.Exp).then_inc(second_exped, 1)

    def gpsimd(pool):
        pool.wait_ge(route_loads, 16)
        pool.wait_ge(k.s_zeroed, 16)
        pool.wait_ge(places_ready, 2)
        for b in range(B):
            for m in range(2):
                pool.indirect_dma_start(
                    out=k.sorted_d, out_offset=bass.IndirectOffsetOnAxis(ap=k.places[:, m, b:b + 1], axis=0),
                    in_=rows[:, b, :], in_offset=None).then_inc(scattered, 16)

    def vector(dve):
        st = k.steps["dve"]
        iota = each(k.consts[:, C_IOTA:C_IOTA + E], B)

        def step(ins):
            st.did(ins)
            st.wait()

        def choose(m, logits):
            step(dve.tensor_reduce(peak[:, m, :], logits, AX.X, ALU.max))
            step(dve.tensor_tensor(key[:, :, :], logits, wide(peak[:, m, :], E), ALU.is_lt))
            step(dve.scalar_tensor_tensor(out=key[:, :, :], in0=key[:, :, :], scalar=float(E), in1=iota,
                                          op0=ALU.mult, op1=ALU.add))
            step(dve.tensor_reduce(index[:, m, :], key[:, :, :], AX.X, ALU.min))
            step(dve.tensor_tensor(chosen[m][:, :, :], iota, wide(index[:, m, :], E), ALU.is_equal))

        dve.wait_ge(route_loads, 16)
        dve.wait_ge(k.logits_read, B)
        step(dve.tensor_reduce(norm[:, 0, :], k.logits[:, :, :], AX.X, ALU.max))
        step(dve.tensor_tensor(less[:, :, :], k.logits[:, :, :], wide(norm[:, 0, :], E), ALU.subtract))
        choose(0, less[:, :, :])
        step(dve.scalar_tensor_tensor(out=other[:, :, :], in0=chosen[0][:, :, :], scalar=LOWEST, in1=less[:, :, :],
                                      op0=ALU.mult, op1=ALU.add))
        choose(1, other[:, :, :])
        dve.tensor_tensor(both[:, :, :], chosen[0][:, :, :], chosen[1][:, :, :], ALU.add).then_inc(chosen_ready, 1)
        dve.sem_inc(second_ready, 1)

        dve.wait_ge(second_exped, 1)
        step(dve.tensor_scalar(norm[:, 1, :], second[:, :], 1.0, None, ALU.add))
        step(dve.reciprocal(k.shares[:, 0, :], norm[:, 1, :]))
        step(dve.tensor_tensor(k.shares[:, 1, :], k.shares[:, 0, :], second[:, :], ALU.mult))

        dve.wait_ge(counted, 1)
        step(dve.tensor_copy(counts[:, :, :], ALL.rearrange("p (b e) -> p e b", b=B)))
        ones = k.consts[:, C_ONES:C_ONES + P]
        step(dve.tensor_tensor_scan(upto[:, :, :].rearrange("p e b -> p (e b)"), ones,
                                    counts[:, :, :].rearrange("p e b -> p (e b)"), 0.0, ALU.mult, ALU.add))
        step(dve.tensor_tensor(before[:, :, :], upto[:, :, :], counts[:, :, :], ALU.subtract))
        a = per_expert
        step(dve.tensor_tensor(a[:, TOTAL, :], upto[:, :, B - 1], before[:, :, 0], ALU.subtract))
        step(dve.tensor_scalar(a[:, NEED, :], a[:, TOTAL, :], 1.0 / ROWS, 0.5 - 0.5 / ROWS, ALU.mult, ALU.add))
        step(dve.tensor_scalar(a[:, BLOCKS_E, :], a[:, NEED, :], MAGIC, MAGIC, ALU.add, ALU.subtract))
        step(dve.tensor_tensor_scan(a[:, UPTO_E, :], ones[:, 0:E], a[:, BLOCKS_E, :], 0.0, ALU.mult, ALU.add))
        step(dve.tensor_tensor(a[:, BEGIN, :], a[:, UPTO_E, :], a[:, BLOCKS_E, :], ALU.subtract))
        step(dve.scalar_tensor_tensor(out=a[:, SHIFT, :], in0=a[:, BEGIN, :], scalar=float(ROWS), in1=before[:, :, 0],
                                      op0=ALU.mult, op1=ALU.subtract))
        step(dve.tensor_tensor(place[:, :, :], RANK.rearrange("p (b e) -> p b e", b=B), each(a[:, SHIFT, :], B), ALU.add))
        step(dve.tensor_tensor(place[:, :, :], place[:, :, :], before[:, :, :].rearrange("p e b -> p b e"), ALU.add))
        for m in range(2):
            step(dve.tensor_tensor(hit[m][:, :, :], place[:, :, :], chosen[m][:, :, :], ALU.mult))
            step(dve.tensor_reduce(sums[:, m, :], hit[m][:, :, :], AX.X, ALU.add))
            dve.tensor_copy(k.places[:, m, :], sums[:, m, :]).then_inc(places_ready, 1)

        step(dve.tensor_tensor(passed[:, :, :], wide(k.consts[:, C_BLOCK:C_BLOCK + BLOCKS], E), each(a[:, UPTO_E, :], BLOCKS),
                               ALU.is_ge))
        step(dve.tensor_reduce(block_sum[:, 0, :], passed[:, :, :], AX.X, ALU.add))
        step(dve.tensor_scalar(block_sum[:, 1, :], block_sum[:, 0, :], float(E - 1), None, ALU.min))
        dve.tensor_copy(k.block_expert[:, :], block_sum[:, 1, :]).then_inc(k.blocks_ready, 1)
        st.done(1, st.at)

    return sync, tensor, vector, scalar, gpsimd


def experts_stage(k):
    nc, t, banks = k.nc, k.t, k.banks
    HALVES = ROWS // P
    with ExitStack() as own:
        weights = [k.buffer(own, f"expert_w{j}", [3 * TILES, P]) for j in range(2)]
        rows = [k.buffer(own, f"expert_rows{j}", [HALVES, D]) for j in range(2)]
        rows_t = [k.buffer(own, f"expert_rows_t{j}", [DC, ROWS]) for j in range(2)]
        silu = [k.buffer(own, f"silu{a}", [ROWS]) for a in range(2)]
        up = [k.buffer(own, f"up{j}", [FC, ROWS]) for j in range(2)]
        y = [k.buffer(own, f"expert_y{j}", [HALVES, D]) for j in range(2)]
    weights_in = [k.semaphore(f"weights_in{j}") for j in range(2)]
    block_in = [k.semaphore(f"block_in{j}") for j in range(2)]
    expert_stored = [k.semaphore(f"expert_stored{j}") for j in range(2)]
    block_turned = k.semaphore("block_turned")
    rows_t_ready = k.semaphore("rows_t_ready")
    up_summed = k.semaphore("up_summed")
    silu_ready = k.semaphore("silu_ready")
    up_ready = k.semaphore("up_ready")
    y_summed = k.semaphore("y_summed")
    y_ready = k.semaphore("y_ready")
    UP, TURN, Y = 0, 2, 4
    TURNS = (BLOCKS - 1) // 2
    assert BLOCKS % 2

    def in_pipeline(emit, eng):
        with eng.Fori(0, TURNS - 1) as i:
            for j in range(2):
                emit(j, 2 * i + j, i, 2)
        emit(0, BLOCKS - 3, TURNS - 1, 2)
        emit(1, BLOCKS - 2, TURNS - 1, 1)
        emit(0, BLOCKS - 1, TURNS, 0)

    def sync(sp):
        def load(j, n):
            expert = sp.value_load(k.block_expert[0:1, bass.ds(n, 1)], min_val=0, max_val=E - 1)
            sp.dma_start(weights[j][:, :, :].rearrange("p (o a) b -> p o (a b)", o=3),
                         k.weights_d[bass.ds(3 * expert + 3, 3)].rearrange("o p n -> p o n")).then_inc(weights_in[j], 16)
            sp.dma_start(rows[j][:, :, :], k.sorted_d[bass.ds(n * ROWS, ROWS), :].rearrange(
                "(a p) d -> p a d", p=P)).then_inc(block_in[j], 16)

        def element(j, n, i, more):
            if more == 2:
                sp.wait_ge(y_summed, n + 1)
                load(j, n + 2)
            sp.wait_ge(y_ready, n + 3)
            sp.dma_start(k.expert_d[bass.ds(n * ROWS, ROWS), :].rearrange("(a p) d -> p a d", p=P),
                         y[j][:, :, :]).then_inc(expert_stored[j], 16)

        for j in range(2):
            sp.sem_inc(expert_stored[j], 16)
        sp.wait_ge(k.blocks_ready, 1)
        load(0, 0)
        load(1, 1)
        in_pipeline(element, sp)
        sp.wait_ge(expert_stored[0], 16 * (TURNS + 2))
        sp.wait_ge(expert_stored[1], 16 * (TURNS + 1))

    def tensor(pe):
        def turn(j, n, i):
            pe.wait_ge(block_in[j], 16 * i + 16)
            for c in range(DC):
                for a in range(HALVES):
                    last = pe.transpose(banks[:, TURN + j, (c * HALVES + a) * P:(c * HALVES + a + 1) * P],
                                        rows[j][:, a, c * P:(c + 1) * P], k.ident)
            last.then_inc(block_turned, 1)

        def element(j, n, i, more):
            w = weights[j]
            pe.wait_ge(weights_in[j], 16 * i + 16)
            pe.wait_ge(rows_t_ready, n + 1)
            for f in range(FC):
                g = FC * n + f
                pe.wait_ge(up_ready, g + 1)
                for m in range(2):
                    for c in range(DC):
                        last = pe.matmul(banks[:, UP + (FC * j + f) % 2, m * ROWS:(m + 1) * ROWS],
                                         w[:, m * TILES + f * DC + c, :], rows_t[j][:, c, :],
                                         start=(c == 0), stop=(c == DC - 1))
                last.then_inc(up_summed, 1)
            if more:
                turn(1 - j, n + 1, i + j)
            pe.wait_ge(y_ready, n + 1)
            for a in range(HALVES):
                for f in range(FC):
                    if a == 0:
                        pe.wait_ge(up_ready, FC * n + f + 3)
                    last = pe.matmul(banks[:, Y + j, a * D:(a + 1) * D], up[j][:, f, a * P:(a + 1) * P],
                                     w[:, 2 * TILES + DC * f:2 * TILES + DC * (f + 1), :].rearrange("p c d -> p (c d)"),
                                     start=(f == 0), stop=(f == FC - 1))
            last.then_inc(y_summed, 1)

        turn(0, 0, 0)
        in_pipeline(element, pe)

    def scalar(act):
        def take_rows(j, n):
            act.wait_ge(block_turned, n + 1)
            act.copy(rows_t[j][:, :, :].rearrange("p c s -> p (c s)"), banks[:, TURN + j, :]).then_inc(rows_t_ready, 1)

        def element(j, n, i, more):
            for f in range(FC):
                act.wait_ge(up_summed, FC * n + f + 1)
                act.activation(silu[(FC * j + f) % 2][:, :], banks[:, UP + (FC * j + f) % 2, 0:ROWS],
                               ACT.Silu).then_inc(silu_ready, 1)
            if more:
                take_rows(1 - j, n + 1)
            act.wait_ge(y_summed, n + 1)
            act.wait_ge(expert_stored[j], 16 * i + 16)
            act.copy(y[j][:, :, :].rearrange("p a d -> p (a d)"), banks[:, Y + j, :]).then_inc(y_ready, 1)

        act.sem_inc(y_ready, 2)
        take_rows(0, 0)
        in_pipeline(element, act)

    def vector(dve):
        def element(j, n, i, more):
            for f in range(FC):
                dve.wait_ge(silu_ready, FC * n + f + 1)
                dve.tensor_tensor(up[j][:, f, :], silu[(FC * j + f) % 2][:, :],
                                  banks[:, UP + (FC * j + f) % 2, ROWS:2 * ROWS], ALU.mult).then_inc(up_ready, 1)

        dve.sem_inc(up_ready, 2)
        in_pipeline(element, dve)

    def gpsimd(pool):
        pass

    return sync, tensor, vector, scalar, gpsimd


def finish_stage(k):
    nc, t = k.nc, k.t
    GROUP = 4
    N_GROUPS = B // GROUP
    with ExitStack() as own:
        taken = [k.buffer(own, f"taken{m}", [B, D]) for m in range(2)]
        h = k.buffer(own, "finish_h", [B, D])
        x = k.buffer(own, "finish_x", [B, D])
        decoded = k.buffer(own, "decoded_rows", [B, D])
        stats = k.buffer(own, "finish_stats", [GROUP, 6])
        mean = k.buffer(own, "finish_mean", [GROUP, 2])
        eps = k.buffer(own, "finish_eps", [GROUP])
        scale = k.buffer(own, "finish_scale", [GROUP])
    finish_loads = k.semaphore("finish_loads")
    gather_begin = k.semaphore("gather_begin")
    gathered = [k.semaphore(f"gathered{j}") for j in range(2)]
    finish_var = k.semaphore("finish_var")
    finish_scale = k.semaphore("finish_scale")
    finish_normed = k.semaphore("finish_normed")
    finish_stored = k.semaphore("finish_stored")

    def sync(sp):
        sp.sem_inc(gather_begin, 1)
        sp.dma_start(h[:, :, :], k.hidden_d.rearrange("(b p) n -> p b n", p=P)).then_inc(finish_loads, 16)
        sp.dma_start(x[:, :, :], k.crossed_d.rearrange("(b p) n -> p b n", p=P)).then_inc(finish_loads, 16)
        with sp.Fori(0, N_GROUPS) as g:
            sp.wait_ge(finish_normed, g + 1)
            sp.dma_start(k.out[bass.ds(g * GROUP * P, GROUP * P), :].rearrange("(b p) n -> p b n", p=P),
                         decoded[:, bass.ds(GROUP * g, GROUP), :]).then_inc(finish_stored, 16)
        sp.wait_ge(finish_stored, 16 * N_GROUPS)

    def gpsimd(pool):
        pool.wait_ge(gather_begin, 1)

        def gather(g):
            for b in range(GROUP * g, GROUP * (g + 1)):
                for m in range(2):
                    pool.indirect_dma_start(
                        out=taken[m][:, b, :], out_offset=None, in_=k.expert_d,
                        in_offset=bass.IndirectOffsetOnAxis(ap=k.places[:, m, b:b + 1], axis=0)).then_inc(gathered[g % 2], 16)

        gather(0)
        for g in range(N_GROUPS):
            if g + 1 < N_GROUPS:
                if g:
                    pool.wait_ge(gathered[(g + 1) % 2], 32 * GROUP * ((g + 1) // 2))
                gather(g + 1)
            pool.wait_ge(finish_var, g + 1)
            pool.tensor_tensor(scale[:, :], eps[:, :], k.minus_half[:, 0:GROUP], ALU.pow).then_inc(finish_scale, 1)

    def vector(dve):
        st = k.steps["dve"]
        dve.wait_ge(finish_loads, 32)
        for b in range(0, B, GROUP):
            last = dve.tensor_tensor(h[:, b:b + GROUP, :], h[:, b:b + GROUP, :], x[:, b:b + GROUP, :], ALU.add)
        st.did(last)
        st.wait()
        for g in range(N_GROUPS):
            tiles = range(GROUP * g, GROUP * (g + 1))
            dve.wait_ge(gathered[g % 2], 32 * GROUP * (g // 2 + 1))
            for m in range(2):
                for b in tiles:
                    last = dve.scalar_tensor_tensor(out=h[:, b, :], in0=taken[m][:, b, :], scalar=k.shares[:, m, b:b + 1],
                                                    in1=h[:, b, :], op0=ALU.mult, op1=ALU.add)
                st.did(last)
                st.wait()
            for a, b in enumerate(tiles):
                last = dve.bn_stats(stats[:, a, :], h[:, b, :])
            st.did(last)
            st.wait()
            for a in range(GROUP):
                last = dve.bn_aggr(mean[:, a, :], stats[:, a, :])
            st.did(last)
            st.wait()
            dve.tensor_scalar(eps[:, :], mean[:, :, 1], EPS, None, ALU.add).then_inc(finish_var, 1)
            dve.wait_ge(finish_scale, g + 1)
            for a, b in enumerate(tiles):
                last = dve.tensor_scalar(decoded[:, b, :], h[:, b, :], mean[:, a, 0:1], scale[:, a:a + 1],
                                         ALU.subtract, ALU.mult)
            last.then_inc(finish_normed, 1)
        st.done(1, st.at)

    def tensor(pe):
        pass

    def scalar(act):
        pass

    return sync, tensor, vector, scalar, gpsimd


STAGES = (prep_stage, mix_stage, cross_stage, attend_stage, route_stage, experts_stage, finish_stage)


def decoder_layer(nc, t, out):
    with ExitStack() as top:
        k = Shared(nc, t, out, top)
        stages = [stage(k) for stage in STAGES]
        s_dve = k.semaphore("dve_steps")
        block = top.enter_context(nc.Block())

        @block.sync
        def _(sp):
            sp.dma_start(k.consts[:, :], t["constants"]).then_inc(k.s_consts, 16)
            sp.wait_ge(k.s_fill, 3)
            sp.dma_start(k.sorted_d.rearrange("(a p) d -> p a d", p=P), each(k.zeros[:, :], SORTED // P)).then_inc(
                k.s_zeroed, 16)
            for sync, *_ in stages:
                sync(sp)

        @block.tensor
        def _(pe):
            pe.wait_ge(k.s_consts, 16)
            for _, tensor, *_ in stages:
                tensor(pe)

        @block.vector
        def _(dve):
            k.steps["dve"] = Steps(dve, s_dve)
            dve.memset(k.magic[:, :], MAGIC).then_inc(k.s_fill, 1)
            dve.memset(k.minus_half[:, :], -0.5).then_inc(k.s_fill, 1)
            dve.memset(k.zeros[:, :], 0.0).then_inc(k.s_fill, 1)
            dve.wait_ge(k.s_consts, 16)
            for _, _, vector, *_ in stages:
                vector(dve)

        @block.scalar
        def _(act):
            act.wait_ge(k.s_consts, 16)
            act.wait_ge(k.s_fill, 3)
            for _, _, _, scalar, _ in stages:
                scalar(act)

        @block.gpsimd
        def _(pool):
            pool.wait_ge(k.s_consts, 16)
            pool.wait_ge(k.s_fill, 3)
            for _, _, _, _, gpsimd in stages:
                gpsimd(pool)


def shape_constants():
    c = np.zeros((P, C_END), np.float32)
    i = np.arange(P)
    c[:, C_ID:C_ID + P] = np.eye(P)
    inv = np.float32(1.0) / np.float32(1000000.0) ** (np.arange(0, HD, 2, dtype=np.float32) / np.float32(HD))
    angle = (i.astype(np.float32)[:, None] * inv[None, :]).astype(np.float32)
    angle = np.concatenate([angle, angle], axis=1)
    c[:, C_COS:C_COS + HD] = np.cos(angle)
    c[:, C_SIN:C_SIN + HD] = np.sin(angle) * np.where(np.arange(HD) < HD // 2, -1, 1)
    c[:, C_MASK:C_MASK + S] = np.where(i[:, None] >= i[None, :], 0.0, MASKED)
    c[:, C_BEFORE:C_BEFORE + P] = i[:, None] < i[None, :]
    c[:, C_ONES:C_ONES + P] = 1.0
    c[:, C_HEAD:C_HEAD + HALF] = i[:, None] // XK == np.arange(HALF)[None, :]
    c[:, C_IOTA:C_IOTA + E] = np.arange(E)
    c[:, C_BLOCK:C_BLOCK + BLOCKS] = np.arange(BLOCKS)
    return c


def laid_out(x, ctx_1024, L0_attn_rkv_w, L0_attn_out_w, L0_attn_time_decay, L0_attn_time_first,
             L0_attn_time_decay_rev, L0_attn_time_first_rev, L0_xattn_Wq, L0_xattn_bq, L0_xattn_Wk, L0_xattn_bk,
             L0_xattn_Wv, L0_xattn_bv, L0_xattn_Wo, L0_xattn_bo, L0_ffn_w_q, L0_ffn_w_k, L0_ffn_w_v, L0_ffn_w_o,
             L0_ffn_g1, L0_ffn_g2, L0_ffn_w_gate, L0_ffn_w1, L0_ffn_w3, L0_ffn_w2):
    def columns(*vectors):
        return np.concatenate([v.reshape(-1, P) for v in vectors]).T

    qkv = np.concatenate([L0_ffn_w_q, L0_ffn_w_k, L0_ffn_w_v])
    tiles = [qkv.reshape(-1, P, DC, P).transpose(1, 2, 0, 3).reshape(P, -1, P),
             L0_ffn_w_o.reshape(DC, P, QH, P).transpose(1, 2, 0, 3).reshape(P, -1, P)]
    tiles.append(np.zeros((P, 3 * TILES - sum(a.shape[1] for a in tiles), P), np.float32))
    jobs = [np.concatenate(tiles, axis=1).reshape(P, 3, TILES * P).transpose(1, 0, 2)]
    for e in range(E):
        for w in (L0_ffn_w1, L0_ffn_w3):
            jobs.append(w[e].reshape(FC, P, DC * P).transpose(1, 0, 2).reshape(1, P, TILES * P))
        jobs.append(L0_ffn_w2[e].reshape(DC, P, FC, P).transpose(1, 2, 0, 3).reshape(1, P, TILES * P))
    arrays = {
        "constants": shape_constants(),
        "x": x.reshape(TOK, D),
        "x_fwd_t": x.reshape(TOK, D).T,
        "x_bwd_t": x[:, ::-1].reshape(TOK, D).T,
        "ctx_t": ctx_1024.reshape(TOK, D).T,
        "rkv_t": L0_attn_rkv_w.T,
        "out_t": L0_attn_out_w.T,
        "decay": columns(L0_attn_time_decay, L0_attn_time_decay_rev),
        "first": columns(L0_attn_time_first, L0_attn_time_first_rev),
        "wq": L0_xattn_Wq, "wk": L0_xattn_Wk, "wv": L0_xattn_Wv, "wo": L0_xattn_Wo,
        "bqk": columns(L0_xattn_bq, L0_xattn_bk),
        "rows": np.stack([L0_xattn_bv, L0_xattn_bo, L0_ffn_g1, L0_ffn_g2]).reshape(4, D),
        "gate_t": L0_ffn_w_gate.T,
        "weight_jobs": np.concatenate(jobs),
    }
    return {f"in_{n}": np.ascontiguousarray(a) for n, a in arrays.items()}


def build(nc, arrays):
    t = {n.removeprefix("in_"): nc.dram_tensor(n, a.shape, F32, kind="ExternalInput").ap() for n, a in arrays.items()}
    out = nc.dram_tensor("decoded", (TOK, D), F32, kind="ExternalOutput").ap()
    decoder_layer(nc, t, out)


def kernel(**inputs):
    import concourse.bacc as bacc
    from concourse.bass_utils import run_bass_kernel_spmd

    arrays = laid_out(**{n: np.asarray(a) for n, a in inputs.items()})
    nc = bacc.Bacc("TRN2", target_bir_lowering=False, num_devices=1)
    build(nc, arrays)
    result = run_bass_kernel_spmd(nc, [arrays], core_ids=[0])
    return result.results[0]["decoded"].reshape(B, S, D)
```

```python
from contextlib import ExitStack

import numpy as np

import concourse.bass as bass
from concourse import mybir

F32 = mybir.dt.float32
I32 = mybir.dt.int32
BF16 = mybir.dt.bfloat16
ALU = mybir.AluOpType
ACT = mybir.ActivationFunctionType
AX = mybir.AxisListType

P = 128
B, S, D = 16, 128, 256
TOK = B * S
DC = D // P
GROUPS, GB = 4, 4
GT = GB * S
UNITS = 4
XH, XK = 16, 16
HALF = 8
QH, KVH, HD = 8, 2, 128
REP = QH // KVH
E, FFN = 8, 896
FC = FFN // P
LEVELS = 15.0
TILES = 14
NUMBERS = 3 + E
WHOLES = 2 * E
ROWS = P
BLOCKS = (2 * TOK + E * (ROWS - 1)) // ROWS
JOB = TILES * P
BANKS_JOB = 4
MAGIC = 12582912.0
LOWEST = -1e38
MASKED = -1e30
EPS = 1e-5

C_ID, C_COS, C_SIN, C_MASK, C_BEFORE, C_ONES, C_HEAD = 0, 128, 256, 384, 512, 640, 768
C_IOTA, C_TOKEN, C_LANE = 776, 784, 800
C_END = 928


class Steps:

    def __init__(self, eng, sem):
        self.eng, self.sem, self.start, self.base, self.at = eng, sem, 0, 0, 0

    def did(self, ins):
        ins.then_inc(self.sem, 1)
        self.at += 1

    def wait(self):
        self.eng.wait_ge(self.sem, self.base + self.at)

    def turn(self, i, per):
        self.base, self.at = self.start + i * per, 0

    def done(self, turns, per):
        assert self.at == per, f"{self.at} steps a turn, not {per}"
        self.start += turns * per
        self.base, self.at = self.start, 0


def wide(ap, n):
    p, a = ap.shape
    return ap.rearrange("p (a o) -> p a o", o=1).to_broadcast([p, a, n])


def each(ap, n):
    p, w = ap.shape
    return ap.rearrange("p (o w) -> p o w", o=1).to_broadcast([p, n, w])



class Shared:

    def __init__(self, nc, t, out, top):
        self.nc, self.t, self.out, self.top = nc, t, out, top
        self.steps = {}

        def dram(name, shape, dt=F32):
            return nc.dram_tensor(name, shape, dt, kind="Internal").ap()

        self.numbers_d = dram("numbers_d", (NUMBERS, P, JOB))
        self.levels_d = dram("levels_d", (WHOLES, P, JOB), BF16)
        self.steps_d = dram("steps_d", (WHOLES, P, TILES))
        self.mixed_d = dram("mixed_d", (TOK, D))
        self.crossed_d = dram("crossed_d", (TOK, D))
        self.hidden_d = dram("hidden_d", (TOK + P, D))
        self.normed_d = dram("normed_d", (TOK, D))
        self.banks = top.enter_context(nc.psum_tensor("banks", [P, 8, 512], F32))
        self.consts = self.buffer(top, "consts", [C_END])
        self.ident = self.consts[:, C_ID:C_ID + P]
        self.magic = self.buffer(top, "magic", [1])
        self.minus_magic = self.buffer(top, "minus_magic", [1])
        self.minus_half = self.buffer(top, "minus_half", [4])
        self.logits = self.buffer(top, "logits", [B, E])
        self.ident16 = self.buffer(top, "ident16", [P], BF16)
        self.shares = self.buffer(top, "shares", [2, B])
        self.token_of = self.buffer(top, "token_of", [BLOCKS], I32)
        self.target_of = self.buffer(top, "target_of", [BLOCKS], I32)
        self.share_of = self.buffer(top, "share_of", [BLOCKS])
        self.block_expert = self.buffer(top, "block_expert", [BLOCKS], I32)
        self.attend_w = self.buffer(top, "attend_w", [3 * TILES, P])
        self.gate_w = self.buffer(top, "gate_w", [DC, E])
        self.gains = self.buffer(top, "gains", [2, D])
        self.row_in = [self.buffer(top, f"row_in{j}", [D]) for j in range(2)]
        self.row_res = [self.buffer(top, f"row_res{j}", [D]) for j in range(2)]
        self.row_loaded = [self.semaphore(f"row_loaded{j}") for j in range(2)]
        self.res_loaded = [self.semaphore(f"res_loaded{j}") for j in range(2)]
        self.attend_loads = self.semaphore("attend_loads")
        self.cross_inputs = ExitStack()
        self.cross_w = [self.buffer(self.cross_inputs, n, [DC, D]) for n in ("w_q", "w_k", "w_v", "w_o")]
        self.bqk = self.buffer(self.cross_inputs, "bqk", [2 * DC])
        self.bias_rows = self.buffer(self.cross_inputs, "bias_rows", [2, D])
        self.x_in = [self.buffer(self.cross_inputs, f"x_in{j}", [D]) for j in range(2)]
        self.ctx_t = [self.buffer(self.cross_inputs, f"ctx_t{j}", [DC, S]) for j in range(2)]
        self.mixed = self.buffer(self.cross_inputs, "mixed", [GB, D])
        self.whole_raw = [self.buffer(self.cross_inputs, f"whole_raw{j}", [TILES, P]) for j in range(2)]
        self.whole_in = [self.semaphore(f"whole_in{j}") for j in range(2)]
        self.cross_loads = self.semaphore("cross_loads")
        self.rows_in = [self.semaphore(f"rows_in{j}") for j in range(2)]
        self.mix_inputs = ExitStack()
        self.x_turned = [self.buffer(self.mix_inputs, f"x_turned{d}", [DC, TOK]) for d in range(2)]
        self.w_rkv = self.buffer(self.mix_inputs, "w_rkv", [DC, 6 * D])
        self.w_out = self.buffer(self.mix_inputs, "w_out", [UNITS, D])
        self.decay = self.buffer(self.mix_inputs, "decay", [UNITS])
        self.first = self.buffer(self.mix_inputs, "first", [UNITS])
        self.x_group = self.buffer(self.mix_inputs, "x_group", [GB, D])
        self.mix_loads = self.semaphore("mix_loads")
        self.group_in = self.semaphore("group_in")
        self.begun = self.semaphore("begun")
        self.begins = {stage: n + 1 for n, stage in enumerate(("mix", "cross", "attend", "route"))}
        self.s_consts = self.semaphore("s_consts")
        self.s_fill = self.semaphore("s_fill")
        self.s_held = self.semaphore("s_held")

    def semaphore(self, name):
        return self.top.enter_context(self.nc.semaphore(name))

    def buffer(self, stack, name, shape, dt=F32):
        return stack.enter_context(self.nc.sbuf_tensor(name, [P] + shape, dt))

    def begin(self, sp, stage):
        sp.sem_inc(self.begun, 1)

    def load_mix_inputs(self, sp):
        t = self.t
        for src, dst in ((t["rkv_t"], self.w_rkv), (t["x_fwd_t"], self.x_turned[0]), (t["x_bwd_t"], self.x_turned[1]),
                         (t["out_t"], self.w_out)):
            sp.dma_start(dst[:, :, :], src.rearrange("(c p) n -> p c n", p=P)).then_inc(self.mix_loads, 16)

        sp.dma_start(self.decay[:, :], t["decay"]).then_inc(self.mix_loads, 16)
        sp.dma_start(self.first[:, :], t["first"]).then_inc(self.mix_loads, 16)
        self.load_group(sp, 0)

    def load_group(self, sp, g):
        sp.dma_start(self.x_group[:, :, :], self.t["x"][bass.ds(g * GT, GT), :].rearrange(
            "(b p) n -> p b n", p=P)).then_inc(self.group_in, 16)

    def load_cross_weights(self, sp):
        t = self.t
        for n, dst in zip(("wq", "wk", "wv", "wo"), self.cross_w):
            sp.dma_start(dst[:, :, :], t[n].rearrange("(c p) n -> p c n", p=P)).then_inc(self.cross_loads, 16)
        sp.dma_start(self.bqk[:, :], t["bqk"]).then_inc(self.cross_loads, 16)
        for m in range(2):
            sp.dma_start(self.bias_rows[:, m, :], t["rows"][m:m + 1, :].to_broadcast([P, D])).then_inc(self.cross_loads, 16)

    def load_cross_rows(self, sp, j, n):
        sp.dma_start(self.x_in[j][:, :], self.mixed_d[bass.ds(n * S, S), :]).then_inc(self.rows_in[j], 16)
        sp.dma_start(self.ctx_t[j][:, :, :], self.t["ctx_t"].rearrange("(c p) n -> p c n", p=P)[
            :, :, bass.ds(n * S, S)]).then_inc(self.rows_in[j], 16)

    def load_whole(self, sp, j, n):
        sp.dma_start(self.whole_raw[j][:, :, :], self.t["weight_jobs"][bass.ds(NUMBERS + n, 1)].rearrange(
            "o p (a b) -> (o p) a b", a=TILES)).then_inc(self.whole_in[j], 16)

    def load_attend_rows(self, sp, dst, sem, n):
        sp.dma_start(dst[:, :], self.crossed_d[bass.ds(n * S, S), :]).then_inc(sem, 16)

    def load_attend_weights(self, sp):
        t = self.t
        for m in range(3):
            sp.dma_start(self.attend_w[:, TILES * m:TILES * (m + 1), :],
                         self.numbers_d[m].rearrange("p (a b) -> p a b", a=TILES)).then_inc(self.attend_loads, 16)
        sp.dma_start(self.gate_w[:, :, :], t["gate_t"].rearrange("(c p) e -> p c e", p=P)).then_inc(self.attend_loads, 16)
        for m in range(2):
            sp.dma_start(self.gains[:, m, :], t["rows"][2 + m:3 + m, :].to_broadcast([P, D])).then_inc(self.attend_loads, 16)


MAX, MIN, SCALE, INV, BASE, LOW, HIGH, TMP = range(8)


def group_steps(dve, st, a, groups):
    def step(ins):
        st.did(ins)
        st.wait()

    dve.tensor_reduce(a[:, MAX, :], groups, AX.X, ALU.max)
    step(dve.tensor_reduce(a[:, MIN, :], groups, AX.X, ALU.min))
    step(dve.tensor_tensor(a[:, TMP, :], a[:, MAX, :], a[:, MIN, :], ALU.subtract))
    step(dve.tensor_scalar(a[:, SCALE, :], a[:, TMP, :], 1e-5, 1.0 / LEVELS, ALU.max, ALU.mult))
    step(dve.reciprocal(a[:, INV, :], a[:, SCALE, :]))
    step(dve.scalar_tensor_tensor(out=a[:, TMP, :], in0=a[:, MIN, :], scalar=-1.0, in1=a[:, INV, :],
                                  op0=ALU.mult, op1=ALU.mult))
    step(dve.tensor_scalar(a[:, BASE, :], a[:, TMP, :], MAGIC, MAGIC, ALU.add, ALU.subtract))
    step(dve.tensor_scalar(a[:, TMP, :], a[:, BASE, :], 0.0, LEVELS, ALU.max, ALU.min))
    step(dve.tensor_scalar(a[:, LOW, :], a[:, TMP, :], -1.0, MAGIC, ALU.mult, ALU.add))
    return dve.tensor_scalar(a[:, HIGH, :], a[:, LOW, :], LEVELS, None, ALU.add)


def prep_stage(k):
    nc, t, banks = k.nc, k.t, k.banks
    with ExitStack() as own:
        raw = [k.buffer(own, f"raw{j}", [TILES, P]) for j in range(3)]
        level = [k.buffer(own, f"level{j}", [TILES, P]) for j in range(3)]
        turned = [k.buffer(own, f"turned{j}", [TILES, P]) for j in range(3)]
        stat = [k.buffer(own, f"stat{j}", [8, TILES]) for j in range(3)]
    raw_in = [k.semaphore(f"raw_in{j}") for j in range(3)]
    stored = [k.semaphore(f"stored{j}") for j in range(3)]
    scale_ready = k.semaphore("scale_ready")
    rounded = k.semaphore("rounded")
    clipped = k.semaphore("clipped")
    pool_clipped = k.semaphore("pool_clipped")
    tiles_turned = k.semaphore("tiles_turned")
    k.bank_read = bank_read = k.semaphore("bank_read")
    dequantised = k.semaphore("dequantised")
    TURNS = NUMBERS // 3 - 1
    DVE_TILES = 10

    def in_pipeline(emit, eng, st=None, per=None):
        with eng.Fori(0, TURNS) as i:
            if st:
                st.turn(i, per)
            for j in range(3):
                emit(j, 3 * i + j, i, 3)
        if st:
            st.done(TURNS, per)
        for n in range(3 * TURNS, NUMBERS):
            emit(n % 3, n, n // 3, NUMBERS - 1 - n)

    def sync(sp):
        def load(j, n):
            sp.dma_start(raw[j][:, :, :], t["weight_jobs"][bass.ds(n, 1)].rearrange(
                "o p (a b) -> (o p) a b", a=TILES)).then_inc(raw_in[j], 16)

        def store(j, n):
            sp.wait_ge(bank_read, (n + 2) * BANKS_JOB)
            sp.dma_start(k.numbers_d[bass.ds(n, 1)].rearrange("o p (a b) -> (o p) a b", a=TILES),
                         turned[j][:, :, :]).then_inc(stored[j], 16)

        def element(j, n, more=True, begin=False):
            if more:
                sp.wait_ge(rounded, n + 1)
                load(j, n + 3)
            if not begin:
                store((j + 1) % 3, n - 2)

        for j in range(3):
            load(j, j)
            sp.sem_inc(stored[j], 16)
        for n in range(2):
            element(n, n, begin=True)
        k.load_mix_inputs(sp)
        k.load_cross_weights(sp)
        with sp.Fori(0, TURNS) as i:
            for d in range(3):
                element((2 + d) % 3, 3 * i + 2 + d)
        for n in range(3 * TURNS + 2, NUMBERS):
            element(n % 3, n, more=False)
        for n in range(NUMBERS - 2, NUMBERS):
            store(n % 3, n)
        for j in range(3):
            sp.wait_ge(stored[j], 16 * (1 + len(range(j, NUMBERS, 3))))
        sp.wait_ge(k.s_consts, 32)

    def vector(dve):
        st = k.steps["dve"]

        def steps_of(j, n, i):
            dve.wait_ge(raw_in[j], 16 * i + 16)
            dve.wait_ge(dequantised, n + 1)
            group_steps(dve, st, stat[j], raw[j][:, :, :]).then_inc(scale_ready, 1)

        def element(j, n, i, more):
            if more:
                steps_of((j + 1) % 3, n + 1, i + (j + 1) // 3)
            dve.wait_ge(rounded, n + 1)
            for a in range(DVE_TILES):
                last = dve.tensor_scalar(level[j][:, a, :], level[j][:, a, :], stat[j][:, LOW, a:a + 1],
                                         stat[j][:, HIGH, a:a + 1], ALU.max, ALU.min)
            last.then_inc(clipped, 1)

        dve.tensor_copy(k.ident16[:, :], k.ident).then_inc(k.s_fill, 1)
        steps_of(0, 0, 0)
        st.done(1, 8)
        in_pipeline(element, dve, st, 24)
        st.done(1, st.at)

    def scalar(act):
        def round_levels(j, n):
            act.wait_ge(scale_ready, n + 1)
            for a in range(TILES):
                last = act.activation(level[j][:, a, :], raw[j][:, a, :], ACT.Identity, bias=k.magic[:, :],
                                      scale=stat[j][:, INV, a:a + 1])
            last.then_inc(rounded, 1)

        def take_tiles(j, n, i):
            act.wait_ge(stored[j], 16 * i + 16)
            for b in range(BANKS_JOB):
                tiles = min(4, TILES - 4 * b)
                act.wait_ge(tiles_turned, n * BANKS_JOB + b + 1)
                act.copy(turned[j][:, 4 * b:4 * b + tiles, :],
                         banks[:, 4 * (j % 2) + b, 0:tiles * P].rearrange("p (a b) -> p a b", a=tiles)).then_inc(bank_read, 1)

        def element(j, n, i, more):
            if more > 1:
                round_levels((j + 2) % 3, n + 2)
            take_tiles(j, n, i)

        round_levels(0, 0)
        round_levels(1, 1)
        in_pipeline(element, act)

    def gpsimd(pool):
        def element(j, n, i, more):
            pool.wait_ge(rounded, n + 1)
            pool.sem_inc(k.s_held, 1)
            for a in range(DVE_TILES, TILES):
                last = pool.tensor_scalar(level[j][:, a, :], level[j][:, a, :], stat[j][:, LOW, a:a + 1],
                                          stat[j][:, HIGH, a:a + 1], ALU.max, ALU.min)
            last.then_inc(pool_clipped, 1)
            pool.wait_ge(clipped, n + 1)
            pool.wait_ge(pool_clipped, n + 1)
            pool.sem_inc(k.s_held, 1)
            for a in range(TILES):
                last = pool.tensor_scalar(level[j][:, a, :], level[j][:, a, :], -MAGIC,
                                          stat[j][:, SCALE, a:a + 1], ALU.add, ALU.mult)
            last.then_inc(dequantised, 1)

        pool.sem_inc(dequantised, 3)
        in_pipeline(element, pool)

    def tensor(pe):
        def element(j, n, i, more):
            pe.wait_ge(dequantised, n + 4)
            for b in range(BANKS_JOB):
                if j == 0:
                    pe.wait_ge(bank_read, n * BANKS_JOB + b + 1)
                if j == 2:
                    pe.wait_ge(bank_read, (n - 1) * BANKS_JOB + b + 1)
                for a in range(min(4, TILES - 4 * b)):
                    last = pe.transpose(banks[:, 4 * (j % 2) + b, a * P:(a + 1) * P], level[j][:, 4 * b + a, :], k.ident)
                last.then_inc(tiles_turned, 1)

        pe.sem_inc(bank_read, BANKS_JOB)
        in_pipeline(element, pe)

    return sync, tensor, vector, scalar, gpsimd


def mix_stage(k):
    nc, t, banks = k.nc, k.t, k.banks
    x_turned, w_rkv, w_out = k.x_turned, k.w_rkv, k.w_out
    decay, first, x_group, group_in = k.decay, k.first, k.x_group, k.group_in
    LOADS = 6
    with ExitStack() as own:
        step_decay = k.buffer(own, "step_decay", [UNITS])
        top = [k.buffer(own, f"top{p}", [GB, S + 1]) for p in range(2)]
        weight = [k.buffer(own, f"weight{u}", [4, GT]) for u in range(UNITS)]
        gate = [k.buffer(own, f"gate{u}", [GT]) for u in range(UNITS)]
        values = [k.buffer(own, f"values{p}", [GT]) for p in range(2)]
        new_value = [k.buffer(own, f"new_value{p}", [2, GT]) for p in range(2)]
        carry = [k.buffer(own, f"carry{p}", [2, GT + 1]) for p in range(2)]
        sums = [k.buffer(own, f"mix_sums{p}", [2, GT]) for p in range(2)]
        y = k.buffer(own, "y", [UNITS, GB, S])
        ln_stat = k.buffer(own, "ln_stat", [GB, 6])
        ln_mean = k.buffer(own, "ln_mean", [GB, 2])
        ln_eps = k.buffer(own, "ln_eps", [GB])
        ln_scale = k.buffer(own, "ln_scale", [GB])
    k.mix_inputs.close()
    decay_ready = k.semaphore("decay_ready")
    rkv_ready = k.semaphore("rkv_ready")
    vr_ready = k.semaphore("vr_ready")
    gaps_ready = k.semaphore("gaps_ready")
    weights_ready = k.semaphore("weights_ready")
    new_ready = k.semaphore("new_ready")
    scans_ready = k.semaphore("scans_ready")
    sums_ready = k.semaphore("sums_ready")
    unit_done = k.semaphore("unit_done")
    unit_joined = k.semaphore("unit_joined")
    mix_var = k.semaphore("mix_var")
    mix_scale = k.semaphore("mix_scale")
    mix_normed = k.semaphore("mix_normed")
    mix_stored = k.semaphore("mix_stored")
    N = GROUPS * UNITS
    rows_out = banks[:, 6:8, :].rearrange("p m (b d) -> p (m b) d", b=2)
    FROM_PAST, FROM_NEW, OLD, NOW = range(4)
    EDGES, INNER = slice(0, 4, 3), slice(1, 3)

    def in_groups(emit, eng, st=None, per=None):
        for u in range(UNITS):
            emit(u, u, 0, True, False)
        if st:
            st.done(1, st.at)
        with eng.Fori(0, GROUPS - 2) as i:
            if st:
                st.turn(i, per)
            for u in range(UNITS):
                emit(u, UNITS * i + UNITS + u, i + 1, False, False)
        if st:
            st.done(GROUPS - 2, per)
        for u in range(UNITS):
            emit(u, N - UNITS + u, GROUPS - 1, False, True)

    def sync(sp):
        def element(g, more):
            if more:
                sp.wait_ge(mix_var, g + 2)
                k.load_group(sp, g + 1)
            sp.wait_ge(mix_normed, g + 2)
            sp.dma_start(k.mixed_d[bass.ds(g * GT, GT), :].rearrange("(b p) n -> p b n", p=P),
                         k.mixed[:, :, :]).then_inc(mix_stored, 16)

        k.begin(sp, "mix")
        sp.sem_inc(mix_stored, 16)
        k.load_attend_weights(sp)
        with sp.Fori(0, GROUPS - 1) as g:
            element(g, True)
        sp.wait_ge(mix_stored, 32)
        for j in range(2):
            k.load_cross_rows(sp, j, j)
            k.load_whole(sp, j, j)
        element(GROUPS - 1, False)
        k.begin(sp, "cross")
        sp.wait_ge(mix_stored, 16 * GROUPS + 16)

    def tensor(pe):
        pe.wait_ge(k.bank_read, BANKS_JOB * (NUMBERS + 1))
        pe.wait_ge(k.mix_loads, 16 * LOADS)

        def project(g, u, n, wait=True):
            d, c = u // DC, u % DC
            if wait:
                pe.wait_ge(vr_ready, n - 1)
                pe.wait_ge(gaps_ready, n - 1)
            for m in range(3):
                for kc in range(DC):
                    col = (3 * d + m) * D + c * P
                    last = pe.matmul(banks[:, 3 * (u % 2) + m, :], w_rkv[:, kc, col:col + P],
                                     x_turned[d][:, kc, bass.ds(g * GT, GT)], start=(kc == 0), stop=(kc == DC - 1))
            last.then_inc(rkv_ready, 1)

        def copy_rows(g):
            pe.wait_ge(group_in, 16 * g + 16)
            pe.wait_ge(mix_normed, g + 1)
            for m in range(2):
                pe.matmul(banks[:, 6 + m, :], k.ident, x_group[:, 2 * m:2 * m + 2, :].rearrange("p b d -> p (b d)"),
                          start=True, stop=False)

        def project_out(u, n):
            pe.wait_ge(unit_done, n + 1 + UNITS)
            for b in range(GB):
                last = pe.matmul(banks[:, 6 + b // 2, (b % 2) * D:(b % 2 + 1) * D], y[:, u, b, :],
                                 w_out[:, u, :], start=False, stop=(u == UNITS - 1 and b % 2 == 1))
            last.then_inc(unit_joined, 1)

        def step(u, n, g, is_first, is_last):
            if u < 2 or not is_last:
                project(g + (u + 2) // UNITS, (u + 2) % UNITS, n + 2)
            if u == 1 and not is_first:
                copy_rows(g - 1)
                for out in (0, 1):
                    project_out(out, n - 5 + out)
            if u == 2 and not is_first:
                for out in (2, 3):
                    project_out(out, n - 6 + out)

        project(0, 0, 0, False)
        project(0, 1, 1, False)
        in_groups(step, pe)
        copy_rows(GROUPS - 1)
        for u in range(UNITS):
            project_out(u, N - UNITS + u)

    def scalar(act):
        st = k.steps["act"]

        def begin(u, n):
            p = u % 2
            act.wait_ge(rkv_ready, n + 1)
            act.wait_ge(unit_done, n + 1)
            act.activation(gate[u][:, :], banks[:, 3 * p, :], ACT.Exp, scale=-1.0)
            act.wait_ge(new_ready, 2 * n + 2)
            act.copy(values[p][:, :], banks[:, 3 * p + 2, :]).then_inc(vr_ready, 1)
            act.wait_ge(gaps_ready, n + 1)
            w = weight[u]
            st.did(act.activation(w[:, INNER, :], w[:, EDGES, :], ACT.Relu))
            st.wait()
            st.did(act.activation(w[:, EDGES, :], w[:, EDGES, :], ACT.Relu, scale=-1.0))
            st.wait()
            act.activation(w[:, :, :], w[:, :, :], ACT.Exp, scale=-1.0).then_inc(weights_ready, 1)

        def step(u, n, g, is_first, is_last):
            if u < 2 or not is_last:
                begin((u + 2) % UNITS, n + 2)

        act.wait_ge(k.begun, k.begins["mix"])
        act.wait_ge(k.mix_loads, 16 * LOADS)
        act.activation(step_decay[:, :], decay[:, :], ACT.Exp).then_inc(decay_ready, 1)
        begin(0, 0)
        begin(1, 1)
        st.done(1, 4)
        in_groups(step, act, st, 2 * UNITS)
        st.done(1, st.at)

    def gpsimd(pool):
        st = k.steps["pool"]

        def new_parts(u, n):
            p = u % 2
            pool.wait_ge(weights_ready, n + 1)
            pool.wait_ge(sums_ready, n + 3)
            pool.tensor_tensor(new_value[p][:, 0, :], weight[u][:, FROM_NEW, :], values[p][:, :],
                               ALU.mult).then_inc(new_ready, 1)
            pool.tensor_tensor(new_value[p][:, 1, :], weight[u][:, NOW, :], values[p][:, :],
                               ALU.mult).then_inc(new_ready, 1)

        def add_old(u, n):
            p = u % 2
            pool.wait_ge(scans_ready, n + 1)
            pool.wait_ge(unit_done, n + 3)
            pool.sem_inc(k.s_held, 1)
            for m in range(2):
                last = pool.tensor_tensor(sums[p][:, m, :], weight[u][:, OLD, :], carry[p][:, m, 0:GT], ALU.mult)
            st.did(last)
            st.wait()
            pool.tensor_tensor(sums[p][:, 1, :], sums[p][:, 1, :], weight[u][:, NOW, :], ALU.add)
            pool.tensor_tensor(sums[p][:, 0, :], sums[p][:, 0, :], new_value[p][:, 1, :], ALU.add).then_inc(sums_ready, 1)

        def scale(g):
            pool.wait_ge(mix_var, g + 2)
            pool.tensor_tensor(ln_scale[:, :], ln_eps[:, :], k.minus_half[:, 0:GB], ALU.pow).then_inc(mix_scale, 1)

        def step(u, n, g, is_first, is_last):
            if u < 3 or not is_last:
                new_parts((u + 1) % UNITS, n + 1)
            add_old(u, n)
            if u == 2 and not is_first:
                scale(g - 1)

        pool.wait_ge(k.begun, k.begins["mix"])
        pool.wait_ge(k.mix_loads, 16 * LOADS)
        pool.sem_inc(sums_ready, 4)
        pool.sem_inc(new_ready, 4)
        new_parts(0, 0)
        in_groups(step, pool, st, UNITS)
        scale(GROUPS - 1)
        st.done(1, st.at)

    def vector(dve):
        st = k.steps["dve"]

        def gaps(u, n):
            p = u % 2
            dve.wait_ge(rkv_ready, n + 1)
            key = banks[:, 3 * p + 1, :]
            for b in range(GB):
                last = dve.tensor_tensor_scan(top[p][:, b, 1:S + 1], step_decay[:, u:u + 1].to_broadcast([P, S]),
                                              key[:, b * S:(b + 1) * S], LOWEST, ALU.add, ALU.max)
            st.did(last)
            st.wait()
            dve.wait_ge(sums_ready, n + 1)
            before = top[p][:, :, 0:S]
            keys = key.rearrange("p (b s) -> p b s", b=GB)
            past, now = (weight[u][:, m, :].rearrange("p (b s) -> p b s", b=GB) for m in (FROM_PAST, NOW))
            dve.scalar_tensor_tensor(out=past, in0=before, scalar=step_decay[:, u:u + 1], in1=keys,
                                     op0=ALU.add, op1=ALU.subtract)
            dve.scalar_tensor_tensor(out=now, in0=keys, scalar=first[:, u:u + 1], in1=before,
                                     op0=ALU.add, op1=ALU.subtract).then_inc(gaps_ready, 1)

        def scans(u, n):
            p = u % 2
            dve.wait_ge(weights_ready, n + 1)
            dve.tensor_tensor_scan(carry[p][:, 1, 1:GT + 1], weight[u][:, FROM_PAST, :], weight[u][:, FROM_NEW, :],
                                   0.0, ALU.mult, ALU.add)
            dve.wait_ge(new_ready, 2 * n + 5)
            dve.tensor_tensor_scan(carry[p][:, 0, 1:GT + 1], weight[u][:, FROM_PAST, :], new_value[p][:, 0, :],
                                   0.0, ALU.mult, ALU.add).then_inc(scans_ready, 1)

        def finish(u, n):
            p = u % 2
            dve.wait_ge(sums_ready, n + 5)
            st.did(dve.scalar_tensor_tensor(out=gate[u][:, :], in0=gate[u][:, :], scalar=1.0, in1=sums[p][:, 1, :],
                                            op0=ALU.add, op1=ALU.mult))
            st.wait()
            st.did(dve.reciprocal(sums[p][:, 1, :], gate[u][:, :]))
            st.wait()
            num, rec = (sums[p][:, m, :].rearrange("p (b s) -> p b s", b=GB) for m in range(2))
            to = y[:, u, :, :] if u < DC else y[:, u, :, ::-1]
            dve.tensor_tensor(to, num, rec, ALU.mult).then_inc(unit_done, 1)

        def norm(g):
            dve.wait_ge(unit_joined, UNITS * g + UNITS)
            dve.sem_inc(k.s_held, 1)
            for b in range(GB):
                last = dve.bn_stats(ln_stat[:, b, :], rows_out[:, b, :])
            st.did(last)
            st.wait()
            dve.sem_inc(k.s_held, 1)
            for b in range(GB):
                last = dve.bn_aggr(ln_mean[:, b, :], ln_stat[:, b, :])
            st.did(last)
            st.wait()
            dve.tensor_scalar(ln_eps[:, :], ln_mean[:, :, 1], EPS, None, ALU.add).then_inc(mix_var, 1)

        def norm_rows(g):
            dve.wait_ge(mix_scale, g + 1)
            dve.wait_ge(mix_stored, 16 * g + 16)
            for b in range(GB):
                last = dve.tensor_scalar(k.mixed[:, b, :], rows_out[:, b, :], ln_mean[:, b, 0:1], ln_scale[:, b:b + 1],
                                         ALU.subtract, ALU.mult)
            last.then_inc(mix_normed, 1)

        def step(u, n, g, is_first, is_last):
            scans(u, n)
            if u < 2 or not is_last:
                gaps((u + 2) % UNITS, n + 2)
            if u == 3 and not is_first:
                norm_rows(g - 1)
            if u and not is_first:
                dve.wait_ge(unit_joined, n - UNITS)
            if u or not is_first:
                finish((u - 1) % UNITS, n - 1)
            if u == 2 and not is_first:
                norm(g - 1)

        dve.wait_ge(k.begun, k.begins["mix"])
        dve.wait_ge(k.mix_loads, 16 * LOADS)
        for p in range(2):
            dve.memset(top[p][:, :, 0:1], LOWEST)
            st.did(dve.memset(carry[p][:, :, 0:1], 0.0))
        dve.sem_inc(unit_done, 4)
        dve.sem_inc(mix_var, 1)
        dve.sem_inc(mix_normed, 1)
        dve.wait_ge(decay_ready, 1)
        st.did(dve.tensor_scalar(step_decay[:, :], step_decay[:, :], -1.0, None, ALU.mult))
        st.wait()
        gaps(0, 0)
        gaps(1, 1)
        st.done(1, st.at)
        in_groups(step, dve, st, 3 * UNITS + 2)
        finish(UNITS - 1, N - 1)
        norm(GROUPS - 1)
        norm_rows(GROUPS - 1)
        st.done(1, st.at)

    return sync, tensor, vector, scalar, gpsimd


def norm_stats(k, dve, st, stats, mean, eps, rows):
    st.did(dve.bn_stats(stats, rows))
    st.wait()
    dve.sem_inc(k.s_held, 1)
    st.did(dve.bn_aggr(mean, stats))
    st.wait()
    return dve.tensor_scalar(eps, mean[:, 1:2], EPS, None, ALU.add)


def cross_stage(k):
    nc, t, banks = k.nc, k.t, k.banks
    (wq, wk, wv, wo), bqk, bias_rows, x_in, ctx_t = k.cross_w, k.bqk, k.bias_rows, k.x_in, k.ctx_t
    rows_in = k.rows_in
    with ExitStack() as own:
        level = [k.buffer(own, f"whole_level{j}", [TILES, P]) for j in range(2)]
        whole = [k.buffer(own, f"whole{j}", [TILES, P], BF16) for j in range(2)]
        whole_t = [k.buffer(own, f"whole_t{j}", [TILES, P], BF16) for j in range(2)]
        stat = [k.buffer(own, f"whole_stat{j}", [8, TILES]) for j in range(2)]
        x_t = [k.buffer(own, f"x_t{j}", [DC, S]) for j in range(2)]
        q_t = [k.buffer(own, f"q_t{j}", [DC, S]) for j in range(2)]
        k_t = [k.buffer(own, f"k_t{j}", [DC, S]) for j in range(2)]
        spread = [k.buffer(own, f"spread{h}", [HALF, S]) for h in range(2)]
        v_ones = [k.buffer(own, f"v_ones{j}", [XH, XK + 1]) for j in range(2)]
        x_bias = [k.buffer(own, f"x_bias{j}", [D]) for j in range(2)]
        peak = [k.buffer(own, f"peak{h}", [HALF]) for h in range(2)]
        probs = [k.buffer(own, f"probs{h}", [HALF, S]) for h in range(2)]
        probs_t = [k.buffer(own, f"probs_t{h}", [HALF, S]) for h in range(2)]
        total = k.buffer(own, "total", [XH])
        heads = [k.buffer(own, f"heads{j}", [XH, XK]) for j in range(2)]
        heads_t = [k.buffer(own, f"heads_t{j}", [DC, S]) for j in range(2)]
        joined = [k.buffer(own, f"joined{j}", [D]) for j in range(2)]
        ln = [k.buffer(own, f"cross_ln{j}", [12]) for j in range(2)]
        crossed = [k.buffer(own, f"crossed{j}", [D]) for j in range(2)]
    k.cross_inputs.close()
    raw, raw_in = k.whole_raw, k.whole_in
    scale_ready = k.semaphore("whole_scale_ready")
    rounded = k.semaphore("whole_rounded")
    clipped = k.semaphore("whole_clipped")
    pool_clipped = k.semaphore("whole_pool_clipped")
    whole_ready = k.semaphore("whole_ready")
    whole_turned = k.semaphore("whole_turned")
    whole_read = k.semaphore("whole_read")
    whole_stored = [k.semaphore(f"whole_stored{j}") for j in range(2)]
    steps_stored = [k.semaphore(f"whole_steps_stored{j}") for j in range(2)]
    assert WHOLES == B
    DVE_TILES = 7
    ROUNDS = 4
    ROUND_PARTS = (range(0, 2), range(2, 8), range(8, TILES))
    x_turned = k.semaphore("cross_x_turned")
    x_t_ready = k.semaphore("x_t_ready")
    qk_ready = k.semaphore("qk_ready")
    qk_read = k.semaphore("qk_read")
    v_ready = k.semaphore("v_ready")
    v_read = k.semaphore("v_read")
    spread_ready = k.semaphore("spread_ready")
    bias_added = k.semaphore("bias_added")
    scores_ready = k.semaphore("scores_ready")
    scores_read = k.semaphore("scores_read")
    exp_ready = k.semaphore("exp_ready")
    probs_turned = k.semaphore("probs_turned")
    probs_t_ready = k.semaphore("probs_t_ready")
    heads_summed = k.semaphore("heads_summed")
    heads_ready = k.semaphore("heads_ready")
    heads_turned = k.semaphore("heads_turned")
    heads_t_ready = k.semaphore("heads_t_ready")
    joined_ready = k.semaphore("joined_ready")
    cross_var = k.semaphore("cross_var")
    cross_scale = k.semaphore("cross_scale")
    cross_normed = k.semaphore("cross_normed")
    k.cross_stored = [k.semaphore(f"cross_stored{j}") for j in range(2)]
    LOADS = 7
    TURNS = B // 2
    TURN, QK, V, SCORES, PROBS_T, HEADS = 0, 1, 2, 3, 5, 7

    joined_read = k.semaphore("joined_read")

    def in_steps(emit, eng, st=None, per=None):
        emit(0, 0, -1, False, 2)
        if st:
            st.done(1, st.at)
        with eng.Fori(0, TURNS - 2) as i:
            if st:
                st.turn(i, per)
            for j in (1, 0):
                emit(j, 2 * i + 2 - j, i, True, 2)
        if st:
            st.done(TURNS - 2, per)
        for j, n, more in ((1, B - 3, 2), (0, B - 2, 1), (1, B - 1, 0)):
            emit(j, n, (n - 1) // 2, True, more)

    def sync(sp):
        def store(j, n):
            sp.wait_ge(cross_normed, n + 1)
            sp.dma_start(k.crossed_d[bass.ds(n * S, S), :], crossed[j][:, :]).then_inc(k.cross_stored[j], 16)

        def store_steps(j, n):
            sp.wait_ge(scale_ready, n + 1)
            sp.dma_start(k.steps_d[bass.ds(n, 1)].rearrange("o p a -> (o p) a"), stat[j][:, SCALE, :]).then_inc(
                steps_stored[j], 16)

        def store_whole(j, n):
            sp.wait_ge(whole_read, ROUNDS * n + ROUNDS)
            sp.dma_start(k.levels_d[bass.ds(n, 1)].rearrange("o p (a b) -> (o p) a b", a=TILES),
                         whole_t[j][:, :, :]).then_inc(whole_stored[j], 16)

        def step(j, n, i, prev, more):
            if more == 2:
                sp.wait_ge(rounded, n + 1)
                k.load_whole(sp, j, n + 2)
                sp.wait_ge(v_ready, n + 1)
                sp.wait_ge(bias_added, n + 1)
                k.load_cross_rows(sp, j, n + 2)
            if more:
                store_steps(1 - j, n + 1)
            if prev:
                store(1 - j, n - 1)
            store_whole(j, n)

        for j in range(2):
            sp.sem_inc(k.cross_stored[j], 16)
            sp.sem_inc(whole_stored[j], 16)
            sp.sem_inc(steps_stored[j], 16)
        store_steps(0, 0)
        in_steps(step, sp)
        for j in range(2):
            sp.wait_ge(k.cross_stored[j], 32)
            k.load_attend_rows(sp, k.row_in[j], k.row_loaded[j], j)
            k.load_attend_rows(sp, k.row_res[j], k.res_loaded[j], j)
        store(1, B - 1)
        for j in range(2):
            sp.wait_ge(k.cross_stored[j], 16 * TURNS + 16)
            sp.wait_ge(whole_stored[j], 16 * TURNS + 16)
            sp.wait_ge(steps_stored[j], 16 * TURNS + 16)

    def tensor(pe):
        pe.wait_ge(k.begun, k.begins["cross"])
        pe.wait_ge(k.cross_loads, 16 * LOADS)
        pe.sem_inc(scores_ready, 2)
        pe.sem_inc(probs_turned, 4)

        def front(j, n, i, begin=False):
            pe.wait_ge(rows_in[j], 32 * i + 32)
            if not begin:
                pe.wait_ge(heads_t_ready, n)
            for c in range(DC):
                last = pe.transpose(banks[:, TURN, c * P:(c + 1) * P], x_in[j][:, c * P:(c + 1) * P], k.ident)
            last.then_inc(x_turned, 1)
            if not begin:
                pe.wait_ge(qk_read, n)
            for m in range(DC):
                for c in range(DC):
                    pe.matmul(banks[:, QK, (DC + m) * P:(DC + m + 1) * P], wk[:, c, m * P:(m + 1) * P],
                              ctx_t[j][:, c, :], start=(c == 0), stop=(c == DC - 1))
            pe.wait_ge(x_t_ready, n + 1)
            for m in range(DC):
                for c in range(DC):
                    last = pe.matmul(banks[:, QK, m * P:(m + 1) * P], wq[:, c, m * P:(m + 1) * P],
                                     x_t[j][:, c, :], start=(c == 0), stop=(c == DC - 1))
            last.then_inc(qk_ready, 1)
            if not begin:
                pe.wait_ge(v_read, n)
                pe.wait_ge(joined_read, n)
            for c in range(DC):
                last = pe.matmul(banks[:, V, 0:D], ctx_t[j][:, c, :], wv[:, c, :], start=(c == 0), stop=(c == DC - 1))
            last.then_inc(v_ready, 1)

        def scores(j, h, n, begin=False):
            pe.wait_ge(spread_ready, 2 * n + h + 1)
            if not begin:
                pe.wait_ge(scores_read, 2 * n + h)
            for m in range(2):
                last = pe.matmul(banks[:, SCORES + m, :], q_t[j][:, h, :],
                                 spread[h][:, 4 * m:4 * m + 4, :].rearrange("p h s -> p (h s)"), start=True, stop=True)
            last.then_inc(scores_ready, 1)

        def turn_probs(h, n):
            pe.wait_ge(exp_ready, 2 * n + h + 1)
            for m in range(2):
                pe.wait_ge(probs_t_ready, 4 * n + 2 * h + m + 1)
                for a in range(4):
                    last = pe.transpose(banks[:, PROBS_T + m, a * P:(a + 1) * P], probs[h][:, 4 * m + a, :], k.ident)
                last.then_inc(probs_turned, 1)

        def sums(j, h, n):
            if h == 0:
                pe.wait_ge(v_read, n + 1)
                pe.wait_ge(heads_ready, n + 1)
            for m in range(2):
                pe.wait_ge(probs_t_ready, 4 * n + 2 * h + m + 3)
                for a in range(4):
                    head = HALF * h + 4 * m + a
                    last = pe.matmul(banks[:, HEADS, head * (XK + 1):(head + 1) * (XK + 1)], probs_t[h][:, 4 * m + a, :],
                                     v_ones[j][:, head, :], start=True, stop=True)
            if h:
                last.then_inc(heads_summed, 1)

        def turn_heads(j, n, more):
            pe.wait_ge(heads_ready, n + 2)
            pe.wait_ge(x_t_ready, n + 1 + more)
            pe.wait_ge(whole_read, ROUNDS * n + ROUNDS)
            for c in range(DC):
                last = pe.transpose(banks[:, TURN, c * P:(c + 1) * P],
                                    heads[j][:, HALF * c:HALF * (c + 1), :].rearrange("p h d -> p (h d)"), k.ident)
            last.then_inc(heads_turned, 1)

        def join(j, n, more):
            pe.wait_ge(heads_t_ready, n + 2)
            pe.wait_ge(v_read, n + 1 + more)
            for c in range(DC):
                last = pe.matmul(banks[:, V, 0:D], heads_t[j][:, c, :], wo[:, c, :], start=(c == 0), stop=(c == DC - 1))
            last.then_inc(joined_ready, 1)

        def turn_whole(j, n, r, more):
            if r == 0:
                pe.wait_ge(whole_ready, n + 1)
                pe.wait_ge(x_t_ready, n + 1 + more)
                pe.wait_ge(heads_t_ready, n + 1)
            else:
                pe.wait_ge(whole_read, ROUNDS * n + r)
            for a in range(4 * r, min(4 * r + 4, TILES)):
                last = pe.matmul(banks[:, TURN, (a - 4 * r) * P:(a - 4 * r + 1) * P], whole[j][:, a, :], k.ident16[:, :],
                                 start=True, stop=True)
            last.then_inc(whole_turned, 1)

        def step(j, n, i, prev, more):
            def tiles(r):
                turn_whole(j, n, r, min(more, 1))

            scores(j, 1, n)
            if prev:
                turn_heads(1 - j, n - 1, 1)
            turn_probs(0, n)
            if prev:
                join(1 - j, n - 1, 1)
            if more:
                front(1 - j, n + 1, i + 1)
            tiles(0)
            sums(j, 0, n)
            tiles(1)
            turn_probs(1, n)
            if more:
                scores(1 - j, 0, n + 1)
            tiles(2)
            sums(j, 1, n)
            tiles(3)

        front(0, 0, 0, True)
        scores(0, 0, 0, True)
        in_steps(step, pe)
        turn_heads(1, B - 1, 0)
        join(1, B - 1, 0)

    def scalar(act):
        act.wait_ge(k.begun, k.begins["cross"])
        act.wait_ge(k.cross_loads, 16 * LOADS)
        act.sem_inc(heads_t_ready, 1)
        act.sem_inc(probs_t_ready, 2)

        def take_x(j, n):
            act.wait_ge(x_turned, n + 1)
            act.copy(x_t[j][:, :, :], banks[:, TURN, 0:D].rearrange("p (c s) -> p c s", c=DC)).then_inc(x_t_ready, 1)

        def take_qk(j, n):
            act.wait_ge(qk_ready, n + 1)
            for c in range(DC):
                act.activation(k_t[j][:, c, :], banks[:, QK, (DC + c) * P:(DC + c + 1) * P], ACT.Identity,
                               bias=bqk[:, DC + c:DC + c + 1])
            for c in range(DC):
                last = act.activation(q_t[j][:, c, :], banks[:, QK, c * P:(c + 1) * P], ACT.Identity,
                                      bias=bqk[:, c:c + 1])
            last.then_inc(qk_read, 1)

        def soften(h, n):
            act.wait_ge(scores_read, 2 * n + h + 1)
            act.activation(probs[h][:, :, :], probs[h][:, :, :], ACT.Exp, scale=float(XK) ** -0.5).then_inc(exp_ready, 1)

        def collect(h, n):
            for m in range(2):
                act.wait_ge(probs_turned, 4 * n + 2 * h + m + 5)
                act.copy(probs_t[h][:, 4 * m:4 * m + 4, :], banks[:, PROBS_T + m, :].rearrange(
                    "p (a s) -> p a s", a=4)).then_inc(probs_t_ready, 1)

        def back(j, n):
            act.wait_ge(heads_turned, n + 1)
            act.copy(heads_t[j][:, :, :], banks[:, TURN, 0:D].rearrange("p (c s) -> p c s", c=DC)).then_inc(
                heads_t_ready, 1)

        def round_part(j, n, part):
            if part == 0:
                act.wait_ge(scale_ready, n + 1)
                if not (isinstance(n, int) and n < 2):
                    act.wait_ge(whole_ready, n - 1)
            for a in ROUND_PARTS[part]:
                last = act.activation(level[j][:, a, :], raw[j][:, a, :], ACT.Identity, bias=k.magic[:, :],
                                      scale=stat[j][:, INV, a:a + 1])
            if part == 2:
                last.then_inc(rounded, 1)

        def make_whole(j, n):
            act.wait_ge(clipped, n + 1)
            act.wait_ge(pool_clipped, n + 1)
            act.activation(whole[j][:, :, :], level[j][:, :, :], ACT.Identity, bias=k.minus_magic[:, :]).then_inc(whole_ready, 1)

        def take_whole(j, n, r, i):
            if r == 0:
                act.wait_ge(whole_stored[j], 16 * i + 16)
            act.wait_ge(whole_turned, ROUNDS * n + r + 1)
            tiles = range(4 * r, min(4 * r + 4, TILES))
            act.copy(whole_t[j][:, tiles.start:tiles.stop, :], banks[:, TURN, 0:len(tiles) * P].rearrange(
                "p (a b) -> p a b", a=len(tiles))).then_inc(whole_read, 1)

        def step(j, n, i, prev, more):
            def tiles(r):
                take_whole(j, n, r, i + 1 - j if prev else 0)

            if prev:
                back(1 - j, n - 1)
            collect(0, n)
            soften(1, n)
            if more:
                take_x(1 - j, n + 1)
            make_whole(j, n)
            if more:
                round_part(1 - j, n + 1, 0)
                take_qk(1 - j, n + 1)
            tiles(0)
            if more:
                round_part(1 - j, n + 1, 1)
            tiles(1)
            collect(1, n)
            tiles(2)
            if more:
                round_part(1 - j, n + 1, 2)
            tiles(3)
            if more:
                soften(0, n + 1)

        take_x(0, 0)
        take_qk(0, 0)
        for part in range(3):
            round_part(0, 0, part)
        soften(0, 0)
        in_steps(step, act)
        back(1, B - 1)

    def gpsimd(pool):
        pool.wait_ge(k.begun, k.begins["cross"])
        pool.wait_ge(k.cross_loads, 16 * LOADS)
        head_mask = k.consts[:, C_HEAD:C_HEAD + HALF]

        def spread_keys(j, h, n):
            pool.wait_ge(qk_read, n + 1)
            pool.wait_ge(scores_ready, 2 * n + h + 1)
            pool.tensor_tensor(spread[h][:, :, :], each(k_t[j][:, h, :], HALF), wide(head_mask, S),
                               ALU.mult).then_inc(spread_ready, 1)

        def add_bias(j, n, i, begin=False):
            pool.wait_ge(rows_in[j], 32 * i + 32)
            if not begin:
                pool.wait_ge(joined_read, n)
            pool.tensor_tensor(x_bias[j][:, :], x_in[j][:, :], bias_rows[:, 1, :], ALU.add).then_inc(bias_added, 1)

        def scale(j, n):
            pool.wait_ge(cross_var, n + 1)
            pool.tensor_tensor(ln[j][:, 9:10], ln[j][:, 8:9], k.minus_half[:, 0:1], ALU.pow).then_inc(cross_scale, 1)

        def clip_part(j, n):
            pool.wait_ge(rounded, n + 1)
            pool.sem_inc(k.s_held, 1)
            for a in range(DVE_TILES, TILES):
                last = pool.tensor_scalar(level[j][:, a, :], level[j][:, a, :], stat[j][:, LOW, a:a + 1],
                                          stat[j][:, HIGH, a:a + 1], ALU.max, ALU.min)
            last.then_inc(pool_clipped, 1)

        def step(j, n, i, prev, more):
            clip_part(j, n)
            if prev:
                scale(1 - j, n - 1)
            if more:
                add_bias(1 - j, n + 1, i + 1, not prev)
                spread_keys(1 - j, 0, n + 1)
                spread_keys(1 - j, 1, n + 1)

        add_bias(0, 0, 0, True)
        for h in range(2):
            spread_keys(0, h, 0)
        in_steps(step, pool)
        scale(1, B - 1)

    def vector(dve):
        st = k.steps["dve"]

        def take_values(j, n):
            dve.wait_ge(v_ready, n + 1)
            dve.tensor_tensor(v_ones[j][:, :, 0:XK], banks[:, V, 0:D].rearrange("p (h d) -> p h d", h=XH),
                              bias_rows[:, 0, :].rearrange("p (h d) -> p h d", h=XH), ALU.add).then_inc(v_read, 1)

        def peaks(h, n):
            dve.wait_ge(scores_ready, 2 * n + h + 3)
            chunk = banks[:, SCORES:SCORES + 2, :].rearrange("p m (a s) -> p (m a) s", a=4)
            st.did(dve.tensor_reduce(peak[h][:, :], chunk, AX.X, ALU.max))
            st.wait()
            dve.wait_ge(probs_turned, 4 * n + 2 * h + 2)
            dve.tensor_tensor(probs[h][:, :, :], chunk, wide(peak[h][:, :], S), ALU.subtract).then_inc(scores_read, 1)

        def normalise(j, n):
            dve.wait_ge(heads_summed, n + 1)
            all_heads = banks[:, HEADS, 0:XH * (XK + 1)].rearrange("p (h d) -> p h d", h=XH)
            st.did(dve.reciprocal(total[:, :], all_heads[:, :, XK]))
            st.wait()
            dve.tensor_tensor(heads[j][:, :, :], all_heads[:, :, 0:XK], wide(total[:, :], XK), ALU.mult).then_inc(
                heads_ready, 1)

        def join(j, n, i):
            dve.wait_ge(joined_ready, n + 1)
            dve.wait_ge(bias_added, n + 1)
            dve.tensor_tensor(joined[j][:, :], banks[:, V, 0:D], x_bias[j][:, :], ALU.add).then_inc(joined_read, 1)
            dve.wait_ge(joined_read, n + 2)
            norm_stats(k, dve, st, ln[j][:, 0:6], ln[j][:, 6:8], ln[j][:, 8:9], joined[j][:, :]).then_inc(cross_var, 1)
            dve.wait_ge(cross_scale, n + 1)
            dve.wait_ge(k.cross_stored[j], 16 * i + 16)
            dve.tensor_scalar(crossed[j][:, :], joined[j][:, :], ln[j][:, 6:7], ln[j][:, 9:10],
                              ALU.subtract, ALU.mult).then_inc(cross_normed, 1)

        def steps_of(j, n, i, begin=False):
            dve.wait_ge(raw_in[j], 16 * i + 16)
            dve.wait_ge(steps_stored[j], 16 * i + 16)
            if not begin:
                dve.wait_ge(pool_clipped, n - 1)
            group_steps(dve, st, stat[j], raw[j][:, :, :]).then_inc(scale_ready, 1)

        def clip(j, n):
            dve.wait_ge(rounded, n + 1)
            for a in range(DVE_TILES):
                last = dve.tensor_scalar(level[j][:, a, :], level[j][:, a, :], stat[j][:, LOW, a:a + 1],
                                         stat[j][:, HIGH, a:a + 1], ALU.max, ALU.min)
            last.then_inc(clipped, 1)

        def step(j, n, i, prev, more):
            clip(j, n)
            peaks(1, n)
            if prev:
                join(1 - j, n - 1, i)
            if more:
                take_values(1 - j, n + 1)
            if more == 2:
                steps_of(j, n + 2, i + 2 - j)
            if more:
                peaks(0, n + 1)
            normalise(j, n)

        dve.wait_ge(k.begun, k.begins["cross"])
        dve.wait_ge(k.cross_loads, 16 * LOADS)
        dve.sem_inc(joined_read, 1)
        dve.sem_inc(heads_ready, 1)
        for j in range(2):
            dve.memset(v_ones[j][:, :, XK:XK + 1], 1.0)
        steps_of(0, 0, 0, True)
        take_values(0, 0)
        peaks(0, 0)
        steps_of(1, 1, 0, True)
        st.done(1, st.at)
        in_steps(step, dve, st, 2 * (5 + 8))
        join(1, B - 1, TURNS - 1)
        st.done(1, st.at)

    return sync, tensor, vector, scalar, gpsimd


def attend_stage(k):
    nc, t, banks = k.nc, k.t, k.banks
    weights, gate_w, gains = k.attend_w, k.gate_w, k.gains
    QKV = (QH + 2 * KVH) * HD
    k.levels = k.buffer(k.top, "levels", [2 * E, JOB], BF16)
    k.down = k.buffer(k.top, "down", [2 * E, JOB // 2])
    k.level_steps = k.buffer(k.top, "level_steps", [2 * E, TILES])
    k.expert_loads = k.semaphore("expert_loads")
    with ExitStack() as own:
        squares = [k.buffer(own, f"squares{a}", [D]) for a in range(2)]
        rms = [k.buffer(own, f"rms{a}", [3]) for a in range(2)]
        xn = k.buffer(own, "xn", [D])
        xn_t = k.buffer(own, "xn_t", [DC, S])
        q_rot = k.buffer(own, "q_rot", [QH, HD])
        q_sin = k.buffer(own, "q_sin", [QH, HD])
        kv_stat = k.buffer(own, "kv_stat", [8, 2 * KVH])
        kvq = [k.buffer(own, f"kvq{j}", [2 * KVH, HD]) for j in range(2)]
        k_rot = k.buffer(own, "k_rot", [KVH, HD])
        k_sin = k.buffer(own, "k_sin", [KVH, HD])
        q_turn = k.buffer(own, "q_turn", [QH, S])
        k_turn = k.buffer(own, "k_turn", [KVH, S])
        probs = k.buffer(own, "att_probs", [QH, S])
        low_peak = k.buffer(own, "low_peak", [QH])
        total = k.buffer(own, "att_total", [QH])
        share = k.buffer(own, "att_share", [QH])
        probs_turn = k.buffer(own, "probs_turn", [QH, S])
        o_turn = k.buffer(own, "o_turn", [QH, S])
        hidden = [k.buffer(own, f"hidden{j}", [D]) for j in range(2)]
        normed = [k.buffer(own, f"normed{j}", [D]) for j in range(2)]
        hn_turn = k.buffer(own, "hn_turn", [DC, S])
    names = ("xn_var xn_scale xn_ready xn_turned xn_t_ready kv_ready q_ready roped_q q_rot_ready kv_scaled "
             "kv_rounded k_rot_ready q_turned q_t_ready k_turned k_t_ready scores2 masked peaked exped share_ready probs_ready probs_turned2 "
             "probs_t2 o_summed o_t_ready hidden_ready hn_var hn_scale hn_ready residual_ready hn_turned hn_t_ready logits_ready").split()
    s = {n: k.semaphore(n) for n in names}
    k.logits_read = k.semaphore("logits_read")
    row_in, row_res, row_loaded, res_loaded = k.row_in, k.row_res, k.row_loaded, k.res_loaded
    attend_stored = [k.semaphore(f"attend_stored{j}") for j in range(2)]
    LOADS, TURNS = 6, B // 2
    TURN, Q, KV, PROBS_T, Q_T = 0, 1, 3, 4, 6
    MAX, MIN, SCALE, INV, BASE, LOW, HIGH, TMP = range(8)
    HALF_HD = HD // 2

    def in_steps(emit, eng, st=None, per=None):
        for n in range(3):
            emit(n % 2, n, (n - 1) // 2, n, 3)
        if st:
            st.done(1, st.at)
        with eng.Fori(0, TURNS - 3) as i:
            if st:
                st.turn(i, per)
            for j in (1, 0):
                emit(j, 2 * i + 4 - j, i + 1, 2, 3)
        if st:
            st.done(TURNS - 3, per)
        for j, n, more in ((1, B - 3, 2), (0, B - 2, 1), (1, B - 1, 0)):
            emit(j, n, (n - 1) // 2, 2, more)

    def sync(sp):
        k.begin(sp, "attend")

        def load_row(j, n):
            sp.wait_ge(s["xn_ready"], n - 1)
            k.load_attend_rows(sp, row_in[j], row_loaded[j], n)

        def load_expert(j, n, i):
            sp.dma_start(k.levels[:, bass.ds(n, 1), :].rearrange("p o a -> p (o a)"),
                         k.levels_d[bass.ds(n, 1)].rearrange("o p a -> (o p) a")).then_inc(k.expert_loads, 16)
            sp.dma_start(k.down[:, bass.ds(n, 1), :].rearrange("p o a -> p (o a)"),
                         k.numbers_d[bass.ds(i + 3, 1), :, j * (JOB // 2):(j + 1) * (JOB // 2)].rearrange("o p a -> (o p) a")).then_inc(k.expert_loads, 16)

        def element(j, n, i, rows=True, res=True):
            load_expert(j, n, i)
            for src, dst, ready in ((normed, k.normed_d, "hn_ready"), (hidden, k.hidden_d, "residual_ready")):
                sp.wait_ge(s[ready], n + 1)
                sp.dma_start(dst[bass.ds(n * S, S), :], src[j][:, :]).then_inc(attend_stored[j], 16)
            if res:
                k.load_attend_rows(sp, row_res[j], res_loaded[j], n + 2)
            if rows:
                load_row(1 - j, n + 5)

        sp.dma_start(k.level_steps[:, :, :], k.steps_d.rearrange("m p a -> p m a")).then_inc(k.expert_loads, 16)
        for j in range(2):
            sp.sem_inc(attend_stored[j], 32)
        for n in range(2, 5):
            load_row(n % 2, n)
        with sp.Fori(0, (B - 6) // 2) as i:
            for j in range(2):
                element(j, 2 * i + j, i)
        for n in range(B - 6, B):
            element(n % 2, n, n // 2, n + 5 < B, n + 2 < B)
        for j in range(2):
            sp.wait_ge(attend_stored[j], 32 * TURNS + 32)

    def tensor(pe):
        pe.wait_ge(k.begun, k.begins["attend"])
        pe.wait_ge(k.attend_loads, 16 * LOADS)
        w_qkv = weights[:, 0:2 * QKV // P, :].rearrange("p (c r) j -> p c (r j)", c=DC)
        w_o = weights[:, 2 * QKV // P:2 * QKV // P + DC * QH, :].rearrange("p (h c) j -> p h (c j)", c=DC)

        def turn_x(n):
            pe.wait_ge(s["xn_ready"], n + 1)
            for c in range(DC):
                last = pe.transpose(banks[:, Q_T, c * P:(c + 1) * P], xn[:, c * P:(c + 1) * P], k.ident)
            last.then_inc(s["xn_turned"], 1)

        def project_kv(n, begin=False):
            pe.wait_ge(s["xn_t_ready"], n + 1)
            if not begin:
                pe.wait_ge(s["k_t_ready"], n)
            for c in range(DC):
                last = pe.matmul(banks[:, KV, :], xn_t[:, c, :], w_qkv[:, c, QH * HD:QKV], start=(c == 0), stop=(c == DC - 1))
            last.then_inc(s["kv_ready"], 1)

        def project_q(n, begin=False):
            if not begin:
                pe.wait_ge(s["masked"], n)
            for m in range(2):
                for c in range(DC):
                    last = pe.matmul(banks[:, Q + m, :], xn_t[:, c, :], w_qkv[:, c, 512 * m:512 * m + 512],
                                     start=(c == 0), stop=(c == DC - 1))
            last.then_inc(s["q_ready"], 1)

        def turn_q(n, more):
            if more:
                pe.wait_ge(s["xn_t_ready"], n + 2)
            pe.wait_ge(s["q_rot_ready"], n + 1)
            for m in range(2):
                for a in range(4):
                    last = pe.transpose(banks[:, Q_T + m, a * P:(a + 1) * P], q_rot[:, 4 * m + a, :], k.ident)
                last.then_inc(s["q_turned"], 1)

        def turn_k(n):
            pe.wait_ge(s["k_rot_ready"], n + 1)
            for a in range(KVH):
                last = pe.transpose(banks[:, KV, a * P:(a + 1) * P], k_rot[:, a, :], k.ident)
            last.then_inc(s["k_turned"], 1)

        def scores(n):
            pe.wait_ge(s["q_t_ready"], 2 * n + 2)
            pe.wait_ge(s["k_t_ready"], n + 1)
            for h in range(QH):
                last = pe.matmul(banks[:, Q + h // 4, (h % 4) * S:(h % 4 + 1) * S], q_turn[:, h, :], k_turn[:, h // REP, :],
                                 start=True, stop=True)
            last.then_inc(s["scores2"], 1)

        def turn_probs(n):
            pe.wait_ge(s["probs_ready"], n + 1)
            for m in range(2):
                for a in range(4):
                    last = pe.transpose(banks[:, PROBS_T + m, a * P:(a + 1) * P], probs[:, 4 * m + a, :], k.ident)
                last.then_inc(s["probs_turned2"], 1)

        def sums(j, n, m):
            pe.wait_ge(s["probs_t2"], 2 * n + m + 1)
            pe.matmul(banks[:, PROBS_T + m, :], kvq[j][:, KVH + m, :],
                      probs_turn[:, REP * m:REP * (m + 1), :].rearrange("p h s -> p (h s)"),
                      start=True, stop=True).then_inc(s["o_summed"], 1)

        def join(n):
            pe.wait_ge(k.logits_read, n + 1)
            pe.wait_ge(s["o_t_ready"], 2 * n + 2)
            for h in range(QH):
                last = pe.matmul(banks[:, TURN, 0:D], o_turn[:, h, :], w_o[:, h, :], start=(h == 0), stop=(h == QH - 1))
            last.then_inc(s["hidden_ready"], 1)

        def turn_hn(j, n):
            pe.wait_ge(s["hn_ready"], n + 1)
            for c in range(DC):
                last = pe.transpose(banks[:, TURN, c * P:(c + 1) * P], normed[j][:, c * P:(c + 1) * P], k.ident)
            last.then_inc(s["hn_turned"], 1)

        def route(n):
            pe.wait_ge(s["hn_t_ready"], n + 1)
            for c in range(DC):
                last = pe.matmul(banks[:, TURN, D:D + E], hn_turn[:, c, :], gate_w[:, c, :], start=(c == 0), stop=(c == DC - 1))
            last.then_inc(s["logits_ready"], 1)

        def step(j, n, i, prev, more):
            scores(n)
            if prev == 2:
                turn_hn(j, n - 2)
            if more:
                project_kv(n + 1)
            if prev == 2:
                route(n - 2)
            if more:
                project_q(n + 1)
            if prev:
                join(n - 1)
            if more >= 2:
                turn_x(n + 2)
            turn_probs(n)
            if more:
                turn_q(n + 1, more >= 2)
            for m in range(KVH):
                sums(j, n, m)
                if more and m == 0:
                    turn_k(n + 1)

        turn_x(0)
        project_kv(0, True)
        project_q(0, True)
        turn_x(1)
        turn_q(0, True)
        turn_k(0)
        in_steps(step, pe)
        turn_hn(0, B - 2)
        route(B - 2)
        join(B - 1)
        turn_hn(1, B - 1)
        route(B - 1)

    def scalar(act):
        act.wait_ge(k.begun, k.begins["attend"])
        act.wait_ge(k.attend_loads, 16 * LOADS)

        def take_x(n):
            act.wait_ge(s["xn_turned"], n + 1)
            act.copy(xn_t[:, :, :], banks[:, Q_T, 0:D].rearrange("p (c s) -> p c s", c=DC)).then_inc(s["xn_t_ready"], 1)

        def round_kv(j, n):
            act.wait_ge(s["kv_scaled"], n + 1)
            for a in range(2 * KVH):
                last = act.activation(kvq[j][:, a, :], banks[:, KV, a * HD:(a + 1) * HD], ACT.Identity,
                                      bias=k.magic[:, :], scale=kv_stat[:, INV, a:a + 1])
            last.then_inc(s["kv_rounded"], 1)

        def take_q(n):
            for m in range(2):
                act.wait_ge(s["q_turned"], 2 * n + m + 1)
                act.copy(q_turn[:, 4 * m:4 * m + 4, :], banks[:, Q_T + m, :].rearrange(
                    "p (a s) -> p a s", a=4)).then_inc(s["q_t_ready"], 1)

        def take_k(n):
            act.wait_ge(s["k_turned"], n + 1)
            act.copy(k_turn[:, :, :], banks[:, KV, 0:KVH * S].rearrange("p (a s) -> p a s", a=KVH)).then_inc(
                s["k_t_ready"], 1)

        def soften(n):
            act.wait_ge(s["peaked"], n + 1)
            for h in range(QH):
                last = act.activation(probs[:, h, :], probs[:, h, :], ACT.Exp, bias=low_peak[:, h:h + 1],
                                      accum_out=total[:, h:h + 1])
            last.then_inc(s["exped"], 1)

        def take_probs(n):
            for m in range(2):
                act.wait_ge(s["probs_turned2"], 2 * n + m + 1)
                act.copy(probs_turn[:, 4 * m:4 * m + 4, :], banks[:, PROBS_T + m, :].rearrange(
                    "p (a s) -> p a s", a=4)).then_inc(s["probs_t2"], 1)

        def take_outputs(n, m):
            act.wait_ge(s["o_summed"], 2 * n + m + 1)
            act.copy(o_turn[:, REP * m:REP * (m + 1), :], banks[:, PROBS_T + m, :].rearrange(
                "p (a s) -> p a s", a=REP)).then_inc(s["o_t_ready"], 1)

        def take_hn(n):
            act.wait_ge(s["hn_turned"], n + 1)
            act.copy(hn_turn[:, :, :], banks[:, TURN, 0:D].rearrange("p (c s) -> p c s", c=DC)).then_inc(s["hn_t_ready"], 1)

        def take_logits(n):
            act.wait_ge(s["logits_ready"], n + 1)
            act.copy(k.logits[:, bass.ds(n, 1), :], banks[:, TURN:TURN + 1, D:D + E]).then_inc(k.logits_read, 1)

        def step(j, n, i, prev, more):
            if prev == 2:
                take_hn(n - 2)
                take_logits(n - 2)
            soften(n)
            if more:
                round_kv(1 - j, n + 1)
            if more >= 2:
                take_x(n + 2)
            take_probs(n)
            if more:
                take_q(n + 1)
            for m in range(KVH):
                take_outputs(n, m)
                if more and m == 0:
                    take_k(n + 1)

        act.sem_inc(k.logits_read, 1)
        take_x(0)
        round_kv(0, 0)
        take_x(1)
        take_q(0)
        take_k(0)
        in_steps(step, act)
        take_hn(B - 2)
        take_logits(B - 2)
        take_hn(B - 1)
        take_logits(B - 1)

    def gpsimd(pool):
        pool.wait_ge(k.begun, k.begins["attend"])
        pool.wait_ge(k.attend_loads, 16 * LOADS)

        def rotate(n):
            pool.wait_ge(s["roped_q"], n + 1)
            pool.tensor_tensor(q_rot[:, :, :], q_rot[:, :, :], q_sin[:, :, :], ALU.add).then_inc(s["q_rot_ready"], 1)

        def scale(a, name, n):
            pool.wait_ge(s[name + "_var"], n + 1)
            pool.tensor_tensor(rms[a][:, 2:3], rms[a][:, 1:2], k.minus_half[:, 0:1], ALU.pow).then_inc(s[name + "_scale"], 1)

        def add_input(j, n):
            pool.wait_ge(s["hn_ready"], n + 1)
            pool.tensor_tensor(hidden[j][:, :], hidden[j][:, :], row_res[j][:, :], ALU.add).then_inc(s["residual_ready"], 1)

        def step(j, n, i, prev, more):
            pool.wait_ge(s["share_ready"], n + 1)
            pool.tensor_tensor(probs[:, :, :], probs[:, :, :], wide(share[:, :], S), ALU.mult).then_inc(s["probs_ready"], 1)
            if more:
                rotate(n + 1)
            if prev:
                scale(1, "hn", n - 1)
            if more == 3:
                scale(0, "xn", n + 3)
            if prev:
                add_input(1 - j, n - 1)

        scale(0, "xn", 0)
        scale(0, "xn", 1)
        rotate(0)
        scale(0, "xn", 2)
        in_steps(step, pool)
        scale(1, "hn", B - 1)
        add_input(1, B - 1)

    def vector(dve):
        st = k.steps["dve"]
        dve.wait_ge(k.begun, k.begins["attend"])
        dve.wait_ge(k.attend_loads, 16 * LOADS)
        cos, sin = k.consts[:, C_COS:C_COS + HD], k.consts[:, C_SIN:C_SIN + HD]
        mask = k.consts[:, C_MASK:C_MASK + S]

        def mean_square(a, rows, name):
            st.did(dve.tensor_tensor_reduce(squares[a][:, :], rows, rows, 1.0, 0.0, ALU.mult, ALU.add, rms[a][:, 0:1]))
            st.wait()
            dve.tensor_scalar(rms[a][:, 1:2], rms[a][:, 0:1], 1.0 / D, EPS, ALU.mult, ALU.add).then_inc(s[name + "_var"], 1)

        def x_stats(j, n, i):
            dve.wait_ge(row_loaded[j], 16 * i + 16)
            mean_square(0, row_in[j][:, :], "xn")

        def x_norm(j, n):
            dve.wait_ge(s["xn_scale"], n + 1)
            if not (isinstance(n, int) and n == 0):
                dve.wait_ge(s["xn_turned"], n)
            dve.scalar_tensor_tensor(out=xn[:, :], in0=row_in[j][:, :], scalar=rms[0][:, 2:3], in1=gains[:, 0, :],
                                     op0=ALU.mult, op1=ALU.mult).then_inc(s["xn_ready"], 1)

        def rotate_q(n):
            q = banks[:, Q:Q + 2, :].rearrange("p m (a d) -> p (m a) d", a=4)
            dve.wait_ge(s["q_ready"], n + 1)
            if not (isinstance(n, int) and n == 0):
                dve.wait_ge(s["q_turned"], 2 * n)
            dve.tensor_tensor(q_rot[:, :, :], q, each(cos, QH), ALU.mult)
            for a, b in ((0, HALF_HD), (HALF_HD, 0)):
                last = dve.tensor_tensor(q_sin[:, :, a:a + HALF_HD], q[:, :, b:b + HALF_HD],
                                         each(sin[:, a:a + HALF_HD], QH), ALU.mult)
            last.then_inc(s["roped_q"], 1)

        def kv_stats(n):
            a = kv_stat
            kv = banks[:, KV, :].rearrange("p (g d) -> p g d", g=2 * KVH)
            dve.wait_ge(s["kv_ready"], n + 1)
            dve.tensor_reduce(a[:, MAX, :], kv, AX.X, ALU.max)
            st.did(dve.tensor_reduce(a[:, MIN, :], kv, AX.X, ALU.min))
            st.wait()
            st.did(dve.tensor_tensor(a[:, TMP, :], a[:, MAX, :], a[:, MIN, :], ALU.subtract))
            st.wait()
            st.did(dve.tensor_scalar(a[:, SCALE, :], a[:, TMP, :], 1e-5, 1.0 / LEVELS, ALU.max, ALU.mult))
            st.wait()
            dve.reciprocal(a[:, INV, :], a[:, SCALE, :]).then_inc(s["kv_scaled"], 1)
            dve.wait_ge(s["kv_scaled"], n + 1)
            st.did(dve.scalar_tensor_tensor(out=a[:, TMP, :], in0=a[:, MIN, :], scalar=-1.0, in1=a[:, INV, :],
                                            op0=ALU.mult, op1=ALU.mult))
            st.wait()
            st.did(dve.tensor_scalar(a[:, BASE, :], a[:, TMP, :], MAGIC, MAGIC, ALU.add, ALU.subtract))
            st.wait()
            st.did(dve.tensor_scalar(a[:, TMP, :], a[:, BASE, :], 0.0, LEVELS, ALU.max, ALU.min))
            st.wait()
            st.did(dve.tensor_scalar(a[:, LOW, :], a[:, TMP, :], -1.0, MAGIC, ALU.mult, ALU.add))
            st.wait()
            st.did(dve.tensor_scalar(a[:, HIGH, :], a[:, LOW, :], LEVELS, None, ALU.add))
            st.wait()

        def kv_scale(j, n):
            a, x = kv_stat, kvq[j]
            dve.wait_ge(s["kv_rounded"], n + 1)
            for g in range(2 * KVH):
                last = dve.tensor_scalar(x[:, g, :], x[:, g, :], a[:, LOW, g:g + 1], a[:, HIGH, g:g + 1], ALU.max, ALU.min)
            st.did(last)
            st.wait()
            for g in range(2 * KVH):
                last = dve.tensor_scalar(x[:, g, :], x[:, g, :], MAGIC, a[:, SCALE, g:g + 1], ALU.subtract, ALU.mult)
            st.did(last)

        def rotate_k(j, n):
            keys = kvq[j][:, 0:KVH, :]
            st.wait()
            if not (isinstance(n, int) and n == 0):
                dve.wait_ge(s["k_turned"], n)
            dve.tensor_tensor(k_rot[:, :, :], keys, each(cos, KVH), ALU.mult)
            for lo, hi in ((0, HALF_HD), (HALF_HD, 0)):
                last = dve.tensor_tensor(k_sin[:, :, lo:lo + HALF_HD], keys[:, :, hi:hi + HALF_HD],
                                         each(sin[:, lo:lo + HALF_HD], KVH), ALU.mult)
            st.did(last)
            st.wait()
            dve.tensor_tensor(k_rot[:, :, :], k_rot[:, :, :], k_sin[:, :, :], ALU.add).then_inc(s["k_rot_ready"], 1)

        def mask_scores(n):
            dve.wait_ge(s["scores2"], n + 1)
            if not (isinstance(n, int) and n == 0):
                dve.wait_ge(s["probs_turned2"], 2 * n)
            dve.scalar_tensor_tensor(out=probs[:, :, :], in0=banks[:, Q:Q + 2, :].rearrange("p m (a d) -> p (m a) d", a=4),
                                     scalar=float(HD) ** -0.5, in1=each(mask, QH), op0=ALU.mult, op1=ALU.add).then_inc(s["masked"], 1)
            dve.wait_ge(s["masked"], n + 1)
            dve.tensor_reduce(low_peak[:, :], probs[:, :, :], AX.X, ALU.max, negate=True).then_inc(s["peaked"], 1)

        def shares(n):
            dve.wait_ge(s["exped"], n + 1)
            dve.reciprocal(share[:, :], total[:, :]).then_inc(s["share_ready"], 1)

        def h_stats(j, n, i):
            dve.wait_ge(s["hidden_ready"], n + 1)
            dve.wait_ge(res_loaded[j], 16 * i + 16)
            dve.wait_ge(attend_stored[j], 32 * i + 32)
            st.did(dve.tensor_tensor(hidden[j][:, :], banks[:, TURN, 0:D], row_res[j][:, :], ALU.add))
            st.wait()
            mean_square(1, hidden[j][:, :], "hn")

        def h_norm(j, n):
            dve.wait_ge(s["hn_scale"], n + 1)
            dve.scalar_tensor_tensor(out=normed[j][:, :], in0=hidden[j][:, :], scalar=rms[1][:, 2:3], in1=gains[:, 1, :],
                                     op0=ALU.mult, op1=ALU.mult).then_inc(s["hn_ready"], 1)

        def step(j, n, i, prev, more):
            mask_scores(n)
            if more:
                kv_stats(n + 1)
            shares(n)
            if more:
                rotate_q(n + 1)
            if more:
                kv_scale(1 - j, n + 1)
            if prev:
                h_stats(1 - j, n - 1, i)
            if more:
                rotate_k(1 - j, n + 1)
            if prev:
                h_norm(1 - j, n - 1)
            if more == 3:
                x_stats(1 - j, n + 3, i + 2)
                x_norm(1 - j, n + 3)

        x_stats(0, 0, 0)
        x_norm(0, 0)
        x_stats(1, 1, 0)
        x_norm(1, 1)
        kv_stats(0)
        rotate_q(0)
        kv_scale(0, 0)
        rotate_k(0, 0)
        x_stats(0, 2, 1)
        x_norm(0, 2)
        st.done(1, st.at)
        in_steps(step, dve, st, 2 * (11 + 3))
        h_stats(1, B - 1, TURNS - 1)
        h_norm(1, B - 1)
        st.done(1, st.at)

    return sync, tensor, vector, scalar, gpsimd


def route_stage(k):
    nc, t, banks = k.nc, k.t, k.banks
    with ExitStack() as own:
        less = k.buffer(own, "less", [B, E])
        other = k.buffer(own, "other", [B, E])
        key = k.buffer(own, "key", [B, E])
        chosen = [k.buffer(own, f"chosen{m}", [B, E]) for m in range(2)]
        both = k.buffer(own, "both", [B, E])
        peak = k.buffer(own, "route_peak", [2, B])
        index = k.buffer(own, "index", [2, B])
        second = k.buffer(own, "second", [B])
        norm = k.buffer(own, "route_norm", [2, B])
        counts = k.buffer(own, "counts", [E, B])
        upto = k.buffer(own, "upto", [E, B])
        before = k.buffer(own, "before", [E, B])
        per_expert = k.buffer(own, "per_expert", [6, E])
        place = k.buffer(own, "place", [B, E])
        hit = [k.buffer(own, f"hit{m}", [B, E]) for m in range(2)]
        sums = k.buffer(own, "place_sums", [2, B])
        lane = k.buffer(own, "lane", [2, B])
        block_of = k.buffer(own, "block_of", [2, B])
        row_hit = k.buffer(own, "row_hit", [2, B, ROWS])
        block_hit = k.buffer(own, "block_hit", [2, B, 3, BLOCKS])
        empty = k.buffer(own, "empty", [BLOCKS])
        target = k.buffer(own, "target", [BLOCKS])
        passed = k.buffer(own, "passed", [BLOCKS, E])
        block_sum = k.buffer(own, "block_sum", [2, BLOCKS])
    second_ready = k.semaphore("second_ready")
    second_exped = k.semaphore("second_exped")
    chosen_ready = k.semaphore("chosen_ready")
    counted = k.semaphore("counted")
    blocks_hit = k.semaphore("blocks_hit")
    hits_ready = k.semaphore("hits_ready")
    numbers_ready = k.semaphore("hit_numbers_ready")
    tokens_summed = k.semaphore("tokens_summed")
    k.blocks_ready = k.semaphore("blocks_ready")
    k.tokens_ready = k.semaphore("tokens_ready")
    NEED, BLOCKS_E, UPTO_E, BEGIN, TOTAL, SHIFT = range(6)
    OF_PLACE = banks[:, 1, 0:3 * BLOCKS]
    TOKENS, SHARES, TAKEN = (banks[:, 1, a * BLOCKS:(a + 1) * BLOCKS] for a in range(3))
    RANK, ALL = banks[:, 0, 0:B * E], banks[:, 0, B * E:2 * B * E]

    def sync(sp):
        k.begin(sp, "route")

    def tensor(pe):
        pe.wait_ge(chosen_ready, 1)
        flat = both[:, :, :].rearrange("p b e -> p (b e)")
        pe.matmul(RANK, k.consts[:, C_BEFORE:C_BEFORE + P], flat, start=True, stop=True)
        pe.matmul(ALL, k.consts[:, C_ONES:C_ONES + P], flat, start=True, stop=True).then_inc(counted, 1)
        for m in range(2):
            pe.wait_ge(hits_ready, m + 1)
            pe.wait_ge(numbers_ready, m + 1)
            for b in range(B):
                last = pe.matmul(OF_PLACE, row_hit[:, m, b, :], block_hit[:, m, b, :, :].rearrange("p a b -> p (a b)"), start=(m == 0 and b == 0),
                                 stop=(m == 1 and b == B - 1))
        last.then_inc(tokens_summed, 1)

    def scalar(act):
        act.wait_ge(second_ready, 1)
        act.activation(second[:, :], peak[:, 1, :], ACT.Exp).then_inc(second_exped, 1)

    def gpsimd(pool):
        for m in range(2):
            pool.wait_ge(blocks_hit, m + 1)
            for times, of in enumerate((k.consts[:, C_TOKEN:C_TOKEN + B], k.shares[:, m, :])):
                last = pool.tensor_tensor(block_hit[:, m, :, times, :], block_hit[:, m, :, 2, :], wide(of, BLOCKS), ALU.mult)
            last.then_inc(numbers_ready, 1)

    def vector(dve):
        st = k.steps["dve"]
        iota = each(k.consts[:, C_IOTA:C_IOTA + E], B)

        def step(ins):
            st.did(ins)
            st.wait()

        def choose(m, logits):
            step(dve.tensor_reduce(peak[:, m, :], logits, AX.X, ALU.max))
            step(dve.tensor_tensor(key[:, :, :], logits, wide(peak[:, m, :], E), ALU.is_lt))
            step(dve.scalar_tensor_tensor(out=key[:, :, :], in0=key[:, :, :], scalar=float(E), in1=iota,
                                          op0=ALU.mult, op1=ALU.add))
            step(dve.tensor_reduce(index[:, m, :], key[:, :, :], AX.X, ALU.min))
            step(dve.tensor_tensor(chosen[m][:, :, :], iota, wide(index[:, m, :], E), ALU.is_equal))

        dve.wait_ge(k.begun, k.begins["route"])
        dve.wait_ge(k.logits_read, B + 1)
        step(dve.tensor_reduce(norm[:, 0, :], k.logits[:, :, :], AX.X, ALU.max))
        step(dve.tensor_tensor(less[:, :, :], k.logits[:, :, :], wide(norm[:, 0, :], E), ALU.subtract))
        choose(0, less[:, :, :])
        step(dve.scalar_tensor_tensor(out=other[:, :, :], in0=chosen[0][:, :, :], scalar=LOWEST, in1=less[:, :, :],
                                      op0=ALU.mult, op1=ALU.add))
        choose(1, other[:, :, :])
        dve.tensor_tensor(both[:, :, :], chosen[0][:, :, :], chosen[1][:, :, :], ALU.add).then_inc(chosen_ready, 1)
        dve.sem_inc(second_ready, 1)

        dve.wait_ge(second_exped, 1)
        step(dve.tensor_scalar(norm[:, 1, :], second[:, :], 1.0, None, ALU.add))
        step(dve.reciprocal(k.shares[:, 0, :], norm[:, 1, :]))
        step(dve.tensor_tensor(k.shares[:, 1, :], k.shares[:, 0, :], second[:, :], ALU.mult))

        dve.wait_ge(counted, 1)
        step(dve.tensor_copy(counts[:, :, :], ALL.rearrange("p (b e) -> p e b", b=B)))
        ones = k.consts[:, C_ONES:C_ONES + P]
        step(dve.tensor_tensor_scan(upto[:, :, :].rearrange("p e b -> p (e b)"), ones,
                                    counts[:, :, :].rearrange("p e b -> p (e b)"), 0.0, ALU.mult, ALU.add))
        step(dve.tensor_tensor(before[:, :, :], upto[:, :, :], counts[:, :, :], ALU.subtract))
        a = per_expert
        step(dve.tensor_tensor(a[:, TOTAL, :], upto[:, :, B - 1], before[:, :, 0], ALU.subtract))
        step(dve.tensor_scalar(a[:, NEED, :], a[:, TOTAL, :], 1.0 / ROWS, 0.5 - 0.5 / ROWS, ALU.mult, ALU.add))
        step(dve.tensor_scalar(a[:, BLOCKS_E, :], a[:, NEED, :], MAGIC, MAGIC, ALU.add, ALU.subtract))
        step(dve.tensor_tensor_scan(a[:, UPTO_E, :], ones[:, 0:E], a[:, BLOCKS_E, :], 0.0, ALU.mult, ALU.add))
        step(dve.tensor_tensor(a[:, BEGIN, :], a[:, UPTO_E, :], a[:, BLOCKS_E, :], ALU.subtract))
        step(dve.scalar_tensor_tensor(out=a[:, SHIFT, :], in0=a[:, BEGIN, :], scalar=float(ROWS), in1=before[:, :, 0],
                                      op0=ALU.mult, op1=ALU.subtract))
        step(dve.tensor_tensor(place[:, :, :], RANK.rearrange("p (b e) -> p b e", b=B), each(a[:, SHIFT, :], B), ALU.add))
        step(dve.tensor_tensor(place[:, :, :], place[:, :, :], before[:, :, :].rearrange("p e b -> p b e"), ALU.add))
        for m in range(2):
            step(dve.tensor_tensor(hit[m][:, :, :], place[:, :, :], chosen[m][:, :, :], ALU.mult))
            step(dve.tensor_reduce(sums[:, m, :], hit[m][:, :, :], AX.X, ALU.add))
        step(dve.tensor_scalar(lane[:, :, :], sums[:, :, :], 1.0 / ROWS, 0.5 / ROWS - 0.5, ALU.mult, ALU.add))
        step(dve.tensor_scalar(block_of[:, :, :], lane[:, :, :], MAGIC, MAGIC, ALU.add, ALU.subtract))
        step(dve.scalar_tensor_tensor(out=lane[:, :, :], in0=block_of[:, :, :], scalar=-float(ROWS), in1=sums[:, :, :],
                                      op0=ALU.mult, op1=ALU.add))
        lanes, blocks = k.consts[:, C_LANE:C_LANE + ROWS], k.consts[:, C_LANE:C_LANE + BLOCKS]
        for m in range(2):
            dve.tensor_tensor(block_hit[:, m, :, 2, :], wide(block_of[:, m, :], BLOCKS), each(blocks, B),
                              ALU.is_equal).then_inc(blocks_hit, 1)
        for m in range(2):
            dve.tensor_tensor(row_hit[:, m, :, :], wide(lane[:, m, :], ROWS), each(lanes, B), ALU.is_equal).then_inc(hits_ready, 1)

        step(dve.tensor_tensor(passed[:, :, :], wide(blocks, E), each(a[:, UPTO_E, :], BLOCKS), ALU.is_ge))
        step(dve.tensor_reduce(block_sum[:, 0, :], passed[:, :, :], AX.X, ALU.add))
        step(dve.tensor_scalar(block_sum[:, 1, :], block_sum[:, 0, :], float(E - 1), None, ALU.min))
        dve.tensor_copy(k.block_expert[:, :], block_sum[:, 1, :]).then_inc(k.blocks_ready, 1)
        dve.wait_ge(tokens_summed, 1)
        dve.tensor_copy(k.token_of[:, :], TOKENS).then_inc(k.tokens_ready, 1)
        dve.tensor_copy(k.share_of[:, :], SHARES)
        step(dve.tensor_scalar(empty[:, :], TAKEN, -1.0, 1.0, ALU.mult, ALU.add))
        step(dve.tensor_tensor(target[:, :], empty[:, :], k.consts[:, C_TOKEN:C_TOKEN + 1].to_broadcast([P, BLOCKS]), ALU.mult))
        step(dve.scalar_tensor_tensor(out=target[:, :], in0=empty[:, :], scalar=float(TOK), in1=target[:, :],
                                      op0=ALU.mult, op1=ALU.add))
        step(dve.tensor_tensor(target[:, :], target[:, :], TOKENS, ALU.add))
        dve.tensor_copy(k.target_of[:, :], target[:, :]).then_inc(k.tokens_ready, 1)
        st.done(1, st.at)

    return sync, tensor, vector, scalar, gpsimd


def experts_stage(k):
    nc, t, banks = k.nc, k.t, k.banks
    with ExitStack() as own:
        target = k.buffer(own, "expert_target", [1], I32)
        share = k.buffer(own, "expert_share", [1])
        token = [k.buffer(own, f"token{j}", [1], I32) for j in range(2)]
        steps = [k.buffer(own, f"expert_steps{j}", [2, TILES]) for j in range(2)]
        rows = [k.buffer(own, f"expert_rows{j}", [D]) for j in range(2)]
        x = k.buffer(own, "expert_x", [D])
        rest = k.buffer(own, "expert_rest", [D])
        parts = [k.buffer(own, f"expert_parts{j}", [3, DC, ROWS], BF16) for j in range(2)]
        chunk = [k.buffer(own, f"expert_chunk{a}", [2, ROWS]) for a in range(2)]
        gate = [k.buffer(own, f"expert_gate{a}", [2, ROWS]) for a in range(2)]
        silu = [k.buffer(own, f"silu{a}", [ROWS]) for a in range(2)]
        up = [k.buffer(own, f"up{j}", [FC, ROWS]) for j in range(2)]
        y = [k.buffer(own, f"expert_y{j}", [D]) for j in range(2)]
    token_ready = k.semaphore("token_ready")
    rows_in = [k.semaphore(f"expert_rows_in{j}") for j in range(2)]
    target_ready = k.semaphore("target_ready")
    k.added = k.semaphore("added")
    rows_free = k.semaphore("expert_rows_free")
    block_turned = k.semaphore("block_turned")
    x_ready = k.semaphore("expert_x_ready")
    rest_ready = k.semaphore("rest_ready")
    mid_ready = k.semaphore("mid_ready")
    parts_ready = k.semaphore("parts_ready")
    up_summed = k.semaphore("up_summed")
    chunk_ready = k.semaphore("chunk_ready")
    gate_ready = k.semaphore("gate_ready")
    silu_ready = k.semaphore("silu_ready")
    up_ready = k.semaphore("up_ready")
    y_summed = k.semaphore("y_summed")
    y_ready = k.semaphore("y_ready")
    UP, TURN, Y = 0, 4, 6
    TURNS = BLOCKS // 2
    assert BLOCKS % 2
    AHEAD = 4

    def in_steps(emit, eng):
        emit(0, 0, 0, False, 2)
        with eng.Fori(0, TURNS - 1) as i:
            for j in (1, 0):
                emit(j, 2 * i + 2 - j, i, True, 2)
        emit(1, BLOCKS - 2, TURNS - 1, True, 1)
        emit(0, BLOCKS - 1, TURNS - 1, True, 0)

    def bank(j, f):
        g = FC * (1 - j) + f
        return UP + g % 4, 2 if g < 2 else 4

    def slot(j, f):
        return (FC * (1 - j) + f) % 2

    def sync(sp):
        pass

    def tensor(pe):
        def turn(j, n, i):
            pe.wait_ge(rows_in[j], 16 * i + 16)
            for c in range(DC):
                last = pe.transpose(banks[:, TURN + j, c * P:(c + 1) * P], rows[j][:, c * P:(c + 1) * P], k.ident)
            last.then_inc(block_turned, 1)

        def expert_of(n):
            return pe.value_load(k.block_expert[0:1, bass.ds(n, 1)], min_val=0, max_val=E - 1)

        def up_product(j, n, f, expert):
            at, before = bank(j, f)
            pe.wait_ge(gate_ready, FC * n + f + 1 + AHEAD - before)
            for m in range(2):
                for c in range(DC):
                    for a in range(3):
                        last = pe.matmul(
                            banks[:, at, (m * DC + c) * ROWS:(m * DC + c + 1) * ROWS],
                            levels[:, bass.ds(expert * (2 * JOB) + (m * JOB + (f * DC + c) * P), P)],
                            parts[j][:, a, c, :], start=(a == 0), stop=(a == 2))
            last.then_inc(up_summed, 1)

        def down_product(j, n, f, expert):
            if f == 0:
                pe.wait_ge(y_ready, n + 1)
            pe.wait_ge(up_ready, FC * n + f + 1)
            last = pe.matmul(banks[:, Y + j, 0:D], up[j][:, f, :], down[:, bass.ds(expert * JOB + f * D, D)],
                             start=(f == 0), stop=(f == FC - 1))
            if f == FC - 1:
                last.then_inc(y_summed, 1)

        def step(j, n, i, prev, more):
            expert = expert_of(n)
            last_expert = expert_of(n - 1) if prev else None
            pe.wait_ge(parts_ready, n + 1)
            for f in range(FC):
                up_product(j, n, f, expert)
                if prev:
                    down_product(1 - j, n - 1, f, last_expert)
                if more and f == 1:
                    turn(1 - j, n + 1, i + 1 if prev else 0)

        levels = k.levels[:, :, :].rearrange("p m a -> p (m a)")
        down = k.down[:, :, :].rearrange("p m a -> p (m a)")
        pe.wait_ge(k.blocks_ready, 1)
        pe.wait_ge(k.expert_loads, 16 * (4 * E + 1))
        turn(0, 0, 0)
        in_steps(step, pe)
        expert = expert_of(BLOCKS - 1)
        for f in range(FC):
            down_product(0, BLOCKS - 1, f, expert)

    def scalar(act):
        def take_rows(j, n):
            act.wait_ge(block_turned, n + 1)
            turned = banks[:, TURN + j, 0:D]
            act.copy(x[:, :], turned)
            act.copy(parts[j][:, 0, :, :].rearrange("p c s -> p (c s)"), turned).then_inc(x_ready, 1)

        def second_part(j, n):
            act.wait_ge(rest_ready, n + 1)
            act.copy(parts[j][:, 1, :, :].rearrange("p c s -> p (c s)"), rest[:, :]).then_inc(mid_ready, 1)

        def first_chunk(j, n, f):
            act.wait_ge(up_summed, FC * n + f + 1)
            at, _ = bank(j, f)
            for m in range(2):
                last = act.activation(chunk[slot(j, f)][:, m, :], banks[:, at, m * D:m * D + ROWS], ACT.Copy,
                                      scale=steps[j][:, m, f * DC:f * DC + 1])
            last.then_inc(chunk_ready, 1)

        def soften(j, n, f):
            act.wait_ge(gate_ready, FC * n + f + 1 + AHEAD)
            act.activation(silu[slot(j, f)][:, :], gate[slot(j, f)][:, 0, :], ACT.Silu).then_inc(silu_ready, 1)

        def take_y(j, n):
            act.wait_ge(y_summed, n + 1)
            act.wait_ge(target_ready, n + 1)
            act.wait_ge(rows_free, n + 1)
            act.activation(y[j][:, :], banks[:, Y + j, 0:D], ACT.Copy, scale=share[:, :]).then_inc(y_ready, 1)

        def step(j, n, i, prev, more):
            for f in range(FC):
                first_chunk(j, n, f)
                if f:
                    soften(j, n, f - 1)
                if more and f == 2:
                    take_rows(1 - j, n + 1)
                if more and f == 4:
                    second_part(1 - j, n + 1)
            soften(j, n, FC - 1)
            if prev:
                take_y(1 - j, n - 1)

        act.wait_ge(k.tokens_ready, 2)
        act.wait_ge(k.expert_loads, 16 * (4 * E + 1))
        act.sem_inc(y_ready, 2)
        take_rows(0, 0)
        second_part(0, 0)
        in_steps(step, act)
        take_y(0, BLOCKS - 1)

    def vector(dve):
        def second_chunk(j, n, f):
            if not (isinstance(n, int) and n == 0 and f < 2):
                dve.wait_ge(up_ready, FC * n + f - 1)
            dve.wait_ge(chunk_ready, FC * n + f + 1)
            at, _ = bank(j, f)
            for m in range(2):
                last = dve.scalar_tensor_tensor(out=gate[slot(j, f)][:, m, :], in0=banks[:, at, m * D + ROWS:(m + 1) * D],
                                                scalar=steps[j][:, m, f * DC + 1:f * DC + 2], in1=chunk[slot(j, f)][:, m, :],
                                                op0=ALU.mult, op1=ALU.add)
            last.then_inc(gate_ready, 1)

        def multiply(j, n, f):
            dve.wait_ge(silu_ready, FC * n + f + 1)
            dve.tensor_tensor(up[j][:, f, :], silu[slot(j, f)][:, :], gate[slot(j, f)][:, 1, :], ALU.mult).then_inc(up_ready, 1)

        def step(j, n, i, prev, more):
            for f in range(FC):
                second_chunk(j, n, f)
                if f:
                    multiply(j, n, f - 1)
            multiply(j, n, FC - 1)

        dve.sem_inc(gate_ready, AHEAD)
        in_steps(step, dve)

    def gpsimd(pool):
        def gather(j, n, begin=False):
            if not begin:
                pool.wait_ge(block_turned, n - 1)
            pool.tensor_copy(token[j][:, :], k.token_of[:, bass.ds(n, 1)]).then_inc(token_ready, 1)
            pool.wait_ge(token_ready, n + 1)
            pool.sem_inc(k.s_held, 1)
            pool.indirect_dma_start(out=rows[j][:, :], out_offset=None, in_=k.normed_d,
                                    in_offset=bass.IndirectOffsetOnAxis(ap=token[j][:, :], axis=0)).then_inc(rows_in[j], 16)

        def split(j, n, begin=False):
            expert = pool.value_load(k.block_expert[0:1, bass.ds(n, 1)], min_val=0, max_val=E - 1)
            if not begin:
                pool.wait_ge(up_ready, FC * (n - 1))
            pool.tensor_copy(steps[j][:, :, :], k.level_steps[:, bass.ds(2 * expert, 2), :])
            pool.wait_ge(x_ready, n + 1)
            pool.tensor_tensor(rest[:, :], x[:, :], parts[j][:, 0, :, :].rearrange("p c s -> p (c s)"),
                               ALU.subtract).then_inc(rest_ready, 1)
            pool.wait_ge(mid_ready, n + 1)
            pool.tensor_tensor(parts[j][:, 2, :, :].rearrange("p c s -> p (c s)"), rest[:, :],
                               parts[j][:, 1, :, :].rearrange("p c s -> p (c s)"), ALU.subtract).then_inc(parts_ready, 1)

        def aim(n, begin=False):
            if not begin:
                pool.wait_ge(y_ready, n + 2)
            pool.tensor_copy(target[:, :], k.target_of[:, bass.ds(n, 1)])
            pool.tensor_copy(share[:, :], k.share_of[:, bass.ds(n, 1)]).then_inc(target_ready, 1)

        def add(j, n):
            pool.wait_ge(y_ready, n + 3)
            pool.wait_ge(target_ready, n + 1)
            pool.sem_inc(k.s_held, 1)
            pool.indirect_dma_start(out=k.hidden_d, out_offset=bass.IndirectOffsetOnAxis(ap=target[:, :], axis=0),
                                    in_=y[j][:, :], in_offset=None, compute_op=ALU.add).then_inc(k.added, 16)

        def settle(n):
            pool.wait_ge(k.added, 16 * n + 16)
            pool.sem_inc(rows_free, 1)

        def step(j, n, i, prev, more):
            if more:
                split(1 - j, n + 1, not prev)
            if more == 2:
                gather(j, n + 2)
            if prev:
                aim(n - 1, isinstance(n, int) and n == 1)
                add(1 - j, n - 1)
                settle(n - 1)

        pool.wait_ge(k.tokens_ready, 1)
        gather(0, 0, True)
        gather(1, 1, True)
        pool.wait_ge(k.tokens_ready, 2)
        pool.wait_ge(k.expert_loads, 16 * (4 * E + 1))
        split(0, 0, True)
        pool.sem_inc(rows_free, 2)
        in_steps(step, pool)
        aim(BLOCKS - 1)
        add(0, BLOCKS - 1)

    return sync, tensor, vector, scalar, gpsimd


def finish_stage(k):
    nc, t = k.nc, k.t
    GROUP = 4
    N_GROUPS = B // GROUP
    with ExitStack() as own:
        h = k.buffer(own, "finish_h", [B, D])
        decoded = k.buffer(own, "decoded_rows", [B, D])
        stats = [k.buffer(own, f"finish_stats{j}", [GROUP, 6]) for j in range(2)]
        mean = [k.buffer(own, f"finish_mean{j}", [GROUP, 2]) for j in range(2)]
        eps = [k.buffer(own, f"finish_eps{j}", [GROUP]) for j in range(2)]
        scale = [k.buffer(own, f"finish_scale{j}", [GROUP]) for j in range(2)]
    h_in = [k.semaphore(f"finish_h_in{g}") for g in range(N_GROUPS)]
    finish_var = k.semaphore("finish_var")
    finish_scale = k.semaphore("finish_scale")
    finish_normed = k.semaphore("finish_normed")
    finish_stored = k.semaphore("finish_stored")

    def tiles(g):
        return slice(GROUP * g, GROUP * (g + 1))

    def sync(sp):
        sp.wait_ge(k.added, 16 * BLOCKS)
        for g in range(N_GROUPS):
            sp.dma_start(h[:, tiles(g), :], k.hidden_d[g * GROUP * P:(g + 1) * GROUP * P, :].rearrange(
                "(b p) n -> p b n", p=P)).then_inc(h_in[g], 16)
        for g in range(N_GROUPS):
            sp.wait_ge(finish_normed, g + 1)
            sp.dma_start(k.out[g * GROUP * P:(g + 1) * GROUP * P, :].rearrange("(b p) n -> p b n", p=P),
                         decoded[:, tiles(g), :]).then_inc(finish_stored, 16)
        sp.wait_ge(finish_stored, 16 * N_GROUPS)

    def gpsimd(pool):
        for g in range(N_GROUPS):
            pool.wait_ge(finish_var, g + 1)
            pool.tensor_tensor(scale[g % 2][:, :], eps[g % 2][:, :], k.minus_half[:, 0:GROUP], ALU.pow).then_inc(finish_scale, 1)

    def vector(dve):
        st = k.steps["dve"]

        def norm_stats_of(g):
            j = g % 2
            dve.wait_ge(h_in[g], 16)
            for a in range(GROUP):
                last = dve.bn_stats(stats[j][:, a, :], h[:, GROUP * g + a, :])
            st.did(last)
            st.wait()
            for a in range(GROUP):
                last = dve.bn_aggr(mean[j][:, a, :], stats[j][:, a, :])
            st.did(last)
            st.wait()
            dve.tensor_scalar(eps[j][:, :], mean[j][:, :, 1], EPS, None, ALU.add).then_inc(finish_var, 1)

        def norm_rows(g):
            j = g % 2
            dve.wait_ge(finish_scale, g + 1)
            for a in range(GROUP):
                last = dve.tensor_scalar(decoded[:, GROUP * g + a, :], h[:, GROUP * g + a, :], mean[j][:, a, 0:1],
                                         scale[j][:, a:a + 1], ALU.subtract, ALU.mult)
            last.then_inc(finish_normed, 1)

        norm_stats_of(0)
        for g in range(N_GROUPS):
            if g + 1 < N_GROUPS:
                norm_stats_of(g + 1)
            norm_rows(g)
        st.done(1, st.at)

    def tensor(pe):
        pass

    def scalar(act):
        pass

    return sync, tensor, vector, scalar, gpsimd


STAGES = (prep_stage, mix_stage, cross_stage, attend_stage, route_stage, experts_stage, finish_stage)


def decoder_layer(nc, t, out):
    with ExitStack() as top:
        k = Shared(nc, t, out, top)
        stages = [stage(k) for stage in STAGES]
        steps = {eng: k.semaphore(f"{eng}_steps") for eng in ("dve", "act", "pool")}
        block = top.enter_context(nc.Block())

        @block.sync
        def _(sp):
            sp.dma_start(k.consts[:, :], t["constants"]).then_inc(k.s_consts, 16)
            sp.wait_ge(k.s_consts, 16)
            sp.dma_start(k.hidden_d[TOK:TOK + P, :], k.consts[:, 0:D]).then_inc(k.s_consts, 16)
            for sync, *_ in stages:
                sync(sp)

        @block.tensor
        def _(pe):
            pe.wait_ge(k.s_consts, 16)
            for _, tensor, *_ in stages:
                tensor(pe)

        @block.vector
        def _(dve):
            k.steps["dve"] = Steps(dve, steps["dve"])
            dve.memset(k.magic[:, :], MAGIC).then_inc(k.s_fill, 1)
            dve.memset(k.minus_magic[:, :], -MAGIC).then_inc(k.s_fill, 1)
            dve.memset(k.minus_half[:, :], -0.5).then_inc(k.s_fill, 1)
            dve.wait_ge(k.s_consts, 16)
            for _, _, vector, *_ in stages:
                vector(dve)

        @block.scalar
        def _(act):
            k.steps["act"] = Steps(act, steps["act"])
            act.wait_ge(k.s_consts, 16)
            act.wait_ge(k.s_fill, 3)
            for _, _, _, scalar, _ in stages:
                scalar(act)

        @block.gpsimd
        def _(pool):
            k.steps["pool"] = Steps(pool, steps["pool"])
            pool.wait_ge(k.s_consts, 16)
            pool.wait_ge(k.s_fill, 3)
            for _, _, _, _, gpsimd in stages:
                gpsimd(pool)


def shape_constants():
    c = np.zeros((P, C_END), np.float32)
    i = np.arange(P)
    c[:, C_ID:C_ID + P] = np.eye(P)
    inv = np.float32(1.0) / np.float32(1000000.0) ** (np.arange(0, HD, 2, dtype=np.float32) / np.float32(HD))
    angle = (i.astype(np.float32)[:, None] * inv[None, :]).astype(np.float32)
    angle = np.concatenate([angle, angle], axis=1)
    c[:, C_COS:C_COS + HD] = np.cos(angle)
    c[:, C_SIN:C_SIN + HD] = np.sin(angle) * np.where(np.arange(HD) < HD // 2, -1, 1)
    c[:, C_MASK:C_MASK + S] = np.where(i[:, None] >= i[None, :], 0.0, MASKED)
    c[:, C_BEFORE:C_BEFORE + P] = i[:, None] < i[None, :]
    c[:, C_ONES:C_ONES + P] = 1.0
    c[:, C_HEAD:C_HEAD + HALF] = i[:, None] // XK == np.arange(HALF)[None, :]
    c[:, C_IOTA:C_IOTA + E] = np.arange(E)
    c[:, C_TOKEN:C_TOKEN + B] = i[:, None] + P * np.arange(B)[None, :]
    c[:, C_LANE:C_LANE + P] = i
    return c


def laid_out(x, ctx_1024, L0_attn_rkv_w, L0_attn_out_w, L0_attn_time_decay, L0_attn_time_first,
             L0_attn_time_decay_rev, L0_attn_time_first_rev, L0_xattn_Wq, L0_xattn_bq, L0_xattn_Wk, L0_xattn_bk,
             L0_xattn_Wv, L0_xattn_bv, L0_xattn_Wo, L0_xattn_bo, L0_ffn_w_q, L0_ffn_w_k, L0_ffn_w_v, L0_ffn_w_o,
             L0_ffn_g1, L0_ffn_g2, L0_ffn_w_gate, L0_ffn_w1, L0_ffn_w3, L0_ffn_w2):
    def columns(*vectors):
        return np.concatenate([v.reshape(-1, P) for v in vectors]).T

    qkv = np.concatenate([L0_ffn_w_q, L0_ffn_w_k, L0_ffn_w_v])
    tiles = [qkv.reshape(-1, P, DC, P).transpose(1, 2, 0, 3).reshape(P, -1, P),
             L0_ffn_w_o.reshape(DC, P, QH, P).transpose(1, 2, 0, 3).reshape(P, -1, P)]
    tiles.append(np.zeros((P, 3 * TILES - sum(a.shape[1] for a in tiles), P), np.float32))
    jobs = [np.concatenate(tiles, axis=1).reshape(P, 3, TILES * P).transpose(1, 0, 2)]
    jobs.append(L0_ffn_w2.reshape(E, DC, P, FC, P).transpose(0, 2, 3, 1, 4).reshape(E, P, JOB))
    for e in range(E):
        for w in (L0_ffn_w1, L0_ffn_w3):
            jobs.append(w[e].reshape(FC, P, DC * P).transpose(1, 0, 2).reshape(1, P, JOB))
    arrays = {
        "constants": shape_constants(),
        "x": x.reshape(TOK, D),
        "x_fwd_t": x.reshape(TOK, D).T,
        "x_bwd_t": x[:, ::-1].reshape(TOK, D).T,
        "ctx_t": ctx_1024.reshape(TOK, D).T,
        "rkv_t": L0_attn_rkv_w.T,
        "out_t": L0_attn_out_w.T,
        "decay": columns(L0_attn_time_decay, L0_attn_time_decay_rev),
        "first": columns(L0_attn_time_first, L0_attn_time_first_rev),
        "wq": L0_xattn_Wq, "wk": L0_xattn_Wk, "wv": L0_xattn_Wv, "wo": L0_xattn_Wo,
        "bqk": columns(L0_xattn_bq, L0_xattn_bk),
        "rows": np.stack([L0_xattn_bv, L0_xattn_bo, L0_ffn_g1, L0_ffn_g2]).reshape(4, D),
        "gate_t": L0_ffn_w_gate.T,
        "weight_jobs": np.concatenate(jobs),
    }
    return {f"in_{n}": np.ascontiguousarray(a) for n, a in arrays.items()}


def build(nc, arrays):
    t = {n.removeprefix("in_"): nc.dram_tensor(n, a.shape, F32, kind="ExternalInput").ap() for n, a in arrays.items()}
    out = nc.dram_tensor("decoded", (TOK, D), F32, kind="ExternalOutput").ap()
    decoder_layer(nc, t, out)


def kernel(**inputs):
    import concourse.bacc as bacc
    from concourse.bass_utils import run_bass_kernel_spmd

    arrays = laid_out(**{n: np.asarray(a) for n, a in inputs.items()})
    nc = bacc.Bacc("TRN2", target_bir_lowering=False, num_devices=1)
    build(nc, arrays)
    result = run_bass_kernel_spmd(nc, [arrays], core_ids=[0])
    return result.results[0]["decoded"].reshape(B, S, D)
```
